# Optimizing a Trainium2 kernel written in Bass

```python
import numpy as np
import jax
import jax.numpy as jnp

def _softmax(x, axis=-1):
    return jax.nn.softmax(x, axis=axis)

def _gelu(x):
    return jax.nn.gelu(x, approximate=True)

def _silu(x):
    return jax.nn.silu(x)

def _sigmoid(x):
    return jax.nn.sigmoid(x)

def _layernorm(x, axis=-1, eps=1e-05):
    m = jnp.mean(x, axis=axis, keepdims=True)
    v = jnp.var(x, axis=axis, keepdims=True)
    return (x - m) / jnp.sqrt(v + eps)

def _scatter_add(tgt, idx, src, axis=0):
    return tgt.at[idx].add(src)

def _segment_sum(src, seg, n):
    return jax.ops.segment_sum(src, seg, n)
kernel_name = 'mk_prb_d2_jaxref_r8_822dae'

def setup_inputs(seed: int=0):
    np.random.seed(seed)
    _w = jnp.asarray

    def _L0_attn_setup():
        import jax, jax.numpy as jnp
        import numpy as np
        D_MODEL = 128
        N_HEADS = 16
        D_LATENT = 32
        HEAD_DIM = D_MODEL // N_HEADS

        def apply_rope(x):
            B, T, H, D = x.shape
            inv_freq = 1.0 / 10000.0 ** (jnp.arange(0, D, 2, dtype=jnp.float32) / D)
            t = jnp.arange(T, dtype=jnp.float32)
            freqs = t[:, None] * inv_freq[None, :]
            sin_f = jnp.sin(freqs)[None, :, None, :]
            cos_f = jnp.cos(freqs)[None, :, None, :]
            x1, x2 = jnp.split(x, 2, axis=-1)
            return jnp.concatenate([x1 * cos_f - x2 * sin_f, x1 * sin_f + x2 * cos_f], axis=-1)
        key = jax.random.key(seed)
        ks = jax.random.split(key, 10)
        B, T = (4, 512)
        s = lambda fan_in: 1.0 / np.sqrt(fan_in)
        return {'x': jax.random.normal(ks[0], (B, T, D_MODEL), dtype=jnp.float32), 'Wq': jax.random.normal(ks[1], (D_MODEL, D_MODEL), dtype=jnp.float32) * s(D_MODEL), 'bq': jnp.zeros((D_MODEL,), jnp.float32), 'Wdown': jax.random.normal(ks[2], (D_MODEL, D_LATENT), dtype=jnp.float32) * s(D_MODEL), 'bdown': jnp.zeros((D_LATENT,), jnp.float32), 'Wup': jax.random.normal(ks[3], (D_LATENT, 2 * D_MODEL), dtype=jnp.float32) * s(D_LATENT), 'bup': jnp.zeros((2 * D_MODEL,), jnp.float32), 'Wout': jax.random.normal(ks[4], (D_MODEL, D_MODEL), dtype=jnp.float32) * s(D_MODEL), 'bout': jnp.zeros((D_MODEL,), jnp.float32)}
    _L0_attn_in = _L0_attn_setup()

    def _L0_ffn_setup():
        import jax, jax.numpy as jnp
        import numpy as np
        DIM = 128
        HIDDEN = 384
        SCALE = 1.0 / 127.0

        def _dequant(w_int, dtype):
            return w_int.astype(dtype) * jnp.asarray(SCALE, dtype)
        key = jax.random.key(seed)
        k_x, k_g, k_u, k_d = jax.random.split(key, 4)
        x = jax.random.normal(k_x, (4, 256, DIM), dtype=jnp.float32)
        w_gate = jax.random.randint(k_g, (HIDDEN, DIM), -127, 128, dtype=jnp.int32)
        w_up = jax.random.randint(k_u, (HIDDEN, DIM), -127, 128, dtype=jnp.int32)
        w_down = jax.random.randint(k_d, (DIM, HIDDEN), -127, 128, dtype=jnp.int32)
        return {'x': x, 'w_gate': w_gate, 'w_up': w_up, 'w_down': w_down}
    _L0_ffn_in = _L0_ffn_setup()

    def _L1_attn_setup():
        import jax, jax.numpy as jnp
        import numpy as np
        from jax import lax
        B_, L, DM = (2, 256, 128)
        DI, N, K, R = (256, 16, 4, 64)
        EPS = 1e-05

        def _rmsnorm(x, w, eps=EPS):
            var = jnp.mean(x * x, axis=-1, keepdims=True)
            return x * lax.rsqrt(var + eps) * w

        def _causal_depthwise_conv(u, conv_w, conv_b):
            lhs = jnp.transpose(u, (0, 2, 1))
            lhs = jnp.pad(lhs, ((0, 0), (0, 0), (K - 1, 0)))
            rhs = conv_w[:, None, :]
            out = lax.conv_general_dilated(lhs, rhs, window_strides=(1,), padding='VALID', dimension_numbers=('NCH', 'OIH', 'NCH'), feature_group_count=DI)
            return jnp.transpose(out, (0, 2, 1)) + conv_b

        def _mamba_mixer(h, in_proj_w, conv_w, conv_b, x_proj_w, dt_proj_w, dt_proj_b, A_log, D, out_proj_w):
            xz = h @ in_proj_w
            u, z = jnp.split(xz, 2, axis=-1)
            u = jax.nn.silu(_causal_depthwise_conv(u, conv_w, conv_b))
            xdbl = u @ x_proj_w
            dt_r = xdbl[..., :R]
            Bm = xdbl[..., R:R + N]
            Cm = xdbl[..., R + N:]
            dt = jax.nn.softplus(dt_r @ dt_proj_w + dt_proj_b)
            A = -jnp.exp(A_log)

            def step(hst, inp):
                dt_t, B_t, C_t, u_t = inp
                dA = jnp.exp(dt_t[..., None] * A)
                dBu = dt_t[..., None] * B_t[:, None, :] * u_t[..., None]
                hst = dA * hst + dBu
                y = jnp.einsum('bdn,bn->bd', hst, C_t)
                return (hst, y)
            xs = (jnp.swapaxes(dt, 0, 1), jnp.swapaxes(Bm, 0, 1), jnp.swapaxes(Cm, 0, 1), jnp.swapaxes(u, 0, 1))
            h0 = jnp.zeros((u.shape[0], DI, N), dtype=u.dtype)
            _, ys = lax.scan(step, h0, xs)
            y = jnp.swapaxes(ys, 0, 1) + u * D
            y = y * jax.nn.silu(z)
            return y @ out_proj_w
        key = jax.random.key(seed)
        ks = jax.random.split(key, 12)
        w = lambda k, s: jax.random.normal(k, s, dtype=jnp.float32) * 0.02
        inp = {'x': jax.random.normal(ks[0], (B_, L, DM), dtype=jnp.float32), 'hormone_vectors': jax.random.normal(ks[1], (B_, 64), dtype=jnp.float32), 'norm_w': jnp.ones((DM,), dtype=jnp.float32), 'in_proj_w': w(ks[2], (DM, 2 * DI)), 'conv_w': w(ks[3], (DI, K)), 'conv_b': jnp.zeros((DI,), dtype=jnp.float32), 'x_proj_w': w(ks[4], (DI, R + 2 * N)), 'dt_proj_w': w(ks[5], (R, DI)), 'dt_proj_b': jax.random.uniform(ks[6], (DI,), dtype=jnp.float32, minval=-4.0, maxval=-2.0), 'A_log': jnp.log(jnp.broadcast_to(jnp.arange(1, N + 1, dtype=jnp.float32), (DI, N))), 'D': jnp.ones((DI,), dtype=jnp.float32), 'out_proj_w': w(ks[7], (DI, DM))}
        return inp
    _L1_attn_in = _L1_attn_setup()

    def _L1_ffn_setup():
        import jax, jax.numpy as jnp
        import numpy as np
        D_MODEL, FF_DIM = (128, 256)
        N_SHARED, N_ROUTED, TOP_K = (1, 8, 2)
        BATCH, SEQ = (2, 256)
        key = jax.random.key(seed)
        ks = jax.random.split(key, 8)
        init = lambda k, shape: jax.random.normal(k, shape, jnp.float32) * 0.02
        x = jax.random.normal(ks[0], (BATCH, SEQ, D_MODEL), jnp.float32)
        Wg = init(ks[1], (D_MODEL, N_ROUTED))
        Ws1 = init(ks[2], (D_MODEL, FF_DIM))
        Ws3 = init(ks[3], (D_MODEL, FF_DIM))
        Ws2 = init(ks[4], (FF_DIM, D_MODEL))
        We1 = init(ks[5], (N_ROUTED, D_MODEL, FF_DIM))
        We3 = init(ks[6], (N_ROUTED, D_MODEL, FF_DIM))
        We2 = init(ks[7], (N_ROUTED, FF_DIM, D_MODEL))
        return {'x': x, 'Wg': Wg, 'Ws1': Ws1, 'Ws3': Ws3, 'Ws2': Ws2, 'We1': We1, 'We3': We3, 'We2': We2}
    _L1_ffn_in = _L1_ffn_setup()
    _d = {'L0_attn_x': _L0_attn_in['x'], 'L0_attn_Wq': _L0_attn_in['Wq'], 'L0_attn_bq': _L0_attn_in['bq'], 'L0_attn_Wdown': _L0_attn_in['Wdown'], 'L0_attn_bdown': _L0_attn_in['bdown'], 'L0_attn_Wup': _L0_attn_in['Wup'], 'L0_attn_bup': _L0_attn_in['bup'], 'L0_attn_Wout': _L0_attn_in['Wout'], 'L0_attn_bout': _L0_attn_in['bout'], 'L0_ffn_w_gate': _L0_ffn_in['w_gate'], 'L0_ffn_w_up': _L0_ffn_in['w_up'], 'L0_ffn_w_down': _L0_ffn_in['w_down'], 'L1_attn_hormone_vectors': _L1_attn_in['hormone_vectors'], 'L1_attn_norm_w': _L1_attn_in['norm_w'], 'L1_attn_in_proj_w': _L1_attn_in['in_proj_w'], 'L1_attn_conv_w': _L1_attn_in['conv_w'], 'L1_attn_conv_b': _L1_attn_in['conv_b'], 'L1_attn_x_proj_w': _L1_attn_in['x_proj_w'], 'L1_attn_dt_proj_w': _L1_attn_in['dt_proj_w'], 'L1_attn_dt_proj_b': _L1_attn_in['dt_proj_b'], 'L1_attn_A_log': _L1_attn_in['A_log'], 'L1_attn_D': _L1_attn_in['D'], 'L1_attn_out_proj_w': _L1_attn_in['out_proj_w'], 'L1_ffn_Wg': _L1_ffn_in['Wg'], 'L1_ffn_Ws1': _L1_ffn_in['Ws1'], 'L1_ffn_Ws3': _L1_ffn_in['Ws3'], 'L1_ffn_Ws2': _L1_ffn_in['Ws2'], 'L1_ffn_We1': _L1_ffn_in['We1'], 'L1_ffn_We3': _L1_ffn_in['We3'], 'L1_ffn_We2': _L1_ffn_in['We2']}
    _x0 = _d['L0_attn_x']
    _d['L0_attn_x'] = jax.random.normal(jax.random.fold_in(jax.random.key(seed), 1), (8, 512, 128), dtype=_x0.dtype)
    del _x0
    return _d

def reference(L0_attn_x, L0_attn_Wq, L0_attn_bq, L0_attn_Wdown, L0_attn_bdown, L0_attn_Wup, L0_attn_bup, L0_attn_Wout, L0_attn_bout, L0_ffn_w_gate, L0_ffn_w_up, L0_ffn_w_down, L1_attn_hormone_vectors, L1_attn_norm_w, L1_attn_in_proj_w, L1_attn_conv_w, L1_attn_conv_b, L1_attn_x_proj_w, L1_attn_dt_proj_w, L1_attn_dt_proj_b, L1_attn_A_log, L1_attn_D, L1_attn_out_proj_w, L1_ffn_Wg, L1_ffn_Ws1, L1_ffn_Ws3, L1_ffn_Ws2, L1_ffn_We1, L1_ffn_We3, L1_ffn_We2):

    def _L0_attn_ref(x, Wq, bq, Wdown, bdown, Wup, bup, Wout, bout):
        import jax, jax.numpy as jnp
        import numpy as np
        D_MODEL = 128
        N_HEADS = 16
        D_LATENT = 32
        HEAD_DIM = D_MODEL // N_HEADS

        def apply_rope(x):
            B, T, H, D = x.shape
            inv_freq = 1.0 / 10000.0 ** (jnp.arange(0, D, 2, dtype=jnp.float32) / D)
            t = jnp.arange(T, dtype=jnp.float32)
            freqs = t[:, None] * inv_freq[None, :]
            sin_f = jnp.sin(freqs)[None, :, None, :]
            cos_f = jnp.cos(freqs)[None, :, None, :]
            x1, x2 = jnp.split(x, 2, axis=-1)
            return jnp.concatenate([x1 * cos_f - x2 * sin_f, x1 * sin_f + x2 * cos_f], axis=-1)
        B, T, D = x.shape
        H, Dh = (N_HEADS, HEAD_DIM)
        q = x @ Wq + bq
        kv_latent = x @ Wdown + bdown
        kv = kv_latent @ Wup + bup
        q = q.reshape(B, T, H, Dh)
        kv = kv.reshape(B, T, H, 2 * Dh)
        k, v = jnp.split(kv, 2, axis=-1)
        q = apply_rope(q)
        k = apply_rope(k)
        att = jnp.einsum('bthd,btgd->bthg', q, k) / jnp.sqrt(jnp.float32(Dh))
        att = jax.nn.softmax(att, axis=-1)
        out = jnp.einsum('bthg,btgd->bthd', att, v)
        out = out.reshape(B, T, D)
        return out @ Wout + bout

    def _L0_ffn_ref(x, w_gate, w_up, w_down):
        import jax, jax.numpy as jnp
        import numpy as np
        DIM = 128
        HIDDEN = 384
        SCALE = 1.0 / 127.0

        def _dequant(w_int, dtype):
            return w_int.astype(dtype) * jnp.asarray(SCALE, dtype)
        wg = _dequant(w_gate, x.dtype)
        wu = _dequant(w_up, x.dtype)
        wd = _dequant(w_down, x.dtype)
        gate = jnp.einsum('bsd,hd->bsh', x, wg)
        up = jnp.einsum('bsd,hd->bsh', x, wu)
        h = jax.nn.silu(gate) * up
        return jnp.einsum('bsh,dh->bsd', h, wd)

    def _L1_attn_ref(x, hormone_vectors, norm_w, in_proj_w, conv_w, conv_b, x_proj_w, dt_proj_w, dt_proj_b, A_log, D, out_proj_w):
        import jax, jax.numpy as jnp
        import numpy as np
        from jax import lax
        B_, L, DM = (2, 256, 128)
        DI, N, K, R = (256, 16, 4, 64)
        EPS = 1e-05

        def _rmsnorm(x, w, eps=EPS):
            var = jnp.mean(x * x, axis=-1, keepdims=True)
            return x * lax.rsqrt(var + eps) * w

        def _causal_depthwise_conv(u, conv_w, conv_b):
            lhs = jnp.transpose(u, (0, 2, 1))
            lhs = jnp.pad(lhs, ((0, 0), (0, 0), (K - 1, 0)))
            rhs = conv_w[:, None, :]
            out = lax.conv_general_dilated(lhs, rhs, window_strides=(1,), padding='VALID', dimension_numbers=('NCH', 'OIH', 'NCH'), feature_group_count=DI)
            return jnp.transpose(out, (0, 2, 1)) + conv_b

        def _mamba_mixer(h, in_proj_w, conv_w, conv_b, x_proj_w, dt_proj_w, dt_proj_b, A_log, D, out_proj_w):
            xz = h @ in_proj_w
            u, z = jnp.split(xz, 2, axis=-1)
            u = jax.nn.silu(_causal_depthwise_conv(u, conv_w, conv_b))
            xdbl = u @ x_proj_w
            dt_r = xdbl[..., :R]
            Bm = xdbl[..., R:R + N]
            Cm = xdbl[..., R + N:]
            dt = jax.nn.softplus(dt_r @ dt_proj_w + dt_proj_b)
            A = -jnp.exp(A_log)

            def step(hst, inp):
                dt_t, B_t, C_t, u_t = inp
                dA = jnp.exp(dt_t[..., None] * A)
                dBu = dt_t[..., None] * B_t[:, None, :] * u_t[..., None]
                hst = dA * hst + dBu
                y = jnp.einsum('bdn,bn->bd', hst, C_t)
                return (hst, y)
            xs = (jnp.swapaxes(dt, 0, 1), jnp.swapaxes(Bm, 0, 1), jnp.swapaxes(Cm, 0, 1), jnp.swapaxes(u, 0, 1))
            h0 = jnp.zeros((u.shape[0], DI, N), dtype=u.dtype)
            _, ys = lax.scan(step, h0, xs)
            y = jnp.swapaxes(ys, 0, 1) + u * D
            y = y * jax.nn.silu(z)
            return y @ out_proj_w
        del hormone_vectors
        h = _rmsnorm(x, norm_w)
        return x + _mamba_mixer(h, in_proj_w, conv_w, conv_b, x_proj_w, dt_proj_w, dt_proj_b, A_log, D, out_proj_w)

    def _L1_ffn_ref(x, Wg, Ws1, Ws3, Ws2, We1, We3, We2):
        import jax, jax.numpy as jnp
        import numpy as np
        D_MODEL, FF_DIM = (128, 256)
        N_SHARED, N_ROUTED, TOP_K = (1, 8, 2)
        BATCH, SEQ = (2, 256)
        B, S, d = x.shape
        E = Wg.shape[1]
        xf = x.reshape(-1, d)
        T = xf.shape[0]
        gates = jax.nn.sigmoid(xf @ Wg)
        vals, idx = jax.lax.top_k(gates, TOP_K)
        vals = vals / vals.sum(axis=-1, keepdims=True)
        w = jnp.zeros((T, E), x.dtype).at[jnp.arange(T)[:, None], idx].add(vals)
        shared = jax.nn.silu(xf @ Ws1) * (xf @ Ws3) @ Ws2
        h = jax.nn.silu(jnp.einsum('td,edf->tef', xf, We1)) * jnp.einsum('td,edf->tef', xf, We3)
        routed = jnp.einsum('tef,efd,te->td', h, We2, w)
        out = (shared + routed) / (N_SHARED + TOP_K)
        return out.reshape(B, S, d)
    x = L0_attn_x
    xn = _layernorm(x, axis=-1)
    x = x + _L0_attn_ref(xn, L0_attn_Wq, L0_attn_bq, L0_attn_Wdown, L0_attn_bdown, L0_attn_Wup, L0_attn_bup, L0_attn_Wout, L0_attn_bout) + _L0_ffn_ref(xn, L0_ffn_w_gate, L0_ffn_w_up, L0_ffn_w_down)
    xn = _layernorm(x, axis=-1)
    x = x + _L1_attn_ref(xn, L1_attn_hormone_vectors, L1_attn_norm_w, L1_attn_in_proj_w, L1_attn_conv_w, L1_attn_conv_b, L1_attn_x_proj_w, L1_attn_dt_proj_w, L1_attn_dt_proj_b, L1_attn_A_log, L1_attn_D, L1_attn_out_proj_w) + _L1_ffn_ref(xn, L1_ffn_Wg, L1_ffn_Ws1, L1_ffn_Ws3, L1_ffn_Ws2, L1_ffn_We1, L1_ffn_We3, L1_ffn_We2)
    return x

_drawn_inputs = setup_inputs


def setup_inputs(seed=0):
    import zlib

    import numpy as np

    out = dict(_drawn_inputs(seed))
    spreads = {'L0_attn_bq': (0.0, 0.8),
     'L0_attn_bdown': (0.0, 0.8),
     'L0_attn_bup': (0.0, 0.8),
     'L0_attn_bout': (0.0, 0.8),
     'L1_attn_norm_w': (1.0, 0.6),
     'L1_attn_conv_b': (0.0, 0.8),
     'L1_attn_D': (1.0, 0.6)}
    factors = {'L0_attn_Wq': 8.0,
     'L0_attn_Wdown': 8.0,
     'L0_attn_Wup': 8.0,
     'L0_attn_Wout': 8.0,
     'L1_attn_in_proj_w': 8.0,
     'L1_attn_conv_w': 8.0,
     'L1_attn_x_proj_w': 8.0,
     'L1_attn_dt_proj_b': 8.0,
     'L1_attn_A_log': 8.0,
     'L1_attn_out_proj_w': 8.0,
     'L1_ffn_Wg': 8.0,
     'L1_ffn_Ws1': 8.0,
     'L1_ffn_Ws3': 8.0,
     'L1_ffn_Ws2': 8.0,
     'L1_ffn_We1': 8.0,
     'L1_ffn_We3': 8.0,
     'L1_ffn_We2': 8.0}
    for name, (base, spread) in spreads.items():
        noise = np.random.default_rng([zlib.crc32(name.encode()), seed]).standard_normal(out[name].shape)
        drawn = base * np.exp(spread * noise) if base else spread * noise
        out[name] = jnp.asarray(drawn.astype(out[name].dtype))
    for name, factor in factors.items():
        out[name] = (out[name] * factor).astype(out[name].dtype)
    return out
```

```python
from contextlib import ExitStack

import numpy as np

import concourse.bass as bass
from concourse import mybir

F32 = mybir.dt.float32
BF16 = mybir.dt.bfloat16
I32 = mybir.dt.int32
ALU = mybir.AluOpType
ACT = mybir.ActivationFunctionType
AX = mybir.AxisListType

B, T, D = 8, 512, 128
TT = T // 128
H, DH = 16, 8
LAT = 32
FF0 = 384
FT0 = FF0 // 128
DI, N = 256, 16
ST = DI // 128
GROUPS = DI * N // 128
CONV = 4
RDT = 64
E = 8
FF1 = 256
FT1 = FF1 // 128
UNITS = (E + 1) * FT1
EPS = 1e-5


class Count:

    def __init__(self, sem, per, by=1):
        self.sem, self.per, self.by = sem, per, by
        self.start = 2 * per * by

    def at(self, b, n=None):
        n = self.per if n is None else n
        return (b + 1) * (self.per * self.by) + n * self.by


def constants():
    inv = (1.0 / np.float32(10000.0) ** (np.arange(0, DH, 2, dtype=np.float32) / np.float32(DH))).astype(np.float32)
    angle = (np.arange(T, dtype=np.float32)[None, :] * inv[:, None]).astype(np.float32).astype(np.float64)
    dim = np.arange(128) % DH
    cos = np.cos(angle)[dim % (DH // 2)]
    sin = np.sin(angle)[dim % (DH // 2)] * np.where(dim < DH // 2, -1.0, 1.0)[:, None]
    scale = 1.0 / np.sqrt(DH)
    rope = np.stack([cos * scale, sin * scale, cos, sin]).astype(np.float32)
    rope = np.ascontiguousarray(rope.reshape(4, 128, TT, 128).transpose(3, 0, 2, 1))
    ident = np.eye(128, dtype=np.float32)
    spread = np.zeros((3, 32, 4, 128), np.float32)
    for i in range(4):
        for p in range(128):
            spread[:, i * 8 + p // N, i, p] = 1
    gather = np.zeros((128, 4, 32), np.float32)
    for i in range(4):
        for p in range(128):
            gather[p, i, i * 8 + p // N] = 1
    pick = np.tile(np.eye(E, dtype=np.float32)[None, :, :, None], (3, 1, 1, 128))
    before = np.tile((np.arange(E)[None, :] < np.arange(E)[:, None]).astype(np.float32)[None], (128, 1, 1))
    return {
        "c_rope": rope,
        "c_ident": ident,
        "c_spread": spread.reshape(96, 4, 128),
        "c_gather": gather,
        "c_pick": pick.reshape(3 * E, E, 128),
        "c_before": before,
    }


def program(nc, io, out):
    dram = nc.dram_tensor("layer0_out", (B, T, D), F32, kind="Internal").ap()
    with ExitStack() as ctx:
        keep_sb = ctx
        counts = {}

        def sem(name):
            return ctx.enter_context(nc.semaphore(name))

        def sb(name, shape, dt=F32, where=None):
            return (where or keep_sb).enter_context(nc.sbuf_tensor(name, shape, dt))

        ident = sb("ident", [128, 128])
        win = sb("win", [128, 2 * DI])
        wx_dt = sb("wx_dt", [128, ST, RDT])
        wx_b = sb("wx_b", [128, ST, 128])
        wx_c = sb("wx_c", [128, ST, 128])
        wdt = sb("wdt", [RDT, DI])
        wo1 = sb("wo1", [128, ST, D])
        wgate = sb("wgate", [128, E])
        vecs = sb("vecs", [128, 1 + ST * (CONV + 3)])
        a_log = sb("a_log", [128, GROUPS])
        gather = sb("gather", [128, 4, 32])
        before = sb("before", [128, E, E])
        norm_w = vecs[:, 0:1]
        conv_w = vecs[:, 1:1 + ST * CONV].rearrange("p (s k) -> p s k", s=ST)
        conv_b = vecs[:, 1 + ST * CONV:1 + ST * (CONV + 1)]
        dt_b = vecs[:, 1 + ST * (CONV + 1):1 + ST * (CONV + 2)]
        d_skip = vecs[:, 1 + ST * (CONV + 2):1 + ST * (CONV + 3)]
        w_loaded = sem("w_loaded")
        layer1_loads = [
            (win, "win"), (wx_dt, "wx_dt"), (wx_b, "wx_b"), (wx_c, "wx_c"),
            (wdt, "wdt"), (wo1, "wo1"), (wgate, "wgate"), (vecs, "vecs"), (a_log, "a_log"), (gather, "c_gather"),
            (before, "c_before"),
        ]
        minus_half = sb("minus_half", [128, TT])
        own_wait = sem("own_wait")
        stored0 = sem("stored0")

        def hold(eng):
            eng.sem_inc(own_wait, 1)

        layer0(nc, ctx, io, dram, ident, minus_half, w_loaded, layer1_loads, stored0, hold)
        layer1(nc, ctx, io, dram, out, ident, minus_half, w_loaded, len(layer1_loads), stored0, hold,
               dict(win=win, wx_dt=wx_dt, wx_b=wx_b, wx_c=wx_c, wdt=wdt, wo1=wo1, wgate=wgate,
                    norm_w=norm_w, conv_w=conv_w, conv_b=conv_b, dt_b=dt_b, d_skip=d_skip, a_log=a_log,
                    gather=gather, before=before))


def layer0(nc, outer, io, dram, ident, minus_half, w_loaded, layer1_loads, stored0, hold):
    with ExitStack() as ctx:
        def sb(name, shape, dt=F32):
            return ctx.enter_context(nc.sbuf_tensor(name, shape, dt))

        def ps(name, shape, dt=F32):
            return ctx.enter_context(nc.psum_tensor(name, shape, dt))

        def count(name, per, by=1):
            return Count(outer.enter_context(nc.semaphore(name)), per, by)

        wq = sb("wq", [128, 2, 128])
        wdown = sb("wdown", [128, LAT])
        wup = sb("wup", [LAT + 1, 3, 128])
        wout = sb("wout", [128, D])
        bq = sb("bq", [128, 2, 128])
        bdown = sb("bdown", [LAT, 1])
        bout = sb("bout", [128, D])
        rope = sb("rope", [128, 4, TT, 128])
        wg_i = sb("wg_i", [128, FF0], I32)
        wu_i = sb("wu_i", [128, FF0], I32)
        wd_i = sb("wd_i", [128, FT0, D], I32)
        wg = sb("wg", [128, FF0], BF16)
        wu = sb("wu", [128, FF0], BF16)
        wd = sb("wd", [128, FT0, D])
        q_bias = sb("q_bias", [128, 2, TT, 128])
        x = sb("x", [128, 2, TT, D])
        stats = sb("stats", [128, TT, 6])
        mv = sb("mv", [128, TT, 2])
        ve = sb("ve", [128, TT])
        rstd = sb("rstd", [128, TT])
        xn = sb("xn", [128, TT, D])
        xt = sb("xt", [128, T])
        xp = sb("xp", [128, 3, T], BF16)
        xrest = sb("xrest", [128, T])
        lat = sb("lat", [LAT + 1, T])
        turn = sb("turn", [128, 4, TT, 128])
        rq = sb("rq", [128, TT, H, DH])
        rk = sb("rk", [128, TT, H, DH])
        v = sb("v", [128, TT, H, DH])
        prod = sb("prod", [128, TT, H * H * DH])
        sc = sb("sc", [128, TT, H, H])
        negmax = sb("negmax", [128, TT, H])
        den = sb("den", [128, TT, H])
        rden = sb("rden", [128, TT, H])
        raw = sb("raw", [128, TT, H, DH])
        attn = sb("attn", [128, TT, D])
        attn_t = sb("attn_t", [128, T])
        hid = sb("hid", [128, FT0, T])
        xb = sb("xb", [128, TT, D])
        xf = sb("xf", [128, TT, D])
        x1 = sb("x1", [128, 2, TT, D])

        p_misc = ps("p_misc", [128, T])

        loaded0 = outer.enter_context(nc.semaphore("loaded0"))
        setup = outer.enter_context(nc.semaphore("setup"))
        small_loads = [(ident, "c_ident"), (wq, "wq"), (wdown, "wdown"), (wup, "wup"), (wout, "wout"),
                       (bq, "bq"), (bdown, "bdown"), (bout, "bout"), (rope, "c_rope"),
                       (wg_i, "wg"), (wu_i, "wu"), (wd_i, "wd")]

        x_in = count("x_in", 1, 16)
        ln_stats = count("ln_stats", 2)
        ln_var = count("ln_var", 1)
        ln_rstd = count("ln_rstd", 1)
        ln_done = count("ln_done", 1)
        (XT, Q, QS, LATENT, K, KS, V, GATE0, GATE1, GATE2, UP0, UP1, UP2, DOWN, AT, PROJ) = range(1, 17)
        full = count("full", PROJ)
        free = count("free", PROJ)
        x_rest = count("x_rest", 1)
        x_mid = count("x_mid", 1)
        x_low = count("x_low", 1)
        rope_sum = count("rope_sum", 3)
        xb_done = count("xb_done", 1)
        products = count("products", TT - 1)
        products_pool = count("products_pool", 1)
        scored = count("scored", TT)
        soft = count("soft", 2)
        exp_done = count("exp_done", 1)
        den_step = count("den_step", 2)
        weighed = count("weighed", TT - 1)
        weighed_pool = count("weighed_pool", 1)
        summed = count("summed", TT)
        attn_done = count("attn_done", 1)
        stored = count("stored", 1, 16)

        x_d = io["x"].rearrange("b (t p) d -> b p t d", p=128)
        x1_d = dram.rearrange("b (t p) d -> b p t d", p=128)
        block = ctx.enter_context(nc.Block())

        def start(eng, mine):
            for c in mine:
                eng.sem_inc(c.sem, c.start)

        def score_products(eng, t):
            return eng.tensor_tensor(prod[:, t].rearrange("p (h g d) -> p h g d", h=H, g=H),
                                     rq[:, t].unsqueeze(2).to_broadcast([128, H, H, DH]),
                                     rk[:, t].unsqueeze(1).to_broadcast([128, H, H, DH]), ALU.mult)

        def value_products(eng, t):
            return eng.tensor_tensor(prod[:, t].rearrange("p (h d g) -> p h d g", h=H, g=H),
                                     sc[:, t].unsqueeze(2).to_broadcast([128, H, DH, H]),
                                     v[:, t].rearrange("p g d -> p d g").unsqueeze(1).to_broadcast([128, H, DH, H]), ALU.mult)

        @block.sync
        def _(sp):
            start(sp, [x_in, stored])
            sp.dma_start(x[:, 0], x_d[0]).then_inc(x_in.sem, 16)
            for tile, name in small_loads:
                sp.dma_start(tile[:], io[name]).then_inc(loaded0, 16)
            for tile, name in layer1_loads:
                sp.dma_start(tile[:], io[name]).then_inc(w_loaded, 16)

            def load_next(b, p):
                sp.wait_ge(xb_done.sem, xb_done.at(b - 1))
                hold(sp)
                sp.wait_ge(ln_done.sem, ln_done.at(b))
                hold(sp)
                sp.dma_start(x[:, 1 - p], x_d[bass.ds(b % B, 1)].rearrange("o p t d -> p (o t) d"))\
                    .then_inc(x_in.sem, 16)

            def store(b, p):
                sp.wait_ge(free.sem, free.at(b, PROJ))
                hold(sp)
                sp.dma_start(x1_d[bass.ds(b - 1, 1)].rearrange("o p t d -> p (o t) d"), x1[:, p]).then_inc(stored.sem, 16)

            with sp.Fori(0, B // 2) as pair:
                for p in range(2):
                    b = pair * 2 + (1 + p)
                    load_next(b, p)
                    store(b, p)
            sp.wait_ge(stored.sem, stored.at(B))
            sp.wait_ge(x_in.sem, x_in.at(B + 1))
            sp.sem_inc(stored0, 1)

        @block.gpsimd
        def _(pool):
            start(pool, [ln_rstd, x_rest, x_low, rope_sum, xb_done, products_pool, weighed_pool])
            nc.gpsimd.memset(minus_half[:], -0.5).then_inc(setup, 1)
            pool.wait_ge(setup, 1)
            nc.gpsimd.memset(lat[LAT:LAT + 1, :], 1.0).then_inc(setup, 1)
            pool.wait_ge(loaded0, 16 * len(small_loads))
            pool.wait_ge(setup, 2)

            def prep(b, p):
                pool.wait_ge(ln_var.sem, ln_var.at(b))
                nc.gpsimd.tensor_tensor(rstd[:], ve[:], minus_half[:], ALU.pow).then_inc(ln_rstd.sem, 1)
                pool.wait_ge(free.sem, free.at(b - 1, DOWN))
                bias = bout[:].unsqueeze(1).to_broadcast([128, TT, D])
                nc.gpsimd.tensor_tensor(xb[:], x[:, p], bias, ALU.add).then_inc(xb_done.sem, 1)
                pool.wait_ge(free.sem, free.at(b, XT))
                nc.gpsimd.tensor_tensor(xrest[:], xt[:], xp[:, 0], ALU.subtract).then_inc(x_rest.sem, 1)
                pool.wait_ge(x_mid.sem, x_mid.at(b))
                nc.gpsimd.tensor_tensor(xp[:, 2], xrest[:], xp[:, 1], ALU.subtract).then_inc(x_low.sem, 1)
                pool.wait_ge(free.sem, free.at(b, QS))
                nc.gpsimd.tensor_tensor(turn[:, 0], turn[:, 0], turn[:, 1], ALU.add).then_inc(rope_sum.sem, 1)
                pool.wait_ge(rope_sum.sem, rope_sum.at(b, 1))
                nc.gpsimd.tensor_tensor(rq[:].rearrange("p t h d -> p t (h d)"), turn[:, 0], q_bias[:, 0], ALU.add)\
                    .then_inc(rope_sum.sem, 1)
                pool.wait_ge(free.sem, free.at(b, KS))
                nc.gpsimd.tensor_tensor(rk[:].rearrange("p t h d -> p t (h d)"), turn[:, 2], turn[:, 3], ALU.add)\
                    .then_inc(rope_sum.sem, 1)

            with pool.Fori(0, B // 2) as pair:
                for p in range(2):
                    b = pair * 2 + (1 + p)
                    prep(b, p)
                    pool.wait_ge(rope_sum.sem, rope_sum.at(b))
                    score_products(nc.gpsimd, TT - 1).then_inc(products_pool.sem, 1)
                    pool.wait_ge(exp_done.sem, exp_done.at(b))
                    pool.wait_ge(scored.sem, scored.at(b))
                    value_products(nc.gpsimd, TT - 1).then_inc(weighed_pool.sem, 1)

        @block.scalar
        def _(act):
            start(act, [x_mid, exp_done])
            act.wait_ge(loaded0, 16 * len(small_loads))
            act.wait_ge(setup, 2)

            def prep(b, p):
                act.wait_ge(full.sem, full.at(b, XT))
                act.wait_ge(x_low.sem, x_low.at(b - 1))
                nc.scalar.activation(xt[:], p_misc[:], ACT.Copy)
                nc.scalar.activation(xp[:, 0], p_misc[:], ACT.Copy).then_inc(free.sem, 1)
                act.wait_ge(x_rest.sem, x_rest.at(b))
                nc.scalar.activation(xp[:, 1], xrest[:], ACT.Copy).then_inc(x_mid.sem, 1)
                act.wait_ge(full.sem, full.at(b, LATENT))
                nc.scalar.activation(lat[0:LAT], p_misc[0:LAT, :], ACT.Identity, bias=bdown[:, 0:1]).then_inc(free.sem, 1)
                act.wait_ge(full.sem, full.at(b, V))
                nc.scalar.activation(v[:].rearrange("p t h d -> p (t h d)"), p_misc[:], ACT.Copy).then_inc(free.sem, 1)
                for f in range(FT0):
                    act.wait_ge(full.sem, full.at(b, GATE0 + f))
                    nc.scalar.activation(hid[:, f], p_misc[:], ACT.Silu, scale=1.0 / 127.0).then_inc(free.sem, 1)

            def soften(b):
                act.wait_ge(soft.sem, soft.at(b, 2))
                nc.scalar.activation(sc[:], sc[:], ACT.Exp).then_inc(exp_done.sem, 1)

            def final(b):
                act.wait_ge(full.sem, full.at(b, AT))
                nc.scalar.activation(attn_t[:], p_misc[:], ACT.Copy).then_inc(free.sem, 1)

            with act.Fori(0, B // 2) as pair:
                for p in range(2):
                    b = pair * 2 + (1 + p)
                    prep(b, p)
                    soften(b)
                    final(b)

        @block.vector
        def _(dve):
            start(dve, [ln_stats, ln_var, ln_done, free, products, scored, soft, den_step, weighed, summed, attn_done])
            dve.wait_ge(loaded0, 16 * len(small_loads))
            dve.wait_ge(setup, 2)
            nc.vector.tensor_copy(wg[:], wg_i[:]).then_inc(setup, 1)
            nc.vector.tensor_copy(wu[:], wu_i[:]).then_inc(setup, 1)
            nc.vector.tensor_copy(wd[:], wd_i[:]).then_inc(setup, 1)
            for s in range(2):
                nc.vector.tensor_tensor(q_bias[:, s], rope[:, s], bq[:, s].unsqueeze(1).to_broadcast([128, TT, 128]), ALU.mult)\
                    .then_inc(setup, 1)
            dve.wait_ge(setup, 7)
            nc.vector.tensor_tensor(q_bias[:, 0], q_bias[:, 0], q_bias[:, 1], ALU.add).then_inc(setup, 1)
            dve.wait_ge(setup, 8)

            def norm(b, p):
                dve.wait_ge(x_in.sem, x_in.at(b))
                for t in range(TT):
                    ins = nc.vector.bn_stats(stats[:, t], x[:, p, t])
                ins.then_inc(ln_stats.sem, 1)
                dve.wait_ge(ln_stats.sem, ln_stats.at(b, 1))
                hold(dve)
                for t in range(TT):
                    ins = nc.vector.bn_aggr(mv[:, t], stats[:, t])
                ins.then_inc(ln_stats.sem, 1)
                dve.wait_ge(ln_stats.sem, ln_stats.at(b, 2))
                nc.vector.tensor_scalar(ve[:], mv[:, :, 1], EPS, None, ALU.add).then_inc(ln_var.sem, 1)
                dve.wait_ge(ln_rstd.sem, ln_rstd.at(b))
                dve.wait_ge(full.sem, full.at(b - 1, XT))
                for t in range(TT):
                    ins = nc.vector.tensor_scalar(xn[:, t], x[:, p, t], mv[:, t, 0:1], rstd[:, t:t + 1], ALU.subtract, ALU.mult)
                ins.then_inc(ln_done.sem, 1)

            def turns(b):
                for s, step in enumerate((Q, QS, K, KS)):
                    dve.wait_ge(full.sem, full.at(b, step))
                    if s % 2 == 0:
                        dve.wait_ge(rope_sum.sem, rope_sum.at(b - 1))
                    nc.vector.tensor_tensor(turn[:, s], p_misc[:].rearrange("p (t c) -> p t c", t=TT), rope[:, s], ALU.mult)\
                        .then_inc(free.sem, 1)

            def attention(b):
                dve.wait_ge(rope_sum.sem, rope_sum.at(b))
                dve.wait_ge(summed.sem, summed.at(b - 1))
                for t in range(TT - 1):
                    score_products(nc.vector, t).then_inc(products.sem, 1)
                for t in range(TT):
                    if t < TT - 1:
                        dve.wait_ge(products.sem, products.at(b, t + 1))
                    else:
                        dve.wait_ge(products_pool.sem, products_pool.at(b))
                    nc.vector.tensor_reduce(sc[:, t], prod[:, t].rearrange("p (h g d) -> p h g d", h=H, g=H), AX.X, ALU.add)\
                        .then_inc(scored.sem, 1)
                dve.wait_ge(scored.sem, scored.at(b))
                nc.vector.tensor_reduce(negmax[:], sc[:], AX.X, ALU.max, negate=True).then_inc(soft.sem, 1)
                dve.wait_ge(soft.sem, soft.at(b, 1))
                nc.vector.tensor_tensor(sc[:], sc[:], negmax[:].unsqueeze(3).to_broadcast([128, TT, H, H]), ALU.add)\
                    .then_inc(soft.sem, 1)
                dve.wait_ge(exp_done.sem, exp_done.at(b))
                for t in range(TT - 1):
                    value_products(nc.vector, t).then_inc(weighed.sem, 1)
                nc.vector.tensor_reduce(den[:], sc[:], AX.X, ALU.add).then_inc(den_step.sem, 1)
                for t in range(TT):
                    if t < TT - 1:
                        dve.wait_ge(weighed.sem, weighed.at(b, t + 1))
                    else:
                        dve.wait_ge(weighed_pool.sem, weighed_pool.at(b))
                    nc.vector.tensor_reduce(raw[:, t], prod[:, t].rearrange("p (h d g) -> p h d g", h=H, g=H), AX.X, ALU.add)\
                        .then_inc(summed.sem, 1)
                dve.wait_ge(den_step.sem, den_step.at(b, 1))
                hold(dve)
                nc.vector.reciprocal(rden[:], den[:]).then_inc(den_step.sem, 1)
                dve.wait_ge(den_step.sem, den_step.at(b, 2))
                dve.wait_ge(summed.sem, summed.at(b))
                nc.vector.tensor_tensor(attn[:].rearrange("p t (h d) -> p t h d", h=H), raw[:],
                                        rden[:].unsqueeze(3).to_broadcast([128, TT, H, DH]), ALU.mult).then_inc(attn_done.sem, 1)

            def ffn(b):
                for f in range(FT0):
                    dve.wait_ge(full.sem, full.at(b, UP0 + f))
                    nc.vector.scalar_tensor_tensor(hid[:, f], p_misc[:], 1.0 / 127.0 ** 2, hid[:, f],
                                                   ALU.mult, ALU.mult).then_inc(free.sem, 1)
                dve.wait_ge(full.sem, full.at(b, DOWN))
                dve.wait_ge(xb_done.sem, xb_done.at(b))
                nc.vector.tensor_tensor(xf[:], p_misc[:].rearrange("p (t d) -> p t d", t=TT), xb[:], ALU.add)\
                    .then_inc(free.sem, 1)

            def final(b, p):
                dve.wait_ge(full.sem, full.at(b, PROJ))
                dve.wait_ge(stored.sem, stored.at(b - 2))
                dve.wait_ge(free.sem, free.at(b, AT))
                nc.vector.tensor_tensor(x1[:, p], p_misc[:].rearrange("p (t d) -> p t d", t=TT), xf[:], ALU.add)\
                    .then_inc(free.sem, 1)

            with dve.Fori(0, B // 2) as pair:
                for p in range(2):
                    b = pair * 2 + (1 + p)
                    norm(b, p)
                    turns(b)
                    ffn(b)
                    attention(b)
                    final(b, p)

        @block.tensor
        def _(pe):
            start(pe, [full])
            pe.wait_ge(loaded0, 16 * len(small_loads))
            pe.wait_ge(setup, 8)

            def ready(b, n):
                pe.wait_ge(free.sem, free.at(b, n))

            def by_tile(b, step, lhs, rhs):
                ready(b, step - 1)
                for t in range(TT):
                    ins = nc.tensor.matmul(p_misc[:, bass.ts(t, 128)], lhs[:, bass.ts(t, 128)], rhs, start=True, stop=True)
                ins.then_inc(full.sem, 1)

            def turned(src):
                for t in range(TT):
                    ins = nc.tensor.transpose(p_misc[:, bass.ts(t, 128)], src[:, t], ident[:])
                ins.then_inc(full.sem, 1)

            def prep(b):
                ready(b - 1, PROJ)
                pe.wait_ge(ln_done.sem, ln_done.at(b))
                turned(xn)
                by_tile(b, Q, xt, wq[:, 0])
                by_tile(b, QS, xt, wq[:, 1])
                ready(b, QS)
                nc.tensor.matmul(p_misc[0:LAT], wdown[:], xt[:], start=True, stop=True).then_inc(full.sem, 1)
                by_tile(b, K, lat, wup[:, 0])
                by_tile(b, KS, lat, wup[:, 1])
                by_tile(b, V, lat, wup[:, 2])

            def ffn(b):
                pe.wait_ge(x_low.sem, x_low.at(b))
                for n in range(2 * FT0):
                    ready(b, GATE0 + n - 1)
                    w = wg if n < FT0 else wu
                    for i in range(3):
                        ins = nc.tensor.matmul(p_misc[:], w[:, bass.ts(n % FT0, 128)], xp[:, i], start=(i == 0), stop=(i == 2))
                    ins.then_inc(full.sem, 1)
                ready(b, UP2)
                for t in range(TT):
                    for f in range(FT0):
                        ins = nc.tensor.matmul(p_misc[:, bass.ts(t, 128)], hid[:, f, bass.ts(t, 128)], wd[:, f],
                                               start=(f == 0), stop=(f == FT0 - 1))
                ins.then_inc(full.sem, 1)

            def project(b):
                ready(b, DOWN)
                pe.wait_ge(attn_done.sem, attn_done.at(b))
                turned(attn)
                by_tile(b, PROJ, attn_t, wout[:])

            with pe.Fori(0, B // 2) as pair:
                for p in range(2):
                    b = pair * 2 + (1 + p)
                    prep(b)
                    ffn(b)
                    project(b)


def layer1(nc, outer, io, dram, out, ident, minus_half, w_loaded, n_loads, stored0, hold, w):
    with ExitStack() as ctx:
        def sb(name, shape, dt=F32):
            return ctx.enter_context(nc.sbuf_tensor(name, shape, dt))

        def ps(name, shape, dt=F32):
            return ctx.enter_context(nc.psum_tensor(name, shape, dt))

        def count(name, per, by=1):
            return Count(outer.enter_context(nc.semaphore(name)), per, by)

        ND = 4
        NA = 8
        w1 = sb("w1", [128, E + 1, FF1])
        w3 = sb("w3", [128, E + 1, FF1])
        w2 = sb("w2", [128, E + 1, FT1, D])
        spread = sb("spread", [96, 4, 128], BF16)
        pick = sb("pick", [3 * E, E, 128], BF16)
        ident_b = sb("ident_b", [128, 128], BF16)
        a_neg = sb("a_neg", [128, GROUPS])
        x = sb("y_x", [128, 2, TT, D])
        stats = sb("y_stats", [128, TT, 6])
        mv = sb("y_mv", [128, TT, 2])
        ve = sb("y_ve", [128, 2, TT])
        rstd = sb("y_rstd", [128, 2, TT])
        xn = sb("y_xn", [128, 2, TT, D])
        xr = sb("y_xr", [128, 2, TT, D])
        xt = sb("y_xt", [128, 2, T])
        ht = sb("y_ht", [128, T])
        ur = sb("ur", [128, ST, CONV - 1 + T])
        conv = sb("conv", [128, 2, ST, T])
        u = sb("u", [128, 2, ST, T])
        sz = sb("sz", [128, 2, ST, T])
        dtr = sb("dtr", [RDT, T])
        b_rep = sb("b_rep", [128, 2, T])
        c_rep = sb("c_rep", [128, 2, T])
        dtu = sb("dtu", [128, 2, ST, T])
        ez, rz = dtu[:, 0], dtu[:, 1]
        az, wz = conv[:, 0], conv[:, 1]
        rest = conv
        part = sb("y_part", [128, 3, 2, ST, T], BF16)
        block_in = sb("block_in", [96, 2, ST, 4, T], BF16)
        eg = sb("eg", [128, TT, E])
        gates = sb("gates", [128, 2, TT, E])
        rank2 = sb("rank2", [128, 2, TT, E, E])
        rank = sb("rank", [128, TT, E])
        wsum = sb("wsum", [128, 2, TT])
        wpart = sb("wpart", [128, TT, 3, E], BF16)
        wrest = sb("wrest", [128, TT, E])
        wt = sb("wt", [3 * E, T], BF16)
        xw = sb("xw", [128, E + 1, T])
        da = sb("da", [128, ND, T])
        dbu = sb("dbu", [128, 3, T])
        hs = sb("hs", [128, 4, T])
        hc = sb("hc", [128, NA, T])
        y1 = sb("y1", [128, T])
        yt = sb("yt", [128, ST, T])
        sg = sb("sg", [128, 2, T])
        hid = sb("y_hid", [128, 2, T])
        ot = sb("ot", [128, T])

        p_misc = ps("y_misc", [128, T])
        p_dt = ps("p_dt", [128, 2, T])
        p_du = ps("p_du", [128, T])
        p_y = ps("p_y", [128, T])
        p_g = ps("p_g", [128, T])
        p_u = ps("p_u", [128, T])
        p_acc = ps("p_acc", [128, T])

        begun = outer.enter_context(nc.semaphore("begun"))
        staged = outer.enter_context(nc.semaphore("staged"))
        experts_in = outer.enter_context(nc.semaphore("experts_in"))
        x_in = count("y_in", 1, 16)
        ln_stats = count("y_ln_stats", 4)
        ln_var = count("y_ln_var", 2)
        ln_rstd = count("y_ln_rstd", 2)
        ln_done = count("y_ln_done", 2)
        xr_done = count("y_xr_done", 1)
        (XT, HT, U0, U1, Z0, Z1, DTR, BREP, CREP, DT0, DT1, GATE, WT, WB) = range(1, 15)
        PREP = WB + E - 1
        prep_full = count("y_prep_full", PREP)
        prep_free = count("y_prep_free", PREP)
        x_third = count("x_third", 1)
        conv_step = count("conv_step", 2 * CONV)
        u_done = count("u_done", 2)
        sp_exp = count("sp_exp", 1)
        sp_one = count("sp_one", 1)
        sp_ln = count("sp_ln", 1)
        sp_cut = count("sp_cut", 1)
        dt_step = count("dt_step", 2)
        part1 = count("y_part1", 1)
        rest1 = count("y_rest1", 1)
        part2 = count("y_part2", 1)
        part3 = count("y_part3", 1)
        stacked = [count(f"y_stacked{i}", 3 * 4, 16) for i in range(ST)]
        gate_exp = count("gate_exp", 1)
        route = count("route", 16)
        dt_full = count("dt_full", GROUPS)
        du_full = count("du_full", GROUPS)
        da_done = count("da_done", GROUPS)
        dbu_done = count("dbu_done", GROUPS)
        scanned = count("scanned", GROUPS)
        hc_done = count("hc_done", GROUPS)
        gathered = count("gathered", GROUPS // 4)
        y1_done = count("y1_done", ST)
        y_done = count("y_done", ST)
        g_full = count("g_full", UNITS)
        g_read = count("g_read", UNITS)
        u_full = count("u_full", UNITS)
        hid_done = count("hid_done", UNITS)
        hid_used = count("hid_used", UNITS)
        acc_full = count("acc_full", 1)
        acc_read = count("acc_read", 1)
        back_full = count("back_full", 1)
        res_done = count("res_done", 1)
        stored = count("y_stored", 1, 16)

        x_d = dram.rearrange("b (t p) d -> b p t d", p=128)
        out_d = out.rearrange("b (t p) d -> b p t d", p=128)

        order = [(s, j, i) for s in range(ST) for i in range(4) for j in range(4)]

        block = ctx.enter_context(nc.Block())

        def start(eng, mine):
            for c in mine:
                eng.sem_inc(c.sem, c.start)

        @block.sync
        def _(sp):
            start(sp, [x_in, *stacked, stored])
            sp.dma_start(da[0:3 * E, 0:2], io["c_pick"].rearrange("r (a e) c -> r a (e c)", a=2)).then_inc(staged, 16)
            sp.dma_start(da[0:96, 2], io["c_spread"].rearrange("r i c -> r (i c)")).then_inc(staged, 16)
            sp.wait_ge(stored0, 1)
            sp.dma_start(x[:, 0], x_d[0]).then_inc(x_in.sem, 16)
            for tile, name in ((w1, "w1"), (w3, "w3"), (w2, "w2")):
                sp.dma_start(tile[:], io[name]).then_inc(experts_in, 16)

            def load_next(b, p):
                sp.wait_ge(xr_done.sem, xr_done.at(b - 1))
                hold(sp)
                sp.wait_ge(ln_done.sem, ln_done.at(b))
                hold(sp)
                sp.dma_start(x[:, 1 - p], x_d[bass.ds(b % B, 1)].rearrange("o p t d -> p (o t) d"))\
                    .then_inc(x_in.sem, 16)

            def stack(b, p):
                sp.wait_ge(part3.sem, part3.at(b))
                hold(sp)
                for s in range(ST):
                    sp.wait_ge(du_full.sem, du_full.at(b - 1, GROUPS // ST * (s + 1)))
                    hold(sp)
                    for i in range(3):
                        for c in range(4):
                            sp.dma_start(block_in[32 * i:32 * i + 32, :, s, c], part[32 * c:32 * c + 32, i, :, s])\
                                .then_inc(stacked[s].sem, 16)

            def store(b, p):
                sp.wait_ge(res_done.sem, res_done.at(b))
                hold(sp)
                sp.dma_start(out_d[bass.ds(b - 1, 1)].rearrange("o p t d -> p (o t) d"), xr[:, p]).then_inc(stored.sem, 16)

            with sp.Fori(0, B // 2) as pair:
                for p in range(2):
                    b = pair * 2 + (1 + p)
                    load_next(b, p)
                    stack(b, p)
                    store(b, p)
            sp.wait_ge(stored.sem, stored.at(B))
            hold(sp)
            sp.wait_ge(x_in.sem, x_in.at(B + 1))
            hold(sp)

        @block.gpsimd
        def _(pool):
            start(pool, [ln_rstd, xr_done, dt_step, rest1, part3, hc_done, y_done])
            nc.gpsimd.memset(ur[:, :, 0:CONV - 1], 0.0).then_inc(begun, 1)
            pool.wait_ge(begun, 5)

            def norm(b, p):
                for i in range(2):
                    pool.wait_ge(ln_var.sem, ln_var.at(b, i + 1))
                    nc.gpsimd.tensor_tensor(rstd[:, i], ve[:, i], minus_half[:], ALU.pow).then_inc(ln_rstd.sem, 1)
                pool.wait_ge(ln_done.sem, ln_done.at(b, 1))
                pool.wait_ge(stored.sem, stored.at(b - 2))
                nc.gpsimd.tensor_tensor(xr[:, p], x[:, p], xn[:, 0], ALU.add).then_inc(xr_done.sem, 1)

            def steps(b, p):
                pool.wait_ge(sp_cut.sem, sp_cut.at(b))
                nc.gpsimd.tensor_tensor(dtu[:, 0], ez, rz, ALU.add).then_inc(dt_step.sem, 1)
                pool.wait_ge(dt_step.sem, dt_step.at(b, 1))
                pool.wait_ge(u_done.sem, u_done.at(b))
                nc.gpsimd.tensor_tensor(dtu[:, 1], dtu[:, 0], u[:, p], ALU.mult).then_inc(dt_step.sem, 1)
                pool.wait_ge(part1.sem, part1.at(b))
                pool.wait_ge(dt_step.sem, dt_step.at(b, 2))
                nc.gpsimd.tensor_tensor(rest[:], dtu[:], part[:, 0], ALU.subtract).then_inc(rest1.sem, 1)
                pool.wait_ge(part2.sem, part2.at(b))
                nc.gpsimd.tensor_tensor(part[:, 2], rest[:], part[:, 1], ALU.subtract).then_inc(part3.sem, 1)

            def times_c(b, p, k):
                pool.wait_ge(scanned.sem, scanned.at(b, k + 1))
                if k % 4 == 0:
                    pool.wait_ge(gathered.sem, gathered.at(b, k // 4 - 1) if k >= 8 else gathered.at(b - 1, 7 + k // 4))
                nc.gpsimd.tensor_tensor(hc[:, k % NA], hs[:, k % 4], c_rep[:, p], ALU.mult).then_inc(hc_done.sem, 1)

            def gate_y(b, p, s):
                pool.wait_ge(y1_done.sem, y1_done.at(b, s + 1))
                if s == 0:
                    pool.wait_ge(acc_full.sem, acc_full.at(b - 1))
                nc.gpsimd.tensor_tensor(yt[:, s], y1[:], sz[:, p, s], ALU.mult).then_inc(y_done.sem, 1)

            with pool.Fori(0, B // 2) as pair:
                for p in range(2):
                    b = pair * 2 + (1 + p)
                    norm(b, p)
                    steps(b, p)
                    for k in range(GROUPS):
                        times_c(b, p, k)
                        if k % 16 == 15:
                            gate_y(b, p, k // 16)

        @block.scalar
        def _(act):
            start(act, [prep_free, x_third, u_done, sp_exp, sp_ln, part1, part2, gate_exp, da_done, g_read, acc_read])
            act.wait_ge(w_loaded, 16 * n_loads)
            nc.scalar.activation(a_neg[:], w["a_log"][:], ACT.Exp).then_inc(begun, 1)
            act.wait_ge(begun, 5)

            def full(b, n):
                act.wait_ge(prep_full.sem, prep_full.at(b, n))

            def copy_out(b, n, to, rows=slice(0, 128), func=ACT.Copy, **how):
                full(b, n)
                nc.scalar.activation(to, p_misc[rows, :], func, **how).then_inc(prep_free.sem, 1)

            def project(b, p):
                copy_out(b, XT, xt[:, p])
                act.wait_ge(prep_free.sem, prep_free.at(b, XT))
                nc.scalar.activation(xw[:, E], xt[:, p], ACT.Copy, scale=1.0 / 3.0).then_inc(x_third.sem, 1)
                copy_out(b, HT, ht[:], scale=w["norm_w"])
                copy_out(b, U0, ur[:, 0, CONV - 1:])
                copy_out(b, U1, ur[:, 1, CONV - 1:])
                copy_out(b, Z0, sz[:, p, 0], func=ACT.Silu)
                copy_out(b, Z1, sz[:, p, 1], func=ACT.Silu)
                for s in range(ST):
                    act.wait_ge(conv_step.sem, conv_step.at(b, 4 * s + 4))
                    nc.scalar.activation(u[:, p, s], conv[:, 1, s], ACT.Silu, bias=w["conv_b"][:, s:s + 1]).then_inc(u_done.sem, 1)
                copy_out(b, DTR, dtr[:], slice(0, RDT))
                copy_out(b, BREP, b_rep[:, p])
                copy_out(b, CREP, c_rep[:, p])

            def softplus(b):
                for s in range(ST):
                    full(b, DT0 + s)
                    if s == 0:
                        act.wait_ge(dt_step.sem, dt_step.at(b - 1, 1))
                    nc.scalar.activation(rz[:, s], p_misc[:], ACT.Relu, bias=w["dt_b"][:, s:s + 1])
                    nc.scalar.activation(az[:, s], p_misc[:], ACT.Abs, bias=w["dt_b"][:, s:s + 1]).then_inc(prep_free.sem, 1)
                act.wait_ge(prep_free.sem, prep_free.at(b, DT1))
                nc.scalar.activation(ez, az, ACT.Exp, scale=-1.0).then_inc(sp_exp.sem, 1)
                full(b, GATE)
                nc.scalar.activation(eg[:], p_misc[:, 0:TT * E].rearrange("p (t e) -> p t e", e=E), ACT.Exp, scale=-1.0)\
                    .then_inc(prep_free.sem, 1)
                act.wait_ge(sp_one.sem, sp_one.at(b))
                nc.scalar.activation(az, wz, ACT.Ln).then_inc(sp_ln.sem, 1)

            def parts(b):
                act.wait_ge(dt_step.sem, dt_step.at(b, 2))
                for s in range(ST):
                    act.wait_ge(stacked[s].sem, stacked[s].at(b - 1))
                nc.scalar.activation(part[:, 0], dtu[:], ACT.Copy).then_inc(part1.sem, 1)
                act.wait_ge(rest1.sem, rest1.at(b))
                nc.scalar.activation(part[:, 1], rest[:], ACT.Copy).then_inc(part2.sem, 1)

            def decay(b, k):
                s, j, i = order[k]
                g = 16 * s + 4 * j + i
                act.wait_ge(dt_full.sem, dt_full.at(b, k + 1))
                act.wait_ge(scanned.sem, scanned.at(b, k - ND + 1) if k >= ND else scanned.at(b - 1, GROUPS - ND + k + 1))
                nc.scalar.activation(da[:, k % ND], p_dt[:, k % 2], ACT.Exp, scale=a_neg[:, g:g + 1]).then_inc(da_done.sem, 1)

            def gate(b, m):
                act.wait_ge(g_full.sem, g_full.at(b, m + 1))
                act.wait_ge(hid_done.sem, hid_done.at(b, m - 1) if m >= 2 else hid_done.at(b - 1, UNITS - 1 + m))
                nc.scalar.activation(sg[:, m % 2], p_g[:], ACT.Silu).then_inc(g_read.sem, 1)

            with act.Fori(0, B // 2) as pair:
                for p in range(2):
                    b = pair * 2 + (1 + p)
                    project(b, p)
                    softplus(b)
                    parts(b)
                    full(b, WT)
                    nc.scalar.activation(wt[:], p_misc[:].bitcast(BF16)[0:3 * E, 0:T], ACT.Copy).then_inc(prep_free.sem, 1)
                    for k in range(GROUPS):
                        decay(b, k)
                    for m in range(UNITS):
                        gate(b, m)
                    act.wait_ge(acc_full.sem, acc_full.at(b))
                    act.wait_ge(back_full.sem, back_full.at(b - 1))
                    nc.scalar.activation(ot[:], p_acc[:], ACT.Copy).then_inc(acc_read.sem, 1)

        @block.vector
        def _(dve):
            start(dve, [ln_stats, ln_var, ln_done, conv_step, sp_one, sp_cut, route, dbu_done, scanned, y1_done,
                        hid_done, res_done])
            dve.wait_ge(w_loaded, 16 * n_loads)
            dve.wait_ge(staged, 32)
            nc.vector.tensor_copy(spread[:].rearrange("r i c -> r (i c)"), da[0:96, 2]).then_inc(begun, 1)
            nc.vector.tensor_copy(pick[:].rearrange("r (a e) c -> r a (e c)", a=2), da[0:3 * E, 0:2]).then_inc(begun, 1)
            nc.vector.tensor_copy(ident_b[:], ident[:]).then_inc(begun, 1)
            dve.wait_ge(begun, 5)
            nc.vector.tensor_scalar(a_neg[:], a_neg[:], -1.0, None, ALU.mult).then_inc(begun, 1)

            def norm(b, p):
                dve.wait_ge(x_in.sem, x_in.at(b))
                for t in range(TT):
                    ins = nc.vector.bn_stats(stats[:, t], x[:, p, t])
                ins.then_inc(ln_stats.sem, 1)
                dve.wait_ge(ln_stats.sem, ln_stats.at(b, 1))
                hold(dve)
                for t in range(TT):
                    ins = nc.vector.bn_aggr(mv[:, t], stats[:, t])
                ins.then_inc(ln_stats.sem, 1)
                dve.wait_ge(ln_stats.sem, ln_stats.at(b, 2))
                nc.vector.tensor_scalar(ve[:, 0], mv[:, :, 1], EPS, None, ALU.add).then_inc(ln_var.sem, 1)
                dve.wait_ge(ln_rstd.sem, ln_rstd.at(b, 1))
                nc.vector.tensor_tensor(wsum[:, 0], rstd[:, 0], rstd[:, 0], ALU.mult).then_inc(ln_stats.sem, 1)
                dve.wait_ge(ln_stats.sem, ln_stats.at(b, 3))
                nc.vector.tensor_tensor(wsum[:, 1], wsum[:, 0], mv[:, :, 1], ALU.mult).then_inc(ln_stats.sem, 1)
                dve.wait_ge(ln_stats.sem, ln_stats.at(b, 4))
                nc.vector.tensor_scalar(ve[:, 1], wsum[:, 1], EPS, None, ALU.add).then_inc(ln_var.sem, 1)
                dve.wait_ge(prep_full.sem, prep_full.at(b - 1, HT))
                dve.wait_ge(xr_done.sem, xr_done.at(b - 1))
                for t in range(TT):
                    ins = nc.vector.tensor_scalar(xn[:, 0, t], x[:, p, t], mv[:, t, 0:1], rstd[:, 0, t:t + 1],
                                                  ALU.subtract, ALU.mult)
                ins.then_inc(ln_done.sem, 1)
                dve.wait_ge(ln_done.sem, ln_done.at(b, 1))
                dve.wait_ge(ln_rstd.sem, ln_rstd.at(b, 2))
                for t in range(TT):
                    ins = nc.vector.tensor_scalar(xn[:, 1, t], xn[:, 0, t], rstd[:, 1, t:t + 1], None, ALU.mult)
                ins.then_inc(ln_done.sem, 1)

            def convolve(b):
                for s in range(ST):
                    dve.wait_ge(prep_free.sem, prep_free.at(b, U0 + s))
                    if s == 0:
                        dve.wait_ge(part3.sem, part3.at(b - 1))
                    for k in range(CONV):
                        taps = ur[:, s, k:k + T]
                        wk = w["conv_w"][:, s, k:k + 1]
                        if k == 0:
                            ins = nc.vector.tensor_scalar(conv[:, 0, s], taps, wk, None, ALU.mult)
                        else:
                            dve.wait_ge(conv_step.sem, conv_step.at(b, 4 * s + k))
                            ins = nc.vector.scalar_tensor_tensor(conv[:, k % 2, s], taps, wk, conv[:, 1 - k % 2, s],
                                                                 ALU.mult, ALU.add)
                        ins.then_inc(conv_step.sem, 1)

            def softplus(b):
                dve.wait_ge(sp_exp.sem, sp_exp.at(b))
                nc.vector.tensor_scalar(wz, ez, 1.0, None, ALU.add).then_inc(sp_one.sem, 1)

            def softplus_end(b):
                dve.wait_ge(sp_one.sem, sp_one.at(b))
                nc.vector.scalar_tensor_tensor(ez, wz, -1.0, ez, ALU.add, ALU.subtract).then_inc(route.sem, 1)
                dve.wait_ge(sp_ln.sem, sp_ln.at(b))
                dve.wait_ge(route.sem, route.at(b, 1))
                nc.vector.tensor_tensor(ez, az, ez, ALU.subtract).then_inc(sp_cut.sem, 1)

            def routing(b):
                n = [1]

                def link(ins):
                    n[0] += 1
                    ins.then_inc(route.sem, 1)
                    dve.wait_ge(route.sem, route.at(b, n[0]))

                dve.wait_ge(prep_free.sem, prep_free.at(b, GATE))
                link(nc.vector.tensor_scalar(gates[:, 1], eg[:], 1.0, None, ALU.add))
                hold(dve)
                link(nc.vector.reciprocal(gates[:, 0], gates[:, 1]))
                g = gates[:, 0]
                others = g.unsqueeze(2).to_broadcast([128, TT, E, E])
                mine = g.unsqueeze(3).to_broadcast([128, TT, E, E])
                nc.vector.tensor_tensor(rank2[:, 0], others, mine, ALU.is_gt)
                link(nc.vector.tensor_tensor(rank2[:, 1], others, mine, ALU.is_equal))
                first = w["before"][:].unsqueeze(1).to_broadcast([128, TT, E, E])
                link(nc.vector.tensor_tensor(rank2[:, 1], rank2[:, 1], first, ALU.mult))
                link(nc.vector.tensor_tensor(rank2[:, 0], rank2[:, 0], rank2[:, 1], ALU.add))
                link(nc.vector.tensor_reduce(rank[:], rank2[:, 0], AX.X, ALU.add))
                link(nc.vector.scalar_tensor_tensor(gates[:, 1], rank[:], 2.0, g, ALU.is_lt, ALU.mult))
                link(nc.vector.tensor_reduce(wsum[:, 0], gates[:, 1], AX.X, ALU.add))
                link(nc.vector.tensor_scalar(wsum[:, 1], wsum[:, 0], 3.0, None, ALU.mult))
                hold(dve)
                link(nc.vector.reciprocal(wsum[:, 0], wsum[:, 1]))
                link(nc.vector.tensor_tensor(gates[:, 0], gates[:, 1], wsum[:, 0].unsqueeze(2).to_broadcast([128, TT, E]), ALU.mult))
                dve.wait_ge(prep_full.sem, prep_full.at(b - 1, WT))
                link(nc.vector.tensor_copy(wpart[:, :, 0], gates[:, 0]))
                link(nc.vector.tensor_tensor(wrest[:], gates[:, 0], wpart[:, :, 0], ALU.subtract))
                link(nc.vector.tensor_copy(wpart[:, :, 1], wrest[:]))
                link(nc.vector.tensor_tensor(wpart[:, :, 2], wrest[:], wpart[:, :, 1], ALU.subtract))

            def weigh_x(b, p):
                dve.wait_ge(hid_used.sem, hid_used.at(b - 1))
                for e in range(E):
                    dve.wait_ge(prep_full.sem, prep_full.at(b, WB + e))
                    nc.vector.tensor_tensor(xw[:, e], p_misc[:], xt[:, p], ALU.mult).then_inc(prep_free.sem, 1)

            def inject(b, p, k):
                dve.wait_ge(scanned.sem, scanned.at(b, k - 2) if k >= 3 else scanned.at(b - 1, GROUPS - 2 + k))
                dve.wait_ge(du_full.sem, du_full.at(b, k + 1))
                nc.vector.tensor_tensor(dbu[:, k % 3], p_du[:], b_rep[:, p], ALU.mult).then_inc(dbu_done.sem, 1)

            def scan(b, k):
                dve.wait_ge(da_done.sem, da_done.at(b, k + 1))
                dve.wait_ge(dbu_done.sem, dbu_done.at(b, k + 1))
                dve.wait_ge(hc_done.sem, hc_done.at(b, k - 3) if k >= 4 else hc_done.at(b - 1, GROUPS - 3 + k))
                nc.vector.tensor_tensor_scan(hs[:, k % 4], da[:, k % ND], dbu[:, k % 3], 0.0, ALU.mult, ALU.add)\
                    .then_inc(scanned.sem, 1)

            def skip(b, p, s):
                dve.wait_ge(gathered.sem, gathered.at(b, 4 * s + 4))
                dve.wait_ge(y_done.sem, y_done.at(b, s) if s else y_done.at(b - 1))
                nc.vector.scalar_tensor_tensor(y1[:], u[:, p, s], w["d_skip"][:, s:s + 1], p_y[:], ALU.mult, ALU.add)\
                    .then_inc(y1_done.sem, 1)

            def hidden(b, m):
                dve.wait_ge(g_read.sem, g_read.at(b, m + 1))
                dve.wait_ge(u_full.sem, u_full.at(b, m + 1))
                dve.wait_ge(hid_used.sem, hid_used.at(b, m - 1) if m >= 2 else hid_used.at(b - 1, UNITS - 1 + m))
                nc.vector.tensor_tensor(hid[:, m % 2], p_u[:], sg[:, m % 2], ALU.mult).then_inc(hid_done.sem, 1)

            with dve.Fori(0, B // 2) as pair:
                for p in range(2):
                    b = pair * 2 + (1 + p)
                    norm(b, p)
                    convolve(b)
                    softplus(b)
                    softplus_end(b)
                    routing(b)
                    weigh_x(b, p)
                    inject(b, p, 0)
                    for k in range(GROUPS):
                        if k + 1 < GROUPS:
                            inject(b, p, k + 1)
                        scan(b, k)
                        if k == 19:
                            skip(b, p, 0)
                    skip(b, p, 1)
                    for m in range(UNITS):
                        hidden(b, m)
                    dve.wait_ge(back_full.sem, back_full.at(b))
                    nc.vector.tensor_tensor(xr[:, p], p_misc[:].rearrange("p (t d) -> p t d", t=TT), xr[:, p], ALU.add)\
                        .then_inc(res_done.sem, 1)

        @block.tensor
        def _(pe):
            start(pe, [prep_full, dt_full, du_full, gathered, g_full, u_full, hid_used, acc_full, back_full])
            pe.wait_ge(w_loaded, 16 * n_loads)
            pe.wait_ge(begun, 6)

            def free(b, n):
                pe.wait_ge(prep_free.sem, prep_free.at(b, n))

            def turn_x(b, i):
                pe.wait_ge(ln_done.sem, ln_done.at(b, i + 1))
                for t in range(TT):
                    ins = nc.tensor.transpose(p_misc[:, bass.ts(t, 128)], xn[:, i, t], ident[:])
                ins.then_inc(prep_full.sem, 1)

            def in_proj(b):
                for n in range(4):
                    free(b, HT + n)
                    nc.tensor.matmul(p_misc[:], w["win"][:, bass.ts(n, 128)], ht[:], start=True, stop=True)\
                        .then_inc(prep_full.sem, 1)

            def x_proj(b, p):
                pe.wait_ge(u_done.sem, u_done.at(b))
                for n, (wt_, rows) in enumerate(((w["wx_dt"], RDT), (w["wx_b"], 128), (w["wx_c"], 128))):
                    free(b, Z1 + n)
                    for s in range(ST):
                        ins = nc.tensor.matmul(p_misc[0:rows], wt_[:, s], u[:, p, s], start=(s == 0), stop=(s == ST - 1))
                    ins.then_inc(prep_full.sem, 1)
                for s in range(ST):
                    free(b, CREP + s)
                    nc.tensor.matmul(p_misc[:], w["wdt"][:, bass.ts(s, 128)], dtr[:], start=True, stop=True)\
                        .then_inc(prep_full.sem, 1)

            def gate_logits(b, p):
                free(b, DT1)
                for t in range(TT):
                    ins = nc.tensor.matmul(p_misc[:, bass.ts(t, E)], xt[:, p, bass.ts(t, 128)], w["wgate"][:], start=True, stop=True)
                ins.then_inc(prep_full.sem, 1)

            def spread_weights(b):
                free(b, GATE)
                pe.wait_ge(route.sem, route.at(b))
                turned = p_misc[:].bitcast(BF16)
                for t in range(TT):
                    ins = nc.tensor.transpose(turned[0:3 * E, bass.ts(t, 128)], wpart[:, t].rearrange("p i e -> p (i e)"), ident_b[:])
                ins.then_inc(prep_full.sem, 1)
                for e in range(E):
                    free(b, WT + e)
                    nc.tensor.matmul(p_misc[:], pick[:, e], wt[:], start=True, stop=True).then_inc(prep_full.sem, 1)

            def spread_dt(b, p, k):
                s, j, i = order[k]
                if k % 16 == 0:
                    pe.wait_ge(stacked[s].sem, stacked[s].at(b))
                pe.wait_ge(da_done.sem, da_done.at(b, k - 1) if k >= 2 else da_done.at(b - 1, GROUPS - 1 + k))
                nc.tensor.matmul(p_dt[:, k % 2], spread[:, i], block_in[:, 0, s, j], start=True, stop=True)\
                    .then_inc(dt_full.sem, 1)

            def spread_du(b, p, k):
                s, j, i = order[k]
                pe.wait_ge(dbu_done.sem, dbu_done.at(b, k) if k else dbu_done.at(b - 1))
                nc.tensor.matmul(p_du[:], spread[:, i], block_in[:, 1, s, j], start=True, stop=True)\
                    .then_inc(du_full.sem, 1)

            def gather_y(b, q):
                pe.wait_ge(hc_done.sem, hc_done.at(b, 4 * q + 4))
                if q % 4 == 0:
                    pe.wait_ge(y1_done.sem, y1_done.at(b, q // 4) if q else y1_done.at(b - 1))
                for k in range(4 * q, 4 * q + 4):
                    s, j, i = order[k]
                    ins = nc.tensor.matmul(p_y[32 * j:32 * j + 32], w["gather"][:, i], hc[:, k % NA], start=(i == 0), stop=(i == 3))
                ins.then_inc(gathered.sem, 1)

            def gate_up(b, p, m):
                e, f = divmod(m, FT1)
                pe.wait_ge(g_read.sem, g_read.at(b, m) if m else g_read.at(b - 1))
                nc.tensor.matmul(p_g[:], w1[:, e, bass.ts(f, 128)], xt[:, p], start=True, stop=True).then_inc(g_full.sem, 1)
                pe.wait_ge(hid_done.sem, hid_done.at(b, m) if m else hid_done.at(b - 1))
                nc.tensor.matmul(p_u[:], w3[:, e, bass.ts(f, 128)], xw[:, e], start=True, stop=True).then_inc(u_full.sem, 1)

            def down(b, m):
                e, f = divmod(m, FT1)
                if m == 0:
                    pe.wait_ge(acc_read.sem, acc_read.at(b - 1))
                pe.wait_ge(hid_done.sem, hid_done.at(b, m + 1))
                nc.tensor.matmul(p_acc[:], w2[:, e, f], hid[:, m % 2], start=(m == 0), stop=False).then_inc(hid_used.sem, 1)

            def out_proj(b):
                pe.wait_ge(y_done.sem, y_done.at(b))
                for s in range(ST):
                    ins = nc.tensor.matmul(p_acc[:], w["wo1"][:, s], yt[:, s], start=False, stop=(s == ST - 1))
                ins.then_inc(acc_full.sem, 1)

            def turn_back(b):
                pe.wait_ge(acc_read.sem, acc_read.at(b))
                for t in range(TT):
                    ins = nc.tensor.transpose(p_misc[:, bass.ts(t, 128)], ot[:, bass.ts(t, 128)], ident[:])
                ins.then_inc(back_full.sem, 1)

            with pe.Fori(0, B // 2) as pair:
                for p in range(2):
                    b = pair * 2 + (1 + p)
                    pe.wait_ge(res_done.sem, res_done.at(b - 1))
                    turn_x(b, 0)
                    free(b, XT)
                    pe.wait_ge(x_third.sem, x_third.at(b))
                    turn_x(b, 1)
                    in_proj(b)
                    x_proj(b, p)
                    gate_logits(b, p)
                    spread_weights(b)
                    spread_dt(b, p, 0)
                    spread_dt(b, p, 1)
                    spread_du(b, p, 0)
                    for k in range(GROUPS):
                        if k + 2 < GROUPS:
                            spread_dt(b, p, k + 2)
                        if k + 1 < GROUPS:
                            spread_du(b, p, k + 1)
                        if k % 4 == 3 and k > 4:
                            gather_y(b, k // 4 - 1)
                    gather_y(b, GROUPS // 4 - 1)
                    pe.wait_ge(experts_in, 48)
                    gate_up(b, p, 0)
                    for m in range(UNITS):
                        if m + 1 < UNITS:
                            gate_up(b, p, m + 1)
                        down(b, m)
                    out_proj(b)
                    turn_back(b)


def laid_out(i):
    a = {k: np.asarray(v) for k, v in i.items()}
    c = np.ascontiguousarray
    column = np.arange(H * DH)
    head, dim = column // DH, column % DH
    swapped = (dim + DH // 2) % DH
    q_cols = [column, head * DH + swapped]
    up_cols = [head * 2 * DH + dim, head * 2 * DH + swapped, head * 2 * DH + DH + dim]
    wup = np.concatenate([a["L0_attn_Wup"], a["L0_attn_bup"][None]], 0)
    per_tile = lambda v: v.reshape(ST, 128, -1).transpose(1, 0, 2).reshape(128, -1)
    xp = a["L1_attn_x_proj_w"].reshape(ST, 128, RDT + 2 * N).transpose(1, 0, 2)
    stacked = lambda routed, shared: np.concatenate([routed, shared[None]], 0)
    return {
        "x": c(a["L0_attn_x"]),
        "wq": c(np.stack([a["L0_attn_Wq"][:, q] for q in q_cols], 1)),
        "wdown": c(a["L0_attn_Wdown"]),
        "wup": c(np.stack([wup[:, k] for k in up_cols], 1)),
        "wout": c(a["L0_attn_Wout"]),
        "bq": c(np.tile(np.stack([a["L0_attn_bq"][q] for q in q_cols])[None], (128, 1, 1))),
        "bdown": c(a["L0_attn_bdown"][:, None]),
        "bout": c(np.tile(a["L0_attn_bout"][None], (128, 1))),
        "wg": c(a["L0_ffn_w_gate"].T),
        "wu": c(a["L0_ffn_w_up"].T),
        "wd": c(a["L0_ffn_w_down"].T.reshape(FT0, 128, D).transpose(1, 0, 2)),
        "w1": c(stacked(a["L1_ffn_We1"], a["L1_ffn_Ws1"]).transpose(1, 0, 2)),
        "w3": c(stacked(a["L1_ffn_We3"], a["L1_ffn_Ws3"]).transpose(1, 0, 2)),
        "w2": c(stacked(a["L1_ffn_We2"], a["L1_ffn_Ws2"]).reshape(E + 1, FT1, 128, D).transpose(2, 0, 1, 3)),
        "win": c(a["L1_attn_in_proj_w"]),
        "wx_dt": c(xp[:, :, :RDT]),
        "wx_b": c(np.tile(xp[:, :, RDT:RDT + N], (1, 1, 128 // N))),
        "wx_c": c(np.tile(xp[:, :, RDT + N:], (1, 1, 128 // N))),
        "wdt": c(a["L1_attn_dt_proj_w"]),
        "wo1": c(a["L1_attn_out_proj_w"].reshape(ST, 128, D).transpose(1, 0, 2)),
        "wgate": c(a["L1_ffn_Wg"]),
        "vecs": c(np.concatenate([a["L1_attn_norm_w"][:, None], per_tile(a["L1_attn_conv_w"]), per_tile(a["L1_attn_conv_b"]),
                                  per_tile(a["L1_attn_dt_proj_b"]), per_tile(a["L1_attn_D"])], 1)),
        "a_log": c(a["L1_attn_A_log"].reshape(GROUPS, 128 // N, N).transpose(1, 2, 0).reshape(128, GROUPS)),
    }


def kernel(**inputs):
    import concourse.bacc as bacc
    from concourse.bass_utils import run_bass_kernel_spmd

    arrays = {**laid_out(inputs), **constants()}
    nc = bacc.Bacc("TRN2", target_bir_lowering=False, num_devices=1)
    io = {n: nc.dram_tensor("in_" + n, v.shape, mybir.dt.from_np(v.dtype), kind="ExternalInput").ap() for n, v in arrays.items()}
    out = nc.dram_tensor("out", (B, T, D), F32, kind="ExternalOutput").ap()
    program(nc, io, out)
    return run_bass_kernel_spmd(nc, [{"in_" + n: v for n, v in arrays.items()}], core_ids=[0]).results[0]["out"]
```

```python
from contextlib import ExitStack

import numpy as np

import concourse.bass as bass
from concourse import mybir

F32 = mybir.dt.float32
BF16 = mybir.dt.bfloat16
I32 = mybir.dt.int32
ALU = mybir.AluOpType
ACT = mybir.ActivationFunctionType
AX = mybir.AxisListType

B, T, D = 8, 512, 128
TT = T // 128
HALF = TT // 2
H, DH = 16, 8
LAT = 32
FF0 = 384
FT0 = FF0 // 128
DI, N = 256, 16
ST = DI // 128
GROUPS = DI * N // 128
CONV = 4
RDT = 64
E = 8
FF1 = 256
FT1 = FF1 // 128
UNITS = (E + 1) * FT1
EPS = 1e-5


class Count:

    def __init__(self, sem, per, by=1):
        self.sem, self.per, self.by = sem, per, by
        self.start = 2 * per * by

    def at(self, b, n=None):
        n = self.per if n is None else n
        return (b + 1) * (self.per * self.by) + n * self.by


def constants():
    inv = (1.0 / np.float32(10000.0) ** (np.arange(0, DH, 2, dtype=np.float32) / np.float32(DH))).astype(np.float32)
    angle = (np.arange(T, dtype=np.float32)[None, :] * inv[:, None]).astype(np.float32).astype(np.float64)
    dim = np.arange(128) % DH
    cos = np.cos(angle)[dim % (DH // 2)]
    sin = np.sin(angle)[dim % (DH // 2)] * np.where(dim < DH // 2, -1.0, 1.0)[:, None]
    scale = 1.0 / np.sqrt(DH)
    rope = np.stack([cos * scale, sin * scale, cos, sin]).astype(np.float32)
    rope = np.ascontiguousarray(rope.reshape(4, 128, TT, 128).transpose(3, 0, 2, 1))
    ident = np.eye(128, dtype=np.float32)
    spread = np.zeros((3, 32, 4, 128), np.float32)
    for i in range(4):
        for p in range(128):
            spread[:, i * 8 + p // N, i, p] = 1
    gather = np.zeros((128, 4, 32), np.float32)
    for i in range(4):
        for p in range(128):
            gather[p, i, i * 8 + p // N] = 1
    pick = np.tile(np.eye(E, dtype=np.float32)[None, :, :, None], (3, 1, 1, 128))
    before = np.tile((np.arange(E)[None, :] < np.arange(E)[:, None]).astype(np.float32)[None], (128, 1, 1))
    return {
        "c_rope": rope,
        "c_ident": ident,
        "c_spread": spread.reshape(96, 4, 128),
        "c_gather": gather,
        "c_pick": pick.reshape(3 * E, E, 128),
        "c_before": before,
    }


def program(nc, io, out):
    dram = nc.dram_tensor("layer0_out", (B, T, D), F32, kind="Internal").ap()
    with ExitStack() as ctx:
        def sem(name):
            return ctx.enter_context(nc.semaphore(name))

        def sb(name, shape, dt=F32):
            return ctx.enter_context(nc.sbuf_tensor(name, shape, dt))

        ident = sb("ident", [128, 128])
        win = sb("win", [128, 2 * DI])
        wx_dt = sb("wx_dt", [128, ST, RDT])
        wx_b = sb("wx_b", [128, ST, 128])
        wx_c = sb("wx_c", [128, ST, 128])
        wdt = sb("wdt", [RDT, DI])
        wo1 = sb("wo1", [128, ST, D])
        wgate = sb("wgate", [128, E])
        vecs = sb("vecs", [128, 1 + ST * (CONV + 3)])
        a_log = sb("a_log", [128, GROUPS])
        gather = sb("gather", [128, 4, 32])
        before = sb("before", [128, E, E])
        w1 = sb("w1", [128, E + 1, FF1])
        w3 = sb("w3", [128, E + 1, FF1])
        w2 = sb("w2", [128, E + 1, FT1, D])
        norm_w = vecs[:, 0:1]
        conv_w = vecs[:, 1:1 + ST * CONV].rearrange("p (s k) -> p s k", s=ST)
        conv_b = vecs[:, 1 + ST * CONV:1 + ST * (CONV + 1)]
        dt_b = vecs[:, 1 + ST * (CONV + 1):1 + ST * (CONV + 2)]
        d_skip = vecs[:, 1 + ST * (CONV + 2):1 + ST * (CONV + 3)]
        w_loaded = sem("w_loaded")
        layer1_loads = [
            (win, "win"), (wx_dt, "wx_dt"), (wx_b, "wx_b"), (wx_c, "wx_c"),
            (wdt, "wdt"), (wo1, "wo1"), (wgate, "wgate"), (vecs, "vecs"), (a_log, "a_log"), (gather, "c_gather"),
            (before, "c_before"), (w1, "w1"), (w3, "w3"), (w2, "w2"),
        ]
        minus_half = sb("minus_half", [128, TT])
        own_wait = sem("own_wait")
        stored0 = sem("stored0")

        def hold(eng):
            eng.sem_inc(own_wait, 1)

        layer0(nc, ctx, io, dram, ident, minus_half, w_loaded, layer1_loads, stored0, hold)
        layer1(nc, ctx, io, dram, out, ident, minus_half, w_loaded, len(layer1_loads), stored0, hold,
               dict(win=win, wx_dt=wx_dt, wx_b=wx_b, wx_c=wx_c, wdt=wdt, wo1=wo1, wgate=wgate,
                    norm_w=norm_w, conv_w=conv_w, conv_b=conv_b, dt_b=dt_b, d_skip=d_skip, a_log=a_log,
                    gather=gather, before=before, w1=w1, w3=w3, w2=w2))


def layer0(nc, outer, io, dram, ident, minus_half, w_loaded, layer1_loads, stored0, hold):
    with ExitStack() as ctx:
        def sb(name, shape, dt=F32):
            return ctx.enter_context(nc.sbuf_tensor(name, shape, dt))

        def ps(name, shape, dt=F32):
            return ctx.enter_context(nc.psum_tensor(name, shape, dt))

        def count(name, per, by=1):
            return Count(outer.enter_context(nc.semaphore(name)), per, by)

        wq = sb("wq", [128, 2, 128])
        wdown = sb("wdown", [128, LAT])
        wup = sb("wup", [LAT + 1, 3, 128])
        wout = sb("wout", [128, D])
        bq = sb("bq", [1, 2, 128])
        bdown = sb("bdown", [LAT, 1])
        bout = sb("bout", [1, D])
        one_row = sb("one_row", [1, 128])
        rope = sb("rope", [128, 4, TT, 128])
        wg_i = sb("wg_i", [128, FF0], I32)
        wu_i = sb("wu_i", [128, FF0], I32)
        wd_i = sb("wd_i", [128, FT0, D], I32)
        wg = sb("wg", [128, FF0])
        wu = sb("wu", [128, FF0])
        wd = sb("wd", [128, FT0, D])
        x = sb("x", [128, 2, TT, D])
        stats = sb("stats", [128, TT, 6])
        mv = sb("mv", [128, TT, 2])
        ve = sb("ve", [128, TT])
        rstd = sb("rstd", [128, TT])
        xn = sb("xn", [128, TT, D])
        xt = sb("xt", [128, T])
        lat = sb("lat", [LAT + 1, T])
        turn = sb("turn", [128, 4, TT, 128])
        rq = sb("rq", [128, 2, TT, H, DH])
        rk = sb("rk", [128, 2, TT, H, DH])
        v = sb("v", [128, 2, TT, DH, H])
        score_prod = sb("score_prod", [128, HALF, H * H * DH])
        value_prod = sb("value_prod", [128, HALF, H * H * DH])
        sc = sb("sc", [128, TT, H, H])
        negmax = sb("negmax", [128, TT, H])
        den = sb("den", [128, TT, H])
        rden = sb("rden", [128, TT, H])
        raw = sb("raw", [128, TT, H, DH])
        attn = sb("attn", [128, TT, D])
        attn_t = sb("attn_t", [128, T])
        hid = sb("hid", [128, FT0, T])
        x1 = sb("x1", [128, 2, TT, D])

        p_xt = ps("p_xt", [128, T])
        p_q = ps("p_q", [128, T])
        p_qs = ps("p_qs", [128, T])
        p_lat = ps("p_lat", [128, T])
        p_gate = ps("p_gate", [128, T])
        p_up = ps("p_up", [128, T])
        p_down = ps("p_down", [128, T])
        p_back = ps("p_back", [128, T])

        loaded0 = outer.enter_context(nc.semaphore("loaded0"))
        setup = outer.enter_context(nc.semaphore("setup"))
        small_loads = [(ident, "c_ident"), (wq, "wq"), (wdown, "wdown"), (wup, "wup"), (wout, "wout"),
                       (bq, "bq"), (bdown, "bdown"), (bout, "bout"), (rope, "c_rope"),
                       (wg_i, "wg"), (wu_i, "wu"), (wd_i, "wd")]

        x_in = count("x_in", 1, 16)
        ln_stats = count("ln_stats", 2)
        ln_var = count("ln_var", 1)
        ln_rstd = count("ln_rstd", 1)
        ln_done = count("ln_done", 1)
        xt_full = count("xt_full", 1)
        xt_copied = count("xt_copied", 1)
        q_full = count("q_full", 4)
        turned = count("turned", 4)
        rope_sum = count("rope_sum", 2)
        lat_full = count("lat_full", 2)
        lat_copied = count("lat_copied", 2)
        gate_full = count("gate_full0", FT0)
        gated = count("gated0", FT0)
        up_full = count("up_full0", FT0)
        hidden_done = count("hidden_done0", FT0)
        down_full = count("down_full", 1)
        xf_done = count("xf_done", 1)
        products = count("products", 2)
        products_pool = count("products_pool", 2)
        scored = count("scored", TT)
        soft = count("soft", 4)
        exp_done = count("exp_done", 2)
        den_step = count("den_step", 4)
        weighed = count("weighed", TT)
        summed = count("summed", TT)
        attn_done = count("attn_done", 2)
        back_full = count("back_full0", 2)
        attn_copied = count("attn_copied", 1)
        x1_done = count("x1_done", 1)
        stored = count("stored", 1, 16)

        x_d = io["x"].rearrange("b (t p) d -> b p t d", p=128)
        x1_d = dram.rearrange("b (t p) d -> b p t d", p=128)
        block = ctx.enter_context(nc.Block())

        def start(eng, mine):
            for c in mine:
                eng.sem_inc(c.sem, c.start)

        def schedule(batch, tail, prologue, eng):
            prologue()
            batch(1, 0, first=True, last=False)
            with eng.Fori(0, B // 2 - 1) as pair:
                for i in range(2):
                    batch(pair * 2 + (2 + i), (1 + i) % 2, first=False, last=False)
            batch(B, (B - 1) % 2, first=False, last=True)
            tail(B, (B - 1) % 2)

        def tiles(j):
            return slice(HALF * j, HALF * j + HALF)

        def score_products(eng, p, j, i):
            t = HALF * j + i
            return eng.tensor_tensor(score_prod[:, i].rearrange("p (h g d) -> p h g d", h=H, g=H),
                                     rq[:, p, t].unsqueeze(2).to_broadcast([128, H, H, DH]),
                                     rk[:, p, t].unsqueeze(1).to_broadcast([128, H, H, DH]), ALU.mult)

        def value_products(eng, p, j, i):
            t = HALF * j + i
            return eng.tensor_tensor(value_prod[:, i].rearrange("p (h d g) -> p h d g", h=H, g=H),
                                     sc[:, t].unsqueeze(2).to_broadcast([128, H, DH, H]),
                                     v[:, p, t].unsqueeze(1).to_broadcast([128, H, DH, H]), ALU.mult)

        @block.sync
        def _(sp):
            start(sp, [x_in, stored])
            sp.dma_start(x[:, 0], x_d[0]).then_inc(x_in.sem, 16)
            for tile, name in small_loads:
                sp.dma_start(tile[:], io[name]).then_inc(loaded0, 16)

            def load(index, b, p):
                sp.wait_ge(xf_done.sem, xf_done.at(b - 2))
                hold(sp)
                sp.wait_ge(ln_done.sem, ln_done.at(b - 1))
                hold(sp)
                sp.dma_start(x[:, p], x_d[bass.ds(index, 1)].rearrange("o p t d -> p (o t) d")).then_inc(x_in.sem, 16)

            def store(b, p):
                sp.wait_ge(x1_done.sem, x1_done.at(b))
                hold(sp)
                sp.dma_start(x1_d[bass.ds(b - 1, 1)].rearrange("o p t d -> p (o t) d"), x1[:, p]).then_inc(stored.sem, 16)

            def prologue():
                load(1, 2, 1)
                for tile, name in layer1_loads:
                    sp.dma_start(tile[:], io[name]).then_inc(w_loaded, 16)

            def batch(b, p, first, last):
                if not last:
                    load((b + 1) % B, b + 2, p)
                if not first:
                    store(b - 1, 1 - p)

            schedule(batch, store, prologue, sp)
            sp.wait_ge(stored.sem, stored.at(B))
            sp.wait_ge(x_in.sem, x_in.at(B + 1))
            sp.sem_inc(stored0, 1)

        @block.gpsimd
        def _(pool):
            start(pool, [ln_rstd, rope_sum, products_pool, weighed])
            nc.gpsimd.memset(minus_half[:], -0.5).then_inc(setup, 1)
            pool.wait_ge(setup, 1)
            nc.gpsimd.memset(lat[LAT:LAT + 1, :], 1.0).then_inc(setup, 1)
            pool.wait_ge(setup, 2)
            nc.gpsimd.memset(one_row[:], 1.0).then_inc(setup, 1)
            pool.wait_ge(setup, 3)

            def root(b):
                pool.wait_ge(ln_var.sem, ln_var.at(b))
                nc.gpsimd.tensor_tensor(rstd[:], ve[:], minus_half[:], ALU.pow).then_inc(ln_rstd.sem, 1)

            def add_turns(b, p, n):
                pool.wait_ge(turned.sem, turned.at(b, 2 * n + 2))
                pool.wait_ge(products.sem, products.at(b - 2))
                pool.wait_ge(products_pool.sem, products_pool.at(b - 2))
                nc.gpsimd.tensor_tensor((rk if n else rq)[:, p].rearrange("p t h d -> p t (h d)"), turn[:, 2 * n], turn[:, 2 * n + 1],
                                        ALU.add).then_inc(rope_sum.sem, 1)

            def scores(b, p, j):
                pool.wait_ge(rope_sum.sem, rope_sum.at(b))
                pool.wait_ge(scored.sem, scored.at(b, 2) if j else scored.at(b - 1))
                score_products(nc.gpsimd, p, j, 1).then_inc(products_pool.sem, 1)

            def weigh(b, p, j, i):
                pool.wait_ge(exp_done.sem, exp_done.at(b, j + 1))
                pool.wait_ge(lat_copied.sem, lat_copied.at(b))
                pool.wait_ge(summed.sem, summed.at(b, i + 1) if j else summed.at(b - 1, HALF + i + 1))
                value_products(nc.gpsimd, p, j, i).then_inc(weighed.sem, 1)

            def prologue():
                root(1)
                for n in range(2):
                    add_turns(1, 0, n)
                scores(1, 0, 0)
                root(2)

            def batch(b, p, first, last):
                q = 1 - p
                scores(b, p, 1)
                weigh(b, p, 0, 0)
                weigh(b, p, 0, 1)
                if not last:
                    add_turns(b + 1, q, 0)
                    add_turns(b + 1, q, 1)
                    scores(b + 1, q, 0)
                    root(b + 2)
                weigh(b, p, 1, 0)
                weigh(b, p, 1, 1)

            schedule(batch, lambda b, p: None, prologue, pool)

        @block.scalar
        def _(act):
            start(act, [xt_copied, lat_copied, gated, exp_done, attn_copied])
            act.wait_ge(loaded0, 16 * len(small_loads))
            act.wait_ge(setup, 3)

            def copy_xt(b):
                act.wait_ge(xt_full.sem, xt_full.at(b))
                act.wait_ge(up_full.sem, up_full.at(b - 1))
                nc.scalar.activation(xt[:], p_xt[:], ACT.Copy).then_inc(xt_copied.sem, 1)

            def copy_latent(b):
                act.wait_ge(lat_full.sem, lat_full.at(b, 1))
                nc.scalar.activation(lat[0:LAT], p_lat[0:LAT, :], ACT.Identity, bias=bdown[:, 0:1]).then_inc(lat_copied.sem, 1)

            def copy_v(b, p):
                act.wait_ge(lat_full.sem, lat_full.at(b, 2))
                act.wait_ge(weighed.sem, weighed.at(b - 2))
                nc.scalar.activation(v[:, p].rearrange("p t d g -> p (t d g)"), p_lat[:], ACT.Copy).then_inc(lat_copied.sem, 1)

            def gates(b):
                for f in range(FT0):
                    act.wait_ge(gate_full.sem, gate_full.at(b, f + 1))
                    if f == 0:
                        act.wait_ge(down_full.sem, down_full.at(b - 1))
                    nc.scalar.activation(hid[:, f], p_gate[:], ACT.Silu, scale=1.0 / 127.0).then_inc(gated.sem, 1)

            def soften(b, j):
                act.wait_ge(soft.sem, soft.at(b, 2 * j + 2))
                nc.scalar.activation(sc[:, tiles(j)], sc[:, tiles(j)], ACT.Exp).then_inc(exp_done.sem, 1)

            def copy_attention(b):
                act.wait_ge(back_full.sem, back_full.at(b, 1))
                nc.scalar.activation(attn_t[:], p_back[:], ACT.Copy).then_inc(attn_copied.sem, 1)

            def prologue():
                copy_xt(1)
                copy_latent(1)
                copy_v(1, 0)
                gates(1)
                soften(1, 0)

            def batch(b, p, first, last):
                q = 1 - p
                if not last:
                    copy_xt(b + 1)
                    copy_latent(b + 1)
                if not first:
                    copy_attention(b - 1)
                if not last:
                    copy_v(b + 1, q)
                soften(b, 1)
                if not last:
                    gates(b + 1)
                    soften(b + 1, 0)

            schedule(batch, lambda b, p: copy_attention(b), prologue, act)

        @block.vector
        def _(dve):
            start(dve, [ln_stats, ln_var, ln_done, turned, hidden_done, xf_done, products, scored, soft, den_step, summed,
                        attn_done, x1_done])

            def statistics(b, p):
                dve.wait_ge(x_in.sem, x_in.at(b))
                for t in range(TT):
                    ins = nc.vector.bn_stats(stats[:, t], x[:, p, t])
                ins.then_inc(ln_stats.sem, 1)
                dve.wait_ge(ln_stats.sem, ln_stats.at(b, 1))
                hold(dve)
                for t in range(TT):
                    ins = nc.vector.bn_aggr(mv[:, t], stats[:, t])
                ins.then_inc(ln_stats.sem, 1)
                dve.wait_ge(ln_stats.sem, ln_stats.at(b, 2))
                nc.vector.tensor_scalar(ve[:], mv[:, :, 1], EPS, None, ALU.add).then_inc(ln_var.sem, 1)

            def normalize(b, p):
                dve.wait_ge(ln_rstd.sem, ln_rstd.at(b))
                dve.wait_ge(xt_full.sem, xt_full.at(b - 1))
                for t in range(TT):
                    ins = nc.vector.tensor_scalar(xn[:, t], x[:, p, t], mv[:, t, 0:1], rstd[:, t:t + 1], ALU.subtract, ALU.mult)
                ins.then_inc(ln_done.sem, 1)

            def turns(b, n):
                for i, source in enumerate((p_q, p_qs)):
                    s = 2 * n + i
                    dve.wait_ge(q_full.sem, q_full.at(b, s + 1))
                    if i == 0:
                        dve.wait_ge(rope_sum.sem, rope_sum.at(b - 1, n + 1))
                    nc.vector.tensor_tensor(turn[:, s], source[:].rearrange("p (t c) -> p t c", t=TT), rope[:, s], ALU.mult)\
                        .then_inc(turned.sem, 1)

            def scores(b, p, j):
                dve.wait_ge(rope_sum.sem, rope_sum.at(b))
                dve.wait_ge(scored.sem, scored.at(b, 1) if j else scored.at(b - 1, HALF + 1))
                score_products(nc.vector, p, j, 0).then_inc(products.sem, 1)

            def sum_scores(b, j, i):
                if i == 0:
                    dve.wait_ge(products.sem, products.at(b, j + 1))
                    dve.wait_ge(weighed.sem, weighed.at(b - 1, HALF * (j + 1)))
                else:
                    dve.wait_ge(products_pool.sem, products_pool.at(b, j + 1))
                nc.vector.tensor_reduce(sc[:, HALF * j + i], score_prod[:, i].rearrange("p (h g d) -> p h g d", h=H, g=H),
                                        AX.X, ALU.add).then_inc(scored.sem, 1)

            def less_maximum(b, j):
                dve.wait_ge(scored.sem, scored.at(b, HALF * (j + 1)))
                nc.vector.tensor_reduce(negmax[:, tiles(j)], sc[:, tiles(j)], AX.X, ALU.max, negate=True).then_inc(soft.sem, 1)
                dve.wait_ge(soft.sem, soft.at(b, 2 * j + 1))
                nc.vector.tensor_tensor(sc[:, tiles(j)], sc[:, tiles(j)],
                                        negmax[:, tiles(j)].unsqueeze(3).to_broadcast([128, HALF, H, H]), ALU.add)\
                    .then_inc(soft.sem, 1)

            def denominators(b, j):
                dve.wait_ge(exp_done.sem, exp_done.at(b, j + 1))
                nc.vector.tensor_reduce(den[:, tiles(j)], sc[:, tiles(j)], AX.X, ALU.add).then_inc(den_step.sem, 1)

            def sum_values(b, j, i):
                t = HALF * j + i
                dve.wait_ge(weighed.sem, weighed.at(b, t + 1))
                nc.vector.tensor_reduce(raw[:, t], value_prod[:, i].rearrange("p (h d g) -> p h d g", h=H, g=H), AX.X, ALU.add)\
                    .then_inc(summed.sem, 1)

            def divide(b, j):
                dve.wait_ge(den_step.sem, den_step.at(b, 2 * j + 1))
                hold(dve)
                nc.vector.reciprocal(rden[:, tiles(j)], den[:, tiles(j)]).then_inc(den_step.sem, 1)
                dve.wait_ge(den_step.sem, den_step.at(b, 2 * j + 2))
                dve.wait_ge(summed.sem, summed.at(b, HALF * (j + 1)))
                dve.wait_ge(back_full.sem, back_full.at(b - 1, 1))
                nc.vector.tensor_tensor(attn[:, tiles(j)].rearrange("p t (h d) -> p t h d", h=H), raw[:, tiles(j)],
                                        rden[:, tiles(j)].unsqueeze(3).to_broadcast([128, HALF, H, DH]), ALU.mult)\
                    .then_inc(attn_done.sem, 1)

            def hidden(b, f):
                dve.wait_ge(up_full.sem, up_full.at(b, f + 1))
                dve.wait_ge(gated.sem, gated.at(b, f + 1))
                nc.vector.scalar_tensor_tensor(hid[:, f], p_up[:], 1.0 / 127.0 ** 2, hid[:, f],
                                               ALU.mult, ALU.mult).then_inc(hidden_done.sem, 1)

            def add_ffn(b, p):
                dve.wait_ge(down_full.sem, down_full.at(b))
                dve.wait_ge(stored.sem, stored.at(b - 2))
                nc.vector.tensor_tensor(x1[:, p], p_down[:].rearrange("p (t d) -> p t d", t=TT), x[:, p], ALU.add)\
                    .then_inc(xf_done.sem, 1)

            def add_attention(b, p):
                dve.wait_ge(back_full.sem, back_full.at(b, 2))
                nc.vector.tensor_tensor(x1[:, p], p_back[:].rearrange("p (t d) -> p t d", t=TT), x1[:, p], ALU.add)\
                    .then_inc(x1_done.sem, 1)

            def prologue():
                dve.wait_ge(setup, 3)
                statistics(1, 0)
                normalize(1, 0)
                dve.wait_ge(loaded0, 16 * len(small_loads))
                nc.vector.tensor_copy(wg[:], wg_i[:]).then_inc(setup, 1)
                nc.vector.tensor_copy(wu[:], wu_i[:]).then_inc(setup, 1)
                nc.vector.tensor_copy(wd[:], wd_i[:]).then_inc(setup, 1)
                dve.wait_ge(setup, 6)
                for n in range(2):
                    turns(1, n)
                scores(1, 0, 0)
                hidden(1, 0)
                sum_scores(1, 0, 0)
                hidden(1, 1)
                sum_scores(1, 0, 1)
                less_maximum(1, 0)
                hidden(1, 2)
                statistics(2, 1)
                normalize(2, 1)
                add_ffn(1, 0)

            def tail(b, p):
                sum_values(b, 1, 1)
                divide(b, 1)
                add_attention(b, p)

            def batch(b, p, first, last):
                q = 1 - p
                if not first:
                    sum_values(b - 1, 1, 1)
                    divide(b - 1, 1)
                scores(b, p, 1)
                if not last:
                    turns(b + 1, 0)
                sum_scores(b, 1, 0)
                if not last:
                    turns(b + 1, 1)
                sum_scores(b, 1, 1)
                less_maximum(b, 1)
                denominators(b, 0)
                if not first:
                    add_attention(b - 1, q)
                if not last:
                    statistics(b + 2, p)
                sum_values(b, 0, 0)
                sum_values(b, 0, 1)
                divide(b, 0)
                if not last:
                    scores(b + 1, q, 0)
                    hidden(b + 1, 0)
                    sum_scores(b + 1, 0, 0)
                    hidden(b + 1, 1)
                    sum_scores(b + 1, 0, 1)
                    hidden(b + 1, 2)
                    less_maximum(b + 1, 0)
                    normalize(b + 2, p)
                denominators(b, 1)
                sum_values(b, 1, 0)
                if not last:
                    add_ffn(b + 1, q)

            schedule(batch, tail, prologue, dve)

        @block.tensor
        def _(pe):
            start(pe, [xt_full, q_full, lat_full, gate_full, up_full, down_full, back_full])
            pe.wait_ge(loaded0, 16 * len(small_loads))
            pe.wait_ge(setup, 6)

            def by_tile(to, lhs, rhs, bias=None):
                for t in range(TT):
                    ins = nc.tensor.matmul(to[:, bass.ts(t, 128)], lhs[:, bass.ts(t, 128)], rhs, start=True, stop=bias is None)
                    if bias is not None:
                        ins = nc.tensor.matmul(to[:, bass.ts(t, 128)], one_row[:], bias, start=False, stop=True)
                return ins

            def turned_tiles(to, src):
                for t in range(TT):
                    ins = nc.tensor.transpose(to[:, bass.ts(t, 128)], src[:, t], ident[:])
                return ins

            def project_in(b):
                pe.wait_ge(ln_done.sem, ln_done.at(b))
                turned_tiles(p_xt, xn).then_inc(xt_full.sem, 1)
                pe.wait_ge(xt_copied.sem, xt_copied.at(b))
                pe.wait_ge(lat_copied.sem, lat_copied.at(b - 1))
                nc.tensor.matmul(p_lat[0:LAT], wdown[:], xt[:], start=True, stop=True).then_inc(lat_full.sem, 1)
                pe.wait_ge(turned.sem, turned.at(b - 1, 3))
                by_tile(p_q, xt, wq[:, 0], bq[:, 0]).then_inc(q_full.sem, 1)
                pe.wait_ge(turned.sem, turned.at(b - 1, 4))
                by_tile(p_qs, xt, wq[:, 1], bq[:, 1]).then_inc(q_full.sem, 1)

            def project_up(b):
                pe.wait_ge(lat_copied.sem, lat_copied.at(b, 1))
                by_tile(p_lat, lat, wup[:, 2]).then_inc(lat_full.sem, 1)
                for n, to in enumerate((p_q, p_qs)):
                    pe.wait_ge(turned.sem, turned.at(b, n + 1))
                    by_tile(to, lat, wup[:, n]).then_inc(q_full.sem, 1)

            def ffn(b):
                for f in range(FT0):
                    pe.wait_ge(gated.sem, gated.at(b, f) if f else gated.at(b - 1))
                    nc.tensor.matmul(p_gate[:], wg[:, bass.ts(f, 128)], xt[:], start=True, stop=True).then_inc(gate_full.sem, 1)
                    pe.wait_ge(hidden_done.sem, hidden_done.at(b, f) if f else hidden_done.at(b - 1))
                    nc.tensor.matmul(p_up[:], wu[:, bass.ts(f, 128)], xt[:], start=True, stop=True).then_inc(up_full.sem, 1)
                pe.wait_ge(hidden_done.sem, hidden_done.at(b))
                pe.wait_ge(xf_done.sem, xf_done.at(b - 1))
                for t in range(TT):
                    for f in range(FT0):
                        ins = nc.tensor.matmul(p_down[:, bass.ts(t, 128)], hid[:, f, bass.ts(t, 128)], wd[:, f],
                                               start=(f == 0), stop=(f == FT0 - 1))
                ins.then_inc(down_full.sem, 1)

            def turn_attention(b):
                pe.wait_ge(attn_done.sem, attn_done.at(b))
                pe.wait_ge(x1_done.sem, x1_done.at(b - 1))
                turned_tiles(p_back, attn).then_inc(back_full.sem, 1)

            def project_out(b):
                pe.wait_ge(attn_copied.sem, attn_copied.at(b))
                by_tile(p_back, attn_t, wout[:], bout[:]).then_inc(back_full.sem, 1)

            def prologue():
                project_in(1)
                project_up(1)
                ffn(1)

            def tail(b, p):
                turn_attention(b)
                project_out(b)

            def batch(b, p, first, last):
                if not last:
                    project_in(b + 1)
                if not first:
                    turn_attention(b - 1)
                if not last:
                    project_up(b + 1)
                if not first:
                    project_out(b - 1)
                if not last:
                    ffn(b + 1)

            schedule(batch, tail, prologue, pe)


def layer1(nc, outer, io, dram, out, ident, minus_half, w_loaded, n_loads, stored0, hold, w):
    with ExitStack() as ctx:
        def sb(name, shape, dt=F32):
            return ctx.enter_context(nc.sbuf_tensor(name, shape, dt))

        def ps(name, shape, dt=F32):
            return ctx.enter_context(nc.psum_tensor(name, shape, dt))

        def count(name, per, by=1):
            return Count(outer.enter_context(nc.semaphore(name)), per, by)

        ND = 4
        NA = 8
        SEG = GROUPS // ST
        SLOTS = UNITS // ST
        w1, w3, w2 = w["w1"], w["w3"], w["w2"]
        spread = sb("spread", [96, 4, 128], BF16)
        pick = sb("pick", [3 * E, E, 128], BF16)
        ident_b = sb("ident_b", [128, 128], BF16)
        a_neg = sb("a_neg", [128, GROUPS])
        x = sb("y_x", [128, 2, TT, D])
        stats = sb("y_stats", [128, TT, 6])
        mv = sb("y_mv", [128, TT, 2])
        ve = sb("y_ve", [128, 2, TT])
        rstd = sb("y_rstd", [128, 2, TT])
        xn = sb("y_xn", [128, 2, TT, D])
        xr = sb("y_xr", [128, 2, TT, D])
        xt = sb("y_xt", [128, 2, T])
        ht = sb("y_ht", [128, T])
        ur = sb("ur", [128, ST, CONV - 1 + T])
        conv = sb("conv", [128, 2, ST, T])
        u = sb("u", [128, 2, ST, T])
        sz = sb("sz", [128, 2, ST, T])
        dtr = sb("dtr", [RDT, T])
        b_rep = sb("b_rep", [128, 2, T])
        c_rep = sb("c_rep", [128, 2, T])
        dtu = sb("dtu", [128, 2, ST, T])
        ez, rz = dtu[:, 0], dtu[:, 1]
        az, wz = conv[:, 0], conv[:, 1]
        rest = conv
        part = sb("y_part", [128, 3, 2, T], BF16)
        block_in = sb("block_in", [96, 2, ST, 4, T], BF16)
        eg = sb("eg", [128, TT, E])
        gates = sb("gates", [128, 2, TT, E])
        rank2 = sb("rank2", [128, 2, TT, E, E])
        rank = sb("rank", [128, TT, E])
        wsum = sb("wsum", [128, 2, TT])
        wpart = sb("wpart", [128, TT, 3, E], BF16)
        wrest = sb("wrest", [128, TT, E])
        wt = sb("wt", [3 * E, T], BF16)
        xw = sb("xw", [128, 2, T])
        da = sb("da", [128, ND, T])
        dbu = sb("dbu", [128, 3, T])
        hs = sb("hs", [128, 4, T])
        hc = sb("hc", [128, NA, T])
        y1 = sb("y1", [128, T])
        yt = sb("yt", [128, ST, T])
        sg = sb("sg", [128, SLOTS, T])
        hid = sb("y_hid", [128, 2, T])
        ot = sb("ot", [128, T])

        p_misc = ps("y_misc", [128, T])
        p_dt = ps("p_dt", [128, T])
        p_w = ps("p_w", [128, T])
        p_du = ps("p_du", [128, T])
        p_y = ps("p_y", [128, T])
        p_g = ps("p_g", [128, T])
        p_u = ps("p_u", [128, T])
        p_acc = ps("p_acc", [128, T])

        begun = outer.enter_context(nc.semaphore("begun"))
        staged = outer.enter_context(nc.semaphore("staged"))
        x_in = count("y_in", 1, 16)
        ln_stats = count("y_ln_stats", 4)
        ln_var = count("y_ln_var", 2)
        ln_rstd = count("y_ln_rstd", 2)
        ln_done = count("y_ln_done", 2)
        xr_done = count("y_xr_done", 1)
        (XT, HT, U0, U1, Z0, Z1, DTR, BREP, CREP, DT0, DT1, GATE, WT) = range(1, 14)
        prep_full = count("y_prep_full", WT)
        prep_free = count("y_prep_free", WT)
        z_done = count("z_done", 1)
        w_full = count("w_full", E)
        xw_done = count("xw_done", E + 1)
        conv_step = count("conv_step", 2 * CONV)
        u_done = count("u_done", 2)
        sp_exp = count("sp_exp", 1)
        sp_one = count("sp_one", 1)
        sp_ln = count("sp_ln", 1)
        sp_cut = count("sp_cut", 1)
        dt_step = count("dt_step", 4)
        part1 = count("y_part1", 2)
        rest1 = count("y_rest1", 2)
        part2 = count("y_part2", 2)
        part3 = count("y_part3", 2)
        stacked = [count(f"y_stacked{i}", 3 * 4, 16) for i in range(ST)]
        gate_exp = count("gate_exp", 1)
        route = count("route", 16)
        dt_full = count("dt_full", GROUPS)
        du_full = count("du_full", GROUPS)
        da_done = count("da_done", GROUPS)
        dbu_done = count("dbu_done", GROUPS)
        scanned = count("scanned", GROUPS)
        hc_done = count("hc_done", GROUPS)
        gathered = count("gathered", GROUPS // 4)
        y1_done = count("y1_done", ST)
        y_done = count("y_done", ST)
        g_full = count("g_full", UNITS)
        g_read = count("g_read", UNITS)
        u_full = count("u_full", UNITS)
        hid_done = count("hid_done", UNITS)
        hid_used = count("hid_used", UNITS)
        acc_full = count("acc_full", 1)
        acc_read = count("acc_read", 1)
        back_full = count("back_full", 1)
        res_done = count("res_done", 1)
        stored = count("y_stored", 1, 16)

        x_d = dram.rearrange("b (t p) d -> b p t d", p=128)
        out_d = out.rearrange("b (t p) d -> b p t d", p=128)

        order = [(s, j, i) for s in range(ST) for i in range(4) for j in range(4)]

        block = ctx.enter_context(nc.Block())

        def start(eng, mine):
            for c in mine:
                eng.sem_inc(c.sem, c.start)

        def schedule(eng_segment, tail, prologue, eng):
            prologue()
            eng_segment(1, 0, first=True, last=False)
            with eng.Fori(0, B // 2 - 1) as pair:
                for i in range(2):
                    eng_segment(pair * 2 + (2 + i), (1 + i) % 2, first=False, last=False)
            eng_segment(B, (B - 1) % 2, first=False, last=True)
            tail(B, (B - 1) % 2)

        weigh_at = {(m // SLOTS, 2 * (m % SLOTS) - 4): m // FT1 for m in range(0, UNITS, FT1)}

        @block.sync
        def _(sp):
            start(sp, [x_in, *stacked, stored])
            sp.dma_start(da[0:3 * E, 0:2], io["c_pick"].rearrange("r (a e) c -> r a (e c)", a=2)).then_inc(staged, 16)
            sp.dma_start(da[0:96, 2], io["c_spread"].rearrange("r i c -> r (i c)")).then_inc(staged, 16)
            sp.wait_ge(stored0, 1)

            def load(index, b, p):
                sp.wait_ge(xr_done.sem, xr_done.at(b - 2))
                hold(sp)
                sp.wait_ge(ln_done.sem, ln_done.at(b - 1))
                hold(sp)
                sp.dma_start(x[:, p], x_d[bass.ds(index, 1)].rearrange("o p t d -> p (o t) d")).then_inc(x_in.sem, 16)

            def stack(b, s):
                sp.wait_ge(part3.sem, part3.at(b, s + 1))
                hold(sp)
                sp.wait_ge(du_full.sem, du_full.at(b - 1, SEG * (s + 1)))
                hold(sp)
                for i in range(3):
                    for c in range(4):
                        sp.dma_start(block_in[32 * i:32 * i + 32, :, s, c], part[32 * c:32 * c + 32, i]).then_inc(stacked[s].sem, 16)

            def store(b, p):
                sp.wait_ge(res_done.sem, res_done.at(b))
                hold(sp)
                sp.dma_start(out_d[bass.ds(b - 1, 1)].rearrange("o p t d -> p (o t) d"), xr[:, p]).then_inc(stored.sem, 16)

            def prologue():
                load(0, 1, 0)
                load(1, 2, 1)
                stack(1, 0)

            def batch(b, p, first, last):
                stack(b, 1)
                if not first:
                    store(b - 1, 1 - p)
                if not last:
                    load((b + 1) % B, b + 2, p)
                    stack(b + 1, 0)

            schedule(batch, store, prologue, sp)
            sp.wait_ge(stored.sem, stored.at(B))
            sp.wait_ge(x_in.sem, x_in.at(B + 1))

        @block.gpsimd
        def _(pool):
            start(pool, [ln_rstd, xr_done, dt_step, rest1, part3, hc_done, y_done])
            nc.gpsimd.memset(ur[:, :, 0:CONV - 1], 0.0).then_inc(begun, 1)
            pool.wait_ge(begun, 5)

            def norm(b, p):
                for i in range(2):
                    pool.wait_ge(ln_var.sem, ln_var.at(b, i + 1))
                    nc.gpsimd.tensor_tensor(rstd[:, i], ve[:, i], minus_half[:], ALU.pow).then_inc(ln_rstd.sem, 1)
                pool.wait_ge(ln_done.sem, ln_done.at(b, 1))
                pool.wait_ge(stored.sem, stored.at(b - 2))
                nc.gpsimd.tensor_tensor(xr[:, p], x[:, p], xn[:, 0], ALU.add).then_inc(xr_done.sem, 1)

            def steps(b, p, s):
                if s == 0:
                    pool.wait_ge(sp_cut.sem, sp_cut.at(b))
                nc.gpsimd.tensor_tensor(dtu[:, 0, s], ez[:, s], rz[:, s], ALU.add).then_inc(dt_step.sem, 1)
                pool.wait_ge(dt_step.sem, dt_step.at(b, 2 * s + 1))
                if s == 0:
                    pool.wait_ge(u_done.sem, u_done.at(b))
                nc.gpsimd.tensor_tensor(dtu[:, 1, s], dtu[:, 0, s], u[:, p, s], ALU.mult).then_inc(dt_step.sem, 1)

            def second_rest(b, s):
                pool.wait_ge(part1.sem, part1.at(b, s + 1))
                pool.wait_ge(dt_step.sem, dt_step.at(b, 2 * s + 2))
                nc.gpsimd.tensor_tensor(rest[:, :, s], dtu[:, :, s], part[:, 0], ALU.subtract).then_inc(rest1.sem, 1)

            def third_part(b, s):
                pool.wait_ge(part2.sem, part2.at(b, s + 1))
                pool.wait_ge(rest1.sem, rest1.at(b, s + 1))
                nc.gpsimd.tensor_tensor(part[:, 2], rest[:, :, s], part[:, 1], ALU.subtract).then_inc(part3.sem, 1)

            def times_c(b, p, k):
                pool.wait_ge(scanned.sem, scanned.at(b, k + 1))
                if k % 4 == 0:
                    pool.wait_ge(gathered.sem, gathered.at(b, k // 4 - 1) if k >= 8 else gathered.at(b - 1, 7 + k // 4))
                nc.gpsimd.tensor_tensor(hc[:, k % NA], hs[:, k % 4], c_rep[:, p], ALU.mult).then_inc(hc_done.sem, 1)

            def gate_y(b, p, s):
                pool.wait_ge(y1_done.sem, y1_done.at(b, s + 1))
                if s == 0:
                    pool.wait_ge(acc_full.sem, acc_full.at(b - 1))
                    pool.wait_ge(z_done.sem, z_done.at(b))
                nc.gpsimd.tensor_tensor(yt[:, s], y1[:], sz[:, p, s], ALU.mult).then_inc(y_done.sem, 1)

            def tail(b, p):
                gate_y(b, p, 1)

            def prologue():
                norm(1, 0)
                steps(1, 0, 0)
                second_rest(1, 0)
                third_part(1, 0)

            def batch(b, p, first, last):
                steps(b, p, 1)
                second_rest(b, 1)
                third_part(b, 1)
                if not first:
                    tail(b - 1, 1 - p)
                if not last:
                    norm(b + 1, 1 - p)
                for k in range(SEG):
                    times_c(b, p, k)
                gate_y(b, p, 0)
                for k in range(SEG, GROUPS):
                    times_c(b, p, k)
                    if not last:
                        if k == SEG + 7:
                            steps(b + 1, 1 - p, 0)
                        if k == SEG + 9:
                            second_rest(b + 1, 0)
                        if k == SEG + 11:
                            third_part(b + 1, 0)

            schedule(batch, tail, prologue, pool)

        @block.scalar
        def _(act):
            start(act, [prep_free, z_done, u_done, sp_exp, sp_ln, part1, part2, da_done, g_read, acc_read])
            act.wait_ge(w_loaded, 16 * n_loads)
            nc.scalar.activation(a_neg[:], w["a_log"][:], ACT.Exp).then_inc(begun, 1)
            act.wait_ge(begun, 6)

            def copy_out(b, n, to, rows=slice(0, 128), func=ACT.Copy, **how):
                act.wait_ge(prep_full.sem, prep_full.at(b, n))
                nc.scalar.activation(to, p_misc[rows, :], func, **how).then_inc(prep_free.sem, 1)

            def silu_u_z(b, p):
                for s in range(ST):
                    act.wait_ge(conv_step.sem, conv_step.at(b, 4 * s + 4))
                    nc.scalar.activation(u[:, p, s], conv[:, 1, s], ACT.Silu, bias=w["conv_b"][:, s:s + 1]).then_inc(u_done.sem, 1)
                act.wait_ge(prep_free.sem, prep_free.at(b, Z1))
                nc.scalar.activation(sz[:, p], sz[:, p], ACT.Silu).then_inc(z_done.sem, 1)

            def dt_in(b, s):
                act.wait_ge(prep_full.sem, prep_full.at(b, DT0 + s))
                if s == 0:
                    act.wait_ge(rest1.sem, rest1.at(b - 1))
                nc.scalar.activation(rz[:, s], p_misc[:], ACT.Relu, bias=w["dt_b"][:, s:s + 1])
                nc.scalar.activation(az[:, s], p_misc[:], ACT.Abs, bias=w["dt_b"][:, s:s + 1]).then_inc(prep_free.sem, 1)

            def exp_in(b):
                act.wait_ge(prep_free.sem, prep_free.at(b, DT1))
                nc.scalar.activation(ez, az, ACT.Exp, scale=-1.0).then_inc(sp_exp.sem, 1)
                act.wait_ge(prep_full.sem, prep_full.at(b, GATE))
                nc.scalar.activation(eg[:], p_misc[:, 0:TT * E].rearrange("p (t e) -> p t e", e=E), ACT.Exp, scale=-1.0)\
                    .then_inc(prep_free.sem, 1)

            def log_in(b):
                act.wait_ge(sp_one.sem, sp_one.at(b))
                nc.scalar.activation(az, wz, ACT.Ln).then_inc(sp_ln.sem, 1)

            def first_part(b, s):
                act.wait_ge(dt_step.sem, dt_step.at(b, 2 * s + 2))
                before = stacked[0].at(b) if s else stacked[1].at(b - 1)
                act.wait_ge(stacked[1 - s].sem, before)
                nc.scalar.activation(part[:, 0], dtu[:, :, s], ACT.Copy).then_inc(part1.sem, 1)

            def second_part(b, s):
                act.wait_ge(rest1.sem, rest1.at(b, s + 1))
                nc.scalar.activation(part[:, 1], rest[:, :, s], ACT.Copy).then_inc(part2.sem, 1)

            def decay(b, k):
                s, j, i = order[k]
                g = 16 * s + 4 * j + i
                act.wait_ge(dt_full.sem, dt_full.at(b, k + 1))
                act.wait_ge(scanned.sem, scanned.at(b, k - ND + 1) if k >= ND else scanned.at(b - 1, GROUPS - ND + k + 1))
                nc.scalar.activation(da[:, k % ND], p_dt[:], ACT.Exp, scale=a_neg[:, g:g + 1]).then_inc(da_done.sem, 1)

            def gate(b, m):
                act.wait_ge(g_full.sem, g_full.at(b, m + 1))
                act.wait_ge(hid_done.sem, hid_done.at(b, m - SLOTS + 1) if m >= SLOTS else hid_done.at(b - 1, m + SLOTS + 1))
                nc.scalar.activation(sg[:, m % SLOTS], p_g[:], ACT.Silu).then_inc(g_read.sem, 1)

            def weights_out(b):
                act.wait_ge(prep_full.sem, prep_full.at(b, WT))
                nc.scalar.activation(wt[:], p_misc[:].bitcast(BF16)[0:3 * E, 0:T], ACT.Copy).then_inc(prep_free.sem, 1)

            def tail(b, p):
                act.wait_ge(acc_full.sem, acc_full.at(b))
                act.wait_ge(back_full.sem, back_full.at(b - 1))
                nc.scalar.activation(ot[:], p_acc[:], ACT.Copy).then_inc(acc_read.sem, 1)

            def prologue():
                copy_out(1, XT, xt[:, 0])
                copy_out(1, HT, ht[:], scale=w["norm_w"])
                copy_out(1, U0, ur[:, 0, CONV - 1:])
                copy_out(1, U1, ur[:, 1, CONV - 1:])
                copy_out(1, Z0, sz[:, 0, 0])
                copy_out(1, Z1, sz[:, 0, 1])
                silu_u_z(1, 0)
                copy_out(1, DTR, dtr[:], slice(0, RDT))
                copy_out(1, BREP, b_rep[:, 0])
                copy_out(1, CREP, c_rep[:, 0])
                dt_in(1, 0)
                dt_in(1, 1)
                exp_in(1)
                log_in(1)
                first_part(1, 0)
                second_part(1, 0)

            def batch(b, p, first, last):
                q = 1 - p
                weights_out(b)
                for m in range(SLOTS):
                    gate(b, m)
                    if m == 1:
                        first_part(b, 1)
                    if m == 3:
                        second_part(b, 1)
                    if m == 4 and not first:
                        tail(b - 1, q)
                    if m == 7 and not last:
                        copy_out(b + 1, XT, xt[:, q])
                if not last:
                    copy_out(b + 1, HT, ht[:], scale=w["norm_w"])
                for k in range(SEG):
                    decay(b, k)
                    if last:
                        continue
                    if k == 0:
                        copy_out(b + 1, U0, ur[:, 0, CONV - 1:])
                    if k == 2:
                        copy_out(b + 1, U1, ur[:, 1, CONV - 1:])
                    if k == 4:
                        copy_out(b + 1, Z0, sz[:, q, 0])
                    if k == 6:
                        copy_out(b + 1, Z1, sz[:, q, 1])
                for m in range(SLOTS, UNITS):
                    gate(b, m)
                    if last:
                        continue
                    if m == SLOTS:
                        silu_u_z(b + 1, q)
                    if m == SLOTS + 2:
                        copy_out(b + 1, DTR, dtr[:], slice(0, RDT))
                    if m == SLOTS + 3:
                        copy_out(b + 1, BREP, b_rep[:, q])
                    if m == SLOTS + 4:
                        copy_out(b + 1, CREP, c_rep[:, q])
                    if m == SLOTS + 5:
                        dt_in(b + 1, 0)
                    if m == SLOTS + 6:
                        dt_in(b + 1, 1)
                for k in range(SEG, GROUPS):
                    decay(b, k)
                    if last:
                        continue
                    if k == SEG:
                        exp_in(b + 1)
                    if k == SEG + 3:
                        log_in(b + 1)
                    if k == SEG + 9:
                        first_part(b + 1, 0)
                    if k == SEG + 11:
                        second_part(b + 1, 0)

            schedule(batch, tail, prologue, act)

        @block.vector
        def _(dve):
            start(dve, [ln_stats, ln_var, ln_done, conv_step, sp_one, sp_cut, route, xw_done, dbu_done, scanned, y1_done,
                        hid_done, res_done])
            dve.wait_ge(w_loaded, 16 * n_loads)
            dve.wait_ge(staged, 32)
            nc.vector.tensor_copy(spread[:].rearrange("r i c -> r (i c)"), da[0:96, 2]).then_inc(begun, 1)
            nc.vector.tensor_copy(pick[:].rearrange("r (a e) c -> r a (e c)", a=2), da[0:3 * E, 0:2]).then_inc(begun, 1)
            nc.vector.tensor_copy(ident_b[:], ident[:]).then_inc(begun, 1)
            dve.wait_ge(begun, 5)
            nc.vector.tensor_scalar(a_neg[:], a_neg[:], -1.0, None, ALU.mult).then_inc(begun, 1)

            def norm(b, p):
                dve.wait_ge(x_in.sem, x_in.at(b))
                for t in range(TT):
                    ins = nc.vector.bn_stats(stats[:, t], x[:, p, t])
                ins.then_inc(ln_stats.sem, 1)
                dve.wait_ge(ln_stats.sem, ln_stats.at(b, 1))
                hold(dve)
                for t in range(TT):
                    ins = nc.vector.bn_aggr(mv[:, t], stats[:, t])
                ins.then_inc(ln_stats.sem, 1)
                dve.wait_ge(ln_stats.sem, ln_stats.at(b, 2))
                nc.vector.tensor_scalar(ve[:, 0], mv[:, :, 1], EPS, None, ALU.add).then_inc(ln_var.sem, 1)
                dve.wait_ge(ln_rstd.sem, ln_rstd.at(b, 1))
                nc.vector.tensor_tensor(wsum[:, 0], rstd[:, 0], rstd[:, 0], ALU.mult).then_inc(ln_stats.sem, 1)
                dve.wait_ge(ln_stats.sem, ln_stats.at(b, 3))
                nc.vector.tensor_tensor(wsum[:, 1], wsum[:, 0], mv[:, :, 1], ALU.mult).then_inc(ln_stats.sem, 1)
                dve.wait_ge(ln_stats.sem, ln_stats.at(b, 4))
                nc.vector.tensor_scalar(ve[:, 1], wsum[:, 1], EPS, None, ALU.add).then_inc(ln_var.sem, 1)
                dve.wait_ge(prep_full.sem, prep_full.at(b - 1, HT))
                dve.wait_ge(xr_done.sem, xr_done.at(b - 1))
                for t in range(TT):
                    ins = nc.vector.tensor_scalar(xn[:, 0, t], x[:, p, t], mv[:, t, 0:1], rstd[:, 0, t:t + 1],
                                                  ALU.subtract, ALU.mult)
                ins.then_inc(ln_done.sem, 1)
                dve.wait_ge(ln_done.sem, ln_done.at(b, 1))
                dve.wait_ge(ln_rstd.sem, ln_rstd.at(b, 2))
                for t in range(TT):
                    ins = nc.vector.tensor_scalar(xn[:, 1, t], xn[:, 0, t], rstd[:, 1, t:t + 1], None, ALU.mult)
                ins.then_inc(ln_done.sem, 1)

            def convolve(b, n):
                s, k = divmod(n, CONV)
                if k == 0:
                    dve.wait_ge(prep_free.sem, prep_free.at(b, U0 + s))
                    if s == 0:
                        dve.wait_ge(part3.sem, part3.at(b - 1))
                taps = ur[:, s, k:k + T]
                wk = w["conv_w"][:, s, k:k + 1]
                if k == 0:
                    ins = nc.vector.tensor_scalar(conv[:, 0, s], taps, wk, None, ALU.mult)
                else:
                    dve.wait_ge(conv_step.sem, conv_step.at(b, n))
                    ins = nc.vector.scalar_tensor_tensor(conv[:, k % 2, s], taps, wk, conv[:, 1 - k % 2, s], ALU.mult, ALU.add)
                ins.then_inc(conv_step.sem, 1)

            def softplus_one(b):
                dve.wait_ge(sp_exp.sem, sp_exp.at(b))
                nc.vector.tensor_scalar(wz, ez, 1.0, None, ALU.add).then_inc(sp_one.sem, 1)

            def softplus_cut(b):
                dve.wait_ge(sp_one.sem, sp_one.at(b))
                nc.vector.scalar_tensor_tensor(ez, wz, -1.0, ez, ALU.add, ALU.subtract).then_inc(route.sem, 1)

            def softplus_end(b):
                dve.wait_ge(sp_ln.sem, sp_ln.at(b))
                dve.wait_ge(route.sem, route.at(b, 1))
                nc.vector.tensor_tensor(ez, az, ez, ALU.subtract).then_inc(sp_cut.sem, 1)

            def routing(b, n):
                g = gates[:, 0]
                others = g.unsqueeze(2).to_broadcast([128, TT, E, E])
                mine = g.unsqueeze(3).to_broadcast([128, TT, E, E])
                first = w["before"][:].unsqueeze(1).to_broadcast([128, TT, E, E])
                if n == 0:
                    dve.wait_ge(prep_free.sem, prep_free.at(b, GATE))
                dve.wait_ge(route.sem, route.at(b, n + 1))
                if n == 0:
                    ins = nc.vector.tensor_scalar(gates[:, 1], eg[:], 1.0, None, ALU.add)
                elif n == 1:
                    hold(dve)
                    ins = nc.vector.reciprocal(gates[:, 0], gates[:, 1])
                elif n == 2:
                    nc.vector.tensor_tensor(rank2[:, 0], others, mine, ALU.is_gt)
                    ins = nc.vector.tensor_tensor(rank2[:, 1], others, mine, ALU.is_equal)
                elif n == 3:
                    ins = nc.vector.tensor_tensor(rank2[:, 1], rank2[:, 1], first, ALU.mult)
                elif n == 4:
                    ins = nc.vector.tensor_tensor(rank2[:, 0], rank2[:, 0], rank2[:, 1], ALU.add)
                elif n == 5:
                    ins = nc.vector.tensor_reduce(rank[:], rank2[:, 0], AX.X, ALU.add)
                elif n == 6:
                    ins = nc.vector.scalar_tensor_tensor(gates[:, 1], rank[:], 2.0, g, ALU.is_lt, ALU.mult)
                elif n == 7:
                    ins = nc.vector.tensor_reduce(wsum[:, 0], gates[:, 1], AX.X, ALU.add)
                elif n == 8:
                    ins = nc.vector.tensor_scalar(wsum[:, 1], wsum[:, 0], 3.0, None, ALU.mult)
                elif n == 9:
                    hold(dve)
                    ins = nc.vector.reciprocal(wsum[:, 0], wsum[:, 1])
                elif n == 10:
                    ins = nc.vector.tensor_tensor(gates[:, 0], gates[:, 1], wsum[:, 0].unsqueeze(2).to_broadcast([128, TT, E]),
                                                  ALU.mult)
                elif n == 11:
                    dve.wait_ge(prep_full.sem, prep_full.at(b - 1, WT))
                    ins = nc.vector.tensor_copy(wpart[:, :, 0], gates[:, 0])
                elif n == 12:
                    ins = nc.vector.tensor_tensor(wrest[:], gates[:, 0], wpart[:, :, 0], ALU.subtract)
                elif n == 13:
                    ins = nc.vector.tensor_copy(wpart[:, :, 1], wrest[:])
                else:
                    ins = nc.vector.tensor_tensor(wpart[:, :, 2], wrest[:], wpart[:, :, 1], ALU.subtract)
                ins.then_inc(route.sem, 1)

            def weigh_x(b, p, e):
                dve.wait_ge(u_full.sem, u_full.at(b, FT1 * (e - 1)) if e >= 2 else u_full.at(b - 1))
                if e < E:
                    dve.wait_ge(w_full.sem, w_full.at(b, e + 1))
                    ins = nc.vector.tensor_tensor(xw[:, e % 2], p_w[:], xt[:, p], ALU.mult)
                else:
                    ins = nc.vector.tensor_scalar(xw[:, e % 2], xt[:, p], 1.0 / 3.0, None, ALU.mult)
                ins.then_inc(xw_done.sem, 1)

            def inject(b, p, k):
                dve.wait_ge(scanned.sem, scanned.at(b, k - 2) if k >= 3 else scanned.at(b - 1, GROUPS - 2 + k))
                dve.wait_ge(du_full.sem, du_full.at(b, k + 1))
                nc.vector.tensor_tensor(dbu[:, k % 3], p_du[:], b_rep[:, p], ALU.mult).then_inc(dbu_done.sem, 1)

            def scan(b, k):
                dve.wait_ge(da_done.sem, da_done.at(b, k + 1))
                dve.wait_ge(dbu_done.sem, dbu_done.at(b, k + 1))
                dve.wait_ge(hc_done.sem, hc_done.at(b, k - 3) if k >= 4 else hc_done.at(b - 1, GROUPS - 3 + k))
                nc.vector.tensor_tensor_scan(hs[:, k % 4], da[:, k % ND], dbu[:, k % 3], 0.0, ALU.mult, ALU.add)\
                    .then_inc(scanned.sem, 1)

            def skip(b, p, s):
                dve.wait_ge(gathered.sem, gathered.at(b, 4 * s + 4))
                dve.wait_ge(y_done.sem, y_done.at(b, s) if s else y_done.at(b - 1))
                nc.vector.scalar_tensor_tensor(y1[:], u[:, p, s], w["d_skip"][:, s:s + 1], p_y[:], ALU.mult, ALU.add)\
                    .then_inc(y1_done.sem, 1)

            def hidden(b, m):
                dve.wait_ge(g_read.sem, g_read.at(b, m + 1))
                dve.wait_ge(u_full.sem, u_full.at(b, m + 1))
                dve.wait_ge(hid_used.sem, hid_used.at(b, m - 1) if m >= 2 else hid_used.at(b - 1, UNITS - 1 + m))
                nc.vector.tensor_tensor(hid[:, m % 2], p_u[:], sg[:, m % SLOTS], ALU.mult).then_inc(hid_done.sem, 1)

            def result(b, p):
                dve.wait_ge(back_full.sem, back_full.at(b))
                nc.vector.tensor_tensor(xr[:, p], p_misc[:].rearrange("p (t d) -> p t d", t=TT), xr[:, p], ALU.add)\
                    .then_inc(res_done.sem, 1)

            def tail(b, p):
                scan(b, GROUPS - 1)
                hidden(b, UNITS - 1)
                skip(b, p, 1)
                result(b, p)

            def prologue():
                norm(1, 0)
                for n in range(ST * CONV):
                    convolve(1, n)
                softplus_one(1)
                softplus_cut(1)
                softplus_end(1)
                for n in range(15):
                    routing(1, n)

            def slot(b, p, s, i):
                if i % 2 == 0:
                    hidden(b, SLOTS * s + i // 2)
                inject(b, p, SEG * s + i)
                if i:
                    scan(b, SEG * s + i - 1)
                if (s, i) in weigh_at:
                    weigh_x(b, p, weigh_at[s, i])

            def batch(b, p, first, last):
                q = 1 - p
                if not first:
                    tail(b - 1, q)
                weigh_x(b, p, 0)
                if not last:
                    norm(b + 1, q)
                for i in range(SEG):
                    slot(b, p, 0, i)
                    if not last and 5 <= i < 5 + ST * CONV:
                        convolve(b + 1, i - 5)
                scan(b, SEG - 1)
                hidden(b, SLOTS - 1)
                skip(b, p, 0)
                weigh_x(b, p, E // 2 + 1)
                for i in range(SEG):
                    slot(b, p, 1, i)
                    if last:
                        continue
                    if i == 2:
                        softplus_one(b + 1)
                    if i == 3:
                        softplus_cut(b + 1)
                    if i == 5:
                        softplus_end(b + 1)
                    if i > 3:
                        routing(b + 1, i - 4)
                if not last:
                    for n in range(12, 15):
                        routing(b + 1, n)

            schedule(batch, tail, prologue, dve)

        @block.tensor
        def _(pe):
            start(pe, [prep_full, w_full, dt_full, du_full, gathered, g_full, u_full, hid_used, acc_full, back_full])
            pe.wait_ge(w_loaded, 16 * n_loads)
            pe.wait_ge(begun, 6)

            def free(b, n):
                pe.wait_ge(prep_free.sem, prep_free.at(b, n))

            def turn_x(b, i):
                if i == 0:
                    pe.wait_ge(res_done.sem, res_done.at(b - 2))
                else:
                    free(b, XT)
                pe.wait_ge(ln_done.sem, ln_done.at(b, i + 1))
                for t in range(TT):
                    ins = nc.tensor.transpose(p_misc[:, bass.ts(t, 128)], xn[:, i, t], ident[:])
                ins.then_inc(prep_full.sem, 1)

            def in_proj(b, n):
                free(b, HT + n)
                nc.tensor.matmul(p_misc[:], w["win"][:, bass.ts(n, 128)], ht[:], start=True, stop=True).then_inc(prep_full.sem, 1)

            def x_proj(b, p, n):
                wt_, rows = ((w["wx_dt"], RDT), (w["wx_b"], 128), (w["wx_c"], 128))[n]
                if n == 0:
                    pe.wait_ge(u_done.sem, u_done.at(b))
                free(b, Z1 + n)
                for s in range(ST):
                    ins = nc.tensor.matmul(p_misc[0:rows], wt_[:, s], u[:, p, s], start=(s == 0), stop=(s == ST - 1))
                ins.then_inc(prep_full.sem, 1)

            def dt_proj(b, s):
                free(b, CREP + s)
                nc.tensor.matmul(p_misc[:], w["wdt"][:, bass.ts(s, 128)], dtr[:], start=True, stop=True).then_inc(prep_full.sem, 1)

            def gate_logits(b, p):
                free(b, DT1)
                for t in range(TT):
                    ins = nc.tensor.matmul(p_misc[:, bass.ts(t, E)], xt[:, p, bass.ts(t, 128)], w["wgate"][:], start=True, stop=True)
                ins.then_inc(prep_full.sem, 1)

            def turn_weights(b):
                free(b, GATE)
                pe.wait_ge(route.sem, route.at(b))
                turned = p_misc[:].bitcast(BF16)
                for t in range(TT):
                    ins = nc.tensor.transpose(turned[0:3 * E, bass.ts(t, 128)], wpart[:, t].rearrange("p i e -> p (i e)"), ident_b[:])
                ins.then_inc(prep_full.sem, 1)

            def spread_weight(b, e):
                if e == 0:
                    free(b, WT)
                pe.wait_ge(xw_done.sem, xw_done.at(b, e) if e else xw_done.at(b - 1))
                nc.tensor.matmul(p_w[:], pick[:, e], wt[:], start=True, stop=True).then_inc(w_full.sem, 1)

            def spread_dt(b, k):
                s, j, i = order[k]
                if k % SEG == 0:
                    pe.wait_ge(stacked[s].sem, stacked[s].at(b))
                pe.wait_ge(da_done.sem, da_done.at(b, k) if k else da_done.at(b - 1))
                nc.tensor.matmul(p_dt[:], spread[:, i], block_in[:, 0, s, j], start=True, stop=True).then_inc(dt_full.sem, 1)

            def spread_du(b, k):
                s, j, i = order[k]
                pe.wait_ge(dbu_done.sem, dbu_done.at(b, k) if k else dbu_done.at(b - 1))
                nc.tensor.matmul(p_du[:], spread[:, i], block_in[:, 1, s, j], start=True, stop=True).then_inc(du_full.sem, 1)

            def gather_y(b, q):
                pe.wait_ge(hc_done.sem, hc_done.at(b, 4 * q + 4))
                if q % 4 == 0:
                    pe.wait_ge(y1_done.sem, y1_done.at(b, q // 4) if q else y1_done.at(b - 1))
                for k in range(4 * q, 4 * q + 4):
                    s, j, i = order[k]
                    ins = nc.tensor.matmul(p_y[32 * j:32 * j + 32], w["gather"][:, i], hc[:, k % NA], start=(i == 0), stop=(i == 3))
                ins.then_inc(gathered.sem, 1)

            def gate(b, p, m):
                e, f = divmod(m, FT1)
                pe.wait_ge(g_read.sem, g_read.at(b, m) if m else g_read.at(b - 1))
                nc.tensor.matmul(p_g[:], w1[:, e, bass.ts(f, 128)], xt[:, p], start=True, stop=True).then_inc(g_full.sem, 1)

            def up(b, m):
                e, f = divmod(m, FT1)
                pe.wait_ge(hid_done.sem, hid_done.at(b, m) if m else hid_done.at(b - 1))
                pe.wait_ge(xw_done.sem, xw_done.at(b, e + 1))
                nc.tensor.matmul(p_u[:], w3[:, e, bass.ts(f, 128)], xw[:, e % 2], start=True, stop=True).then_inc(u_full.sem, 1)

            def down(b, m):
                e, f = divmod(m, FT1)
                if m == 0:
                    pe.wait_ge(acc_read.sem, acc_read.at(b - 1))
                pe.wait_ge(hid_done.sem, hid_done.at(b, m + 1))
                nc.tensor.matmul(p_acc[:], w2[:, e, f], hid[:, m % 2], start=(m == 0), stop=False).then_inc(hid_used.sem, 1)

            def out_proj(b):
                pe.wait_ge(y_done.sem, y_done.at(b))
                for s in range(ST):
                    ins = nc.tensor.matmul(p_acc[:], w["wo1"][:, s], yt[:, s], start=False, stop=(s == ST - 1))
                ins.then_inc(acc_full.sem, 1)

            def turn_back(b):
                pe.wait_ge(acc_read.sem, acc_read.at(b))
                for t in range(TT):
                    ins = nc.tensor.transpose(p_misc[:, bass.ts(t, 128)], ot[:, bass.ts(t, 128)], ident[:])
                ins.then_inc(back_full.sem, 1)

            def tail(b, p):
                down(b, UNITS - 1)
                gather_y(b, GROUPS // 4 - 1)
                out_proj(b)
                turn_back(b)

            def prologue():
                turn_x(1, 0)
                turn_x(1, 1)
                for n in range(4):
                    in_proj(1, n)
                for n in range(3):
                    x_proj(1, 0, n)
                for s in range(ST):
                    dt_proj(1, s)
                gate_logits(1, 0)

            def slot(b, p, s, i):
                k = SEG * s + i
                spread_dt(b, k)
                spread_du(b, k)
                if i % 2 == 0:
                    up(b, SLOTS * s + i // 2 + 1)
                else:
                    down(b, SLOTS * s + i // 2)
                if i in (6, 10, 14):
                    gather_y(b, 4 * s + (i - 6) // 4)
                if (s, i + 1) in weigh_at and weigh_at[s, i + 1] < E:
                    spread_weight(b, weigh_at[s, i + 1])

            def batch(b, p, first, last):
                q = 1 - p
                turn_weights(b)
                for m in range(SLOTS):
                    gate(b, p, m)
                    if m == 0 and not first:
                        down(b - 1, UNITS - 1)
                    if m == 1 and not first:
                        gather_y(b - 1, GROUPS // 4 - 1)
                    if m == 1:
                        spread_weight(b, 0)
                    if m == 4 and not first:
                        out_proj(b - 1)
                    if m == 6 and not first:
                        turn_back(b - 1)
                    if m == 6:
                        spread_weight(b, 1)
                    if m == 7 and not last:
                        turn_x(b + 1, 0)
                up(b, 0)
                if not last:
                    turn_x(b + 1, 1)
                for i in range(SEG):
                    slot(b, p, 0, i)
                    if not last and i in (0, 2, 4, 6):
                        in_proj(b + 1, i // 2)
                for m in range(SLOTS, UNITS):
                    gate(b, p, m)
                    if m == SLOTS:
                        down(b, SLOTS - 1)
                        spread_weight(b, E // 2 + 1)
                    if m == SLOTS + 1:
                        gather_y(b, 3)
                    if last:
                        continue
                    if m in (SLOTS + 2, SLOTS + 3, SLOTS + 4):
                        x_proj(b + 1, q, m - SLOTS - 2)
                    if m in (SLOTS + 5, SLOTS + 6):
                        dt_proj(b + 1, m - SLOTS - 5)
                    if m == SLOTS + 7:
                        gate_logits(b + 1, q)
                up(b, SLOTS)
                for i in range(SEG):
                    slot(b, p, 1, i)

            schedule(batch, tail, prologue, pe)


def laid_out(i):
    a = {k: np.asarray(v) for k, v in i.items()}
    c = np.ascontiguousarray
    column = np.arange(H * DH)
    head, dim = column // DH, column % DH
    swapped = (dim + DH // 2) % DH
    q_cols = [column, head * DH + swapped]
    up_cols = [head * 2 * DH + dim, head * 2 * DH + swapped, (column % H) * 2 * DH + DH + column // H]
    wup = np.concatenate([a["L0_attn_Wup"], a["L0_attn_bup"][None]], 0)
    per_tile = lambda v: v.reshape(ST, 128, -1).transpose(1, 0, 2).reshape(128, -1)
    xp = a["L1_attn_x_proj_w"].reshape(ST, 128, RDT + 2 * N).transpose(1, 0, 2)
    stacked = lambda routed, shared: np.concatenate([routed, shared[None]], 0)
    return {
        "x": c(a["L0_attn_x"]),
        "wq": c(np.stack([a["L0_attn_Wq"][:, q] for q in q_cols], 1)),
        "wdown": c(a["L0_attn_Wdown"]),
        "wup": c(np.stack([wup[:, k] for k in up_cols], 1)),
        "wout": c(a["L0_attn_Wout"]),
        "bq": c(np.stack([a["L0_attn_bq"][q] for q in q_cols])[None]),
        "bdown": c(a["L0_attn_bdown"][:, None]),
        "bout": c(a["L0_attn_bout"][None]),
        "wg": c(a["L0_ffn_w_gate"].T),
        "wu": c(a["L0_ffn_w_up"].T),
        "wd": c(a["L0_ffn_w_down"].T.reshape(FT0, 128, D).transpose(1, 0, 2)),
        "w1": c(stacked(a["L1_ffn_We1"], a["L1_ffn_Ws1"]).transpose(1, 0, 2)),
        "w3": c(stacked(a["L1_ffn_We3"], a["L1_ffn_Ws3"]).transpose(1, 0, 2)),
        "w2": c(stacked(a["L1_ffn_We2"], a["L1_ffn_Ws2"]).reshape(E + 1, FT1, 128, D).transpose(2, 0, 1, 3)),
        "win": c(a["L1_attn_in_proj_w"]),
        "wx_dt": c(xp[:, :, :RDT]),
        "wx_b": c(np.tile(xp[:, :, RDT:RDT + N], (1, 1, 128 // N))),
        "wx_c": c(np.tile(xp[:, :, RDT + N:], (1, 1, 128 // N))),
        "wdt": c(a["L1_attn_dt_proj_w"]),
        "wo1": c(a["L1_attn_out_proj_w"].reshape(ST, 128, D).transpose(1, 0, 2)),
        "wgate": c(a["L1_ffn_Wg"]),
        "vecs": c(np.concatenate([a["L1_attn_norm_w"][:, None], per_tile(a["L1_attn_conv_w"]), per_tile(a["L1_attn_conv_b"]),
                                  per_tile(a["L1_attn_dt_proj_b"]), per_tile(a["L1_attn_D"])], 1)),
        "a_log": c(a["L1_attn_A_log"].reshape(GROUPS, 128 // N, N).transpose(1, 2, 0).reshape(128, GROUPS)),
    }


def kernel(**inputs):
    import concourse.bacc as bacc
    from concourse.bass_utils import run_bass_kernel_spmd

    arrays = {**laid_out(inputs), **constants()}
    nc = bacc.Bacc("TRN2", target_bir_lowering=False, num_devices=1)
    io = {n: nc.dram_tensor("in_" + n, v.shape, mybir.dt.from_np(v.dtype), kind="ExternalInput").ap() for n, v in arrays.items()}
    out = nc.dram_tensor("out", (B, T, D), F32, kind="ExternalOutput").ap()
    program(nc, io, out)
    return run_bass_kernel_spmd(nc, [{"in_" + n: v for n, v in arrays.items()}], core_ids=[0]).results[0]["out"]
```

```python
from contextlib import ExitStack

import numpy as np

import concourse.bass as bass
from concourse import mybir

F32 = mybir.dt.float32
BF16 = mybir.dt.bfloat16
I32 = mybir.dt.int32
ALU = mybir.AluOpType
ACT = mybir.ActivationFunctionType
AX = mybir.AxisListType

B, T, D = 8, 512, 128
TT = T // 128
HALF = TT // 2
H, DH = 16, 8
LAT = 32
FF0 = 384
FT0 = FF0 // 128
DI, N = 256, 16
ST = DI // 128
GROUPS = DI * N // 128
CONV = 4
RDT = 64
E = 8
FF1 = 256
FT1 = FF1 // 128
UNITS = (E + 1) * FT1
EPS = 1e-5


class Count:

    def __init__(self, sem, per, by=1):
        self.sem, self.per, self.by = sem, per, by
        self.start = 2 * per * by

    def at(self, b, n=None):
        n = self.per if n is None else n
        return (b + 1) * (self.per * self.by) + n * self.by


def constants():
    inv = (1.0 / np.float32(10000.0) ** (np.arange(0, DH, 2, dtype=np.float32) / np.float32(DH))).astype(np.float32)
    angle = (np.arange(T, dtype=np.float32)[None, :] * inv[:, None]).astype(np.float32).astype(np.float64)
    dim = np.arange(128) % DH
    cos = np.cos(angle)[dim % (DH // 2)]
    sin = np.sin(angle)[dim % (DH // 2)] * np.where(dim < DH // 2, -1.0, 1.0)[:, None]
    scale = 1.0 / np.sqrt(DH)
    rope = np.stack([cos * scale, sin * scale, cos, sin]).astype(np.float32)
    rope = np.ascontiguousarray(rope.reshape(4, 128, TT, 128).transpose(3, 0, 2, 1))
    ident = np.eye(128, dtype=np.float32)
    spread = np.zeros((3, 32, 4, 128), np.float32)
    for i in range(4):
        for p in range(128):
            spread[:, i * 8 + p // N, i, p] = 1
    gather = np.zeros((128, 4, 32), np.float32)
    for i in range(4):
        for p in range(128):
            gather[p, i, i * 8 + p // N] = 1
    pick = np.tile(np.eye(E, dtype=np.float32)[None, :, :, None], (3, 1, 1, 128))
    before = np.tile((np.arange(E)[None, :] < np.arange(E)[:, None]).astype(np.float32)[None], (128, 1, 1))
    return {
        "c_rope": rope,
        "c_ident": ident,
        "c_spread": spread.reshape(96, 4, 128),
        "c_gather": gather,
        "c_pick": pick.reshape(3 * E, E, 128),
        "c_before": before,
    }


def program(nc, io, out):
    dram = nc.dram_tensor("layer0_out", (B, T, D), F32, kind="Internal").ap()
    with ExitStack() as ctx:
        def sem(name):
            return ctx.enter_context(nc.semaphore(name))

        def sb(name, shape, dt=F32):
            return ctx.enter_context(nc.sbuf_tensor(name, shape, dt))

        ident = sb("ident", [128, 128])
        win = sb("win", [128, 2 * DI])
        wx = sb("wx", [128, ST, RDT + 2 * N])
        wdt = sb("wdt", [RDT, DI])
        wo1 = sb("wo1", [128, ST, D])
        wgate = sb("wgate", [128, E])
        vecs = sb("vecs", [128, 1 + ST * (CONV + 3)])
        a_log = sb("a_log", [128, GROUPS])
        gather = sb("gather", [128, 4, 32])
        before = sb("before", [128, E, E])
        w1 = sb("w1", [128, E + 1, FF1])
        w3 = sb("w3", [128, E + 1, FF1])
        w2 = sb("w2", [128, E + 1, FT1, D])
        norm_w = vecs[:, 0:1]
        conv_w = vecs[:, 1:1 + ST * CONV].rearrange("p (s k) -> p s k", s=ST)
        conv_b = vecs[:, 1 + ST * CONV:1 + ST * (CONV + 1)]
        dt_b = vecs[:, 1 + ST * (CONV + 1):1 + ST * (CONV + 2)]
        d_skip = vecs[:, 1 + ST * (CONV + 2):1 + ST * (CONV + 3)]
        w_loaded = sem("w_loaded")
        layer1_loads = [
            (win, "win"), (wx, "wx"),
            (wdt, "wdt"), (wo1, "wo1"), (wgate, "wgate"), (vecs, "vecs"), (a_log, "a_log"), (gather, "c_gather"),
            (before, "c_before"), (w1, "w1"), (w3, "w3"), (w2, "w2"),
        ]
        minus_half = sb("minus_half", [128, TT])
        own_wait = sem("own_wait")
        stored0 = sem("stored0")

        def hold(eng):
            eng.sem_inc(own_wait, 1)

        layer0(nc, ctx, io, dram, ident, minus_half, w_loaded, layer1_loads, stored0, hold)
        layer1(nc, ctx, io, dram, out, ident, minus_half, w_loaded, len(layer1_loads), stored0, hold,
               dict(win=win, wx=wx, wdt=wdt, wo1=wo1, wgate=wgate,
                    norm_w=norm_w, conv_w=conv_w, conv_b=conv_b, dt_b=dt_b, d_skip=d_skip, a_log=a_log,
                    gather=gather, before=before, w1=w1, w3=w3, w2=w2))


def layer0(nc, outer, io, dram, ident, minus_half, w_loaded, layer1_loads, stored0, hold):
    with ExitStack() as ctx:
        def sb(name, shape, dt=F32):
            return ctx.enter_context(nc.sbuf_tensor(name, shape, dt))

        def ps(name, shape, dt=F32):
            return ctx.enter_context(nc.psum_tensor(name, shape, dt))

        def count(name, per, by=1):
            return Count(outer.enter_context(nc.semaphore(name)), per, by)

        wq = sb("wq", [128, 2, 128])
        wdown = sb("wdown", [128, LAT])
        wup = sb("wup", [LAT + 1, 3, 128])
        wout = sb("wout", [128, D])
        bq = sb("bq", [1, 2, 128])
        bdown = sb("bdown", [LAT, 1])
        bout = sb("bout", [1, D])
        one_row = sb("one_row", [1, 128])
        rope = sb("rope", [128, 4, TT, 128])
        wg_i = sb("wg_i", [128, FF0], I32)
        wu_i = sb("wu_i", [128, FF0], I32)
        wd_i = sb("wd_i", [128, FT0, D], I32)
        wg = sb("wg", [128, FF0])
        wu = sb("wu", [128, FF0])
        wd = sb("wd", [128, FT0, D])
        x = sb("x", [128, 2, TT, D])
        stats = sb("stats", [128, TT, 6])
        mv = sb("mv", [128, TT, 2])
        ve = sb("ve", [128, TT])
        rstd = sb("rstd", [128, TT])
        xn = sb("xn", [128, TT, D])
        xt = sb("xt", [128, T])
        lat = sb("lat", [LAT + 1, T])
        turn = sb("turn", [128, 4, TT, 128])
        rq = sb("rq", [128, 2, TT, H, DH])
        rk = sb("rk", [128, 2, TT, H, DH])
        v = sb("v", [128, 2, TT, DH, H])
        score_prod = sb("score_prod", [128, HALF, H * H * DH])
        value_prod = sb("value_prod", [128, HALF, H * H * DH])
        sc = sb("sc", [128, TT, H, H])
        negmax = sb("negmax", [128, TT, H])
        den = sb("den", [128, TT, H])
        rden = sb("rden", [128, TT, H])
        raw = sb("raw", [128, 2, H, DH])
        attn = sb("attn", [128, TT, D])
        attn_t = sb("attn_t", [128, T])
        hid = sb("hid", [128, FT0, T])
        x1 = sb("x1", [128, 2, TT, D])

        p_xt = ps("p_xt", [128, T])
        p_q = ps("p_q", [128, T])
        p_qs = ps("p_qs", [128, T])
        p_lat = ps("p_lat", [128, T])
        p_up = ps("p_up", [128, T])
        p_down = ps("p_down", [128, T])
        p_back = ps("p_back", [128, T])
        p_raw = ps("p_raw", [128, 128])

        loaded0 = outer.enter_context(nc.semaphore("loaded0"))
        setup = outer.enter_context(nc.semaphore("setup"))
        small_loads = [(ident, "c_ident"), (wq, "wq"), (wdown, "wdown"), (wup, "wup"), (wout, "wout"),
                       (bq, "bq"), (bdown, "bdown"), (bout, "bout"), (rope, "c_rope"),
                       (wg_i, "wg"), (wu_i, "wu"), (wd_i, "wd")]

        x_in = count("x_in", 1, 16)
        ln_stats = count("ln_stats", 2)
        ln_var = count("ln_var", 1)
        ln_rstd = count("ln_rstd", 1)
        ln_done = count("ln_done", 1)
        xt_full = count("xt_full", 1)
        xt_copied = count("xt_copied", 1)
        q_full = count("q_full", 4)
        turned = count("turned", 4)
        rope_sum = count("rope_sum", 2)
        lat_full = count("lat_full", 2)
        lat_copied = count("lat_copied", 2)
        gate_full = count("gate_full0", FT0)
        gated = count("gated0", FT0)
        up_full = count("up_full0", FT0)
        hidden_done = count("hidden_done0", FT0)
        down_full = count("down_full", 1)
        xf_done = count("xf_done", 1)
        products = count("products", 2)
        products_pool = count("products_pool", 2)
        scored = count("scored", TT)
        soft = count("soft", 4)
        exp_done = count("exp_done", 2)
        den_step = count("den_step", 4)
        weighed = count("weighed", TT)
        summed = count("summed", 2)
        raw_full = count("raw_full", 2)
        attn_done = count("attn_done", 2)
        back_full = count("back_full0", 2)
        attn_copied = count("attn_copied", 1)
        x1_done = count("x1_done", 1)
        stored = count("stored", 1, 16)

        x_d = io["x"].rearrange("b (t p) d -> b p t d", p=128)
        x1_d = dram.rearrange("b (t p) d -> b p t d", p=128)
        block = ctx.enter_context(nc.Block())

        def start(eng, mine):
            for c in mine:
                eng.sem_inc(c.sem, c.start)

        def schedule(batch, tail, prologue, eng):
            prologue()
            batch(1, 0, first=True, last=False)
            with eng.Fori(0, B // 2 - 1) as pair:
                for i in range(2):
                    batch(pair * 2 + (2 + i), (1 + i) % 2, first=False, last=False)
            batch(B, (B - 1) % 2, first=False, last=True)
            tail(B, (B - 1) % 2)

        def tiles(j):
            return slice(HALF * j, HALF * j + HALF)

        def score_products(eng, p, j, i):
            t = HALF * j + i
            return eng.tensor_tensor(score_prod[:, i].rearrange("p (h g d) -> p h g d", h=H, g=H),
                                     rq[:, p, t].unsqueeze(2).to_broadcast([128, H, H, DH]),
                                     rk[:, p, t].unsqueeze(1).to_broadcast([128, H, H, DH]), ALU.mult)

        def value_products(eng, p, j, i):
            t = HALF * j + i
            return eng.tensor_tensor(value_prod[:, i].rearrange("p (h d g) -> p h d g", h=H, g=H),
                                     sc[:, t].unsqueeze(2).to_broadcast([128, H, DH, H]),
                                     v[:, p, t].unsqueeze(1).to_broadcast([128, H, DH, H]), ALU.mult)

        @block.sync
        def _(sp):
            start(sp, [x_in, stored])
            sp.dma_start(x[:, 0], x_d[0]).then_inc(x_in.sem, 16)
            for tile, name in small_loads:
                sp.dma_start(tile[:], io[name]).then_inc(loaded0, 16)

            def load(index, b, p):
                sp.wait_ge(xf_done.sem, xf_done.at(b - 2))
                hold(sp)
                sp.wait_ge(ln_done.sem, ln_done.at(b - 1))
                hold(sp)
                sp.dma_start(x[:, p], x_d[bass.ds(index, 1)].rearrange("o p t d -> p (o t) d")).then_inc(x_in.sem, 16)

            def store(b, p):
                sp.wait_ge(x1_done.sem, x1_done.at(b))
                hold(sp)
                sp.dma_start(x1_d[bass.ds(b - 1, 1)].rearrange("o p t d -> p (o t) d"), x1[:, p]).then_inc(stored.sem, 16)

            def prologue():
                load(1, 2, 1)
                for tile, name in layer1_loads:
                    sp.dma_start(tile[:], io[name]).then_inc(w_loaded, 16)

            def batch(b, p, first, last):
                if not last:
                    load((b + 1) % B, b + 2, p)
                if not first:
                    store(b - 1, 1 - p)

            schedule(batch, store, prologue, sp)
            sp.wait_ge(stored.sem, stored.at(B))
            sp.wait_ge(x_in.sem, x_in.at(B + 1))
            sp.sem_inc(stored0, 1)

        @block.gpsimd
        def _(pool):
            start(pool, [ln_rstd, rope_sum, products_pool, weighed])
            nc.gpsimd.memset(minus_half[:], -0.5).then_inc(setup, 1)
            pool.wait_ge(setup, 1)
            nc.gpsimd.memset(lat[LAT:LAT + 1, :], 1.0).then_inc(setup, 1)
            pool.wait_ge(setup, 2)
            nc.gpsimd.memset(one_row[:], 1.0).then_inc(setup, 1)
            pool.wait_ge(setup, 3)

            def root(b):
                pool.wait_ge(ln_var.sem, ln_var.at(b))
                nc.gpsimd.tensor_tensor(rstd[:], ve[:], minus_half[:], ALU.pow).then_inc(ln_rstd.sem, 1)

            def add_turns(b, p, n):
                pool.wait_ge(turned.sem, turned.at(b, 2 * n + 2))
                pool.wait_ge(products.sem, products.at(b - 2))
                pool.wait_ge(products_pool.sem, products_pool.at(b - 2))
                nc.gpsimd.tensor_tensor((rk if n else rq)[:, p].rearrange("p t h d -> p t (h d)"), turn[:, 2 * n], turn[:, 2 * n + 1],
                                        ALU.add).then_inc(rope_sum.sem, 1)

            def scores(b, p, j):
                pool.wait_ge(rope_sum.sem, rope_sum.at(b))
                pool.wait_ge(scored.sem, scored.at(b, 2) if j else scored.at(b - 1))
                score_products(nc.gpsimd, p, j, 1).then_inc(products_pool.sem, 1)

            def weigh(b, p, j, i):
                pool.wait_ge(exp_done.sem, exp_done.at(b, j + 1))
                pool.wait_ge(lat_copied.sem, lat_copied.at(b))
                last = raw_full if i else summed
                pool.wait_ge(last.sem, last.at(b, 1) if j else last.at(b - 1))
                value_products(nc.gpsimd, p, j, i).then_inc(weighed.sem, 1)

            def prologue():
                root(1)
                for n in range(2):
                    add_turns(1, 0, n)
                scores(1, 0, 0)
                root(2)

            def batch(b, p, first, last):
                q = 1 - p
                scores(b, p, 1)
                weigh(b, p, 0, 0)
                weigh(b, p, 0, 1)
                if not last:
                    add_turns(b + 1, q, 0)
                    add_turns(b + 1, q, 1)
                    scores(b + 1, q, 0)
                    root(b + 2)
                weigh(b, p, 1, 0)
                weigh(b, p, 1, 1)

            schedule(batch, lambda b, p: None, prologue, pool)

        @block.scalar
        def _(act):
            start(act, [xt_copied, lat_copied, gated, exp_done, attn_copied])
            act.wait_ge(loaded0, 16 * len(small_loads))
            act.wait_ge(setup, 3)

            def copy_xt(b):
                act.wait_ge(xt_full.sem, xt_full.at(b))
                act.wait_ge(up_full.sem, up_full.at(b - 1))
                nc.scalar.activation(xt[:], p_xt[:], ACT.Copy).then_inc(xt_copied.sem, 1)

            def copy_latent(b):
                act.wait_ge(lat_full.sem, lat_full.at(b, 1))
                nc.scalar.activation(lat[0:LAT], p_lat[0:LAT, :], ACT.Identity, bias=bdown[:, 0:1]).then_inc(lat_copied.sem, 1)

            def copy_v(b, p):
                act.wait_ge(lat_full.sem, lat_full.at(b, 2))
                act.wait_ge(weighed.sem, weighed.at(b - 2))
                nc.scalar.activation(v[:, p].rearrange("p t d g -> p (t d g)"), p_lat[:], ACT.Copy).then_inc(lat_copied.sem, 1)

            def gates(b):
                for f in range(FT0):
                    act.wait_ge(gate_full.sem, gate_full.at(b, f + 1))
                    if f == 0:
                        act.wait_ge(down_full.sem, down_full.at(b - 1))
                    nc.scalar.activation(hid[:, f], p_back[:], ACT.Silu, scale=1.0 / 127.0).then_inc(gated.sem, 1)

            def soften(b, j):
                act.wait_ge(soft.sem, soft.at(b, 2 * j + 2))
                nc.scalar.activation(sc[:, tiles(j)], sc[:, tiles(j)], ACT.Exp).then_inc(exp_done.sem, 1)

            def copy_attention(b):
                act.wait_ge(back_full.sem, back_full.at(b, 1))
                nc.scalar.activation(attn_t[:], p_back[:], ACT.Copy).then_inc(attn_copied.sem, 1)

            def prologue():
                copy_xt(1)
                copy_latent(1)
                copy_v(1, 0)
                gates(1)
                soften(1, 0)

            def batch(b, p, first, last):
                q = 1 - p
                if not last:
                    copy_xt(b + 1)
                    copy_latent(b + 1)
                if not last:
                    copy_v(b + 1, q)
                if not first:
                    copy_attention(b - 1)
                soften(b, 1)
                if not last:
                    gates(b + 1)
                    soften(b + 1, 0)

            schedule(batch, lambda b, p: copy_attention(b), prologue, act)

        @block.vector
        def _(dve):
            start(dve, [ln_stats, ln_var, ln_done, turned, hidden_done, xf_done, products, scored, soft, den_step, summed,
                        attn_done, x1_done])

            def statistics(b, p):
                dve.wait_ge(x_in.sem, x_in.at(b))
                for t in range(TT):
                    ins = nc.vector.bn_stats(stats[:, t], x[:, p, t])
                ins.then_inc(ln_stats.sem, 1)
                dve.wait_ge(ln_stats.sem, ln_stats.at(b, 1))
                hold(dve)
                for t in range(TT):
                    ins = nc.vector.bn_aggr(mv[:, t], stats[:, t])
                ins.then_inc(ln_stats.sem, 1)
                dve.wait_ge(ln_stats.sem, ln_stats.at(b, 2))
                nc.vector.tensor_scalar(ve[:], mv[:, :, 1], EPS, None, ALU.add).then_inc(ln_var.sem, 1)

            def normalize(b, p):
                dve.wait_ge(ln_rstd.sem, ln_rstd.at(b))
                dve.wait_ge(xt_full.sem, xt_full.at(b - 1))
                for t in range(TT):
                    ins = nc.vector.tensor_scalar(xn[:, t], x[:, p, t], mv[:, t, 0:1], rstd[:, t:t + 1], ALU.subtract, ALU.mult)
                ins.then_inc(ln_done.sem, 1)

            def turns(b, n):
                for i, source in enumerate((p_q, p_qs)):
                    s = 2 * n + i
                    dve.wait_ge(q_full.sem, q_full.at(b, s + 1))
                    if i == 0:
                        dve.wait_ge(rope_sum.sem, rope_sum.at(b - 1, n + 1))
                    nc.vector.tensor_tensor(turn[:, s], source[:].rearrange("p (t c) -> p t c", t=TT), rope[:, s], ALU.mult)\
                        .then_inc(turned.sem, 1)

            def scores(b, p, j):
                dve.wait_ge(rope_sum.sem, rope_sum.at(b))
                dve.wait_ge(scored.sem, scored.at(b, 1) if j else scored.at(b - 1, HALF + 1))
                score_products(nc.vector, p, j, 0).then_inc(products.sem, 1)

            def sum_scores(b, j, i):
                if i == 0:
                    dve.wait_ge(products.sem, products.at(b, j + 1))
                    dve.wait_ge(weighed.sem, weighed.at(b - 1, HALF * (j + 1)))
                else:
                    dve.wait_ge(products_pool.sem, products_pool.at(b, j + 1))
                nc.vector.tensor_reduce(sc[:, HALF * j + i], score_prod[:, i].rearrange("p (h g d) -> p h g d", h=H, g=H),
                                        AX.X, ALU.add).then_inc(scored.sem, 1)

            def less_maximum(b, j):
                dve.wait_ge(scored.sem, scored.at(b, HALF * (j + 1)))
                nc.vector.tensor_reduce(negmax[:, tiles(j)], sc[:, tiles(j)], AX.X, ALU.max, negate=True).then_inc(soft.sem, 1)
                dve.wait_ge(soft.sem, soft.at(b, 2 * j + 1))
                nc.vector.tensor_tensor(sc[:, tiles(j)], sc[:, tiles(j)],
                                        negmax[:, tiles(j)].unsqueeze(3).to_broadcast([128, HALF, H, H]), ALU.add)\
                    .then_inc(soft.sem, 1)

            def denominators(b, j):
                dve.wait_ge(exp_done.sem, exp_done.at(b, j + 1))
                nc.vector.tensor_reduce(den[:, tiles(j)], sc[:, tiles(j)], AX.X, ALU.add).then_inc(den_step.sem, 1)

            def sum_values(b, j):
                dve.wait_ge(weighed.sem, weighed.at(b, HALF * j + 1))
                dve.wait_ge(attn_done.sem, attn_done.at(b - 1, j + 1))
                nc.vector.tensor_reduce(raw[:, j], value_prod[:, 0].rearrange("p (h d g) -> p h d g", h=H, g=H), AX.X, ALU.add)\
                    .then_inc(summed.sem, 1)

            def divide(b, j):
                dve.wait_ge(den_step.sem, den_step.at(b, 2 * j + 1))
                hold(dve)
                nc.vector.reciprocal(rden[:, tiles(j)], den[:, tiles(j)]).then_inc(den_step.sem, 1)
                dve.wait_ge(den_step.sem, den_step.at(b, 2 * j + 2))
                dve.wait_ge(summed.sem, summed.at(b, j + 1))
                dve.wait_ge(raw_full.sem, raw_full.at(b, j + 1))
                dve.wait_ge(back_full.sem, back_full.at(b - 1, 1))
                for i, sums in enumerate((raw[:, j], p_raw[:].rearrange("p (h d) -> p h d", h=H))):
                    t = HALF * j + i
                    ins = nc.vector.tensor_tensor(attn[:, t].rearrange("p (h d) -> p h d", h=H), sums,
                                                  rden[:, t].unsqueeze(2).to_broadcast([128, H, DH]), ALU.mult)
                ins.then_inc(attn_done.sem, 1)

            def hidden(b, f):
                dve.wait_ge(up_full.sem, up_full.at(b, f + 1))
                dve.wait_ge(gated.sem, gated.at(b, f + 1))
                nc.vector.scalar_tensor_tensor(hid[:, f], p_up[:], 1.0 / 127.0 ** 2, hid[:, f],
                                               ALU.mult, ALU.mult).then_inc(hidden_done.sem, 1)

            def add_ffn(b, p):
                dve.wait_ge(down_full.sem, down_full.at(b))
                dve.wait_ge(stored.sem, stored.at(b - 2))
                nc.vector.tensor_tensor(x1[:, p], p_down[:].rearrange("p (t d) -> p t d", t=TT), x[:, p], ALU.add)\
                    .then_inc(xf_done.sem, 1)

            def add_attention(b, p):
                dve.wait_ge(back_full.sem, back_full.at(b, 2))
                nc.vector.tensor_tensor(x1[:, p], p_back[:].rearrange("p (t d) -> p t d", t=TT), x1[:, p], ALU.add)\
                    .then_inc(x1_done.sem, 1)

            def prologue():
                dve.wait_ge(setup, 3)
                statistics(1, 0)
                normalize(1, 0)
                dve.wait_ge(loaded0, 16 * len(small_loads))
                nc.vector.tensor_copy(wg[:], wg_i[:]).then_inc(setup, 1)
                nc.vector.tensor_copy(wu[:], wu_i[:]).then_inc(setup, 1)
                nc.vector.tensor_copy(wd[:], wd_i[:]).then_inc(setup, 1)
                dve.wait_ge(setup, 6)
                for n in range(2):
                    turns(1, n)
                scores(1, 0, 0)
                hidden(1, 0)
                sum_scores(1, 0, 0)
                hidden(1, 1)
                sum_scores(1, 0, 1)
                less_maximum(1, 0)
                hidden(1, 2)
                statistics(2, 1)
                normalize(2, 1)
                add_ffn(1, 0)

            def tail(b, p):
                divide(b, 1)
                add_attention(b, p)

            def batch(b, p, first, last):
                q = 1 - p
                scores(b, p, 1)
                if not last:
                    turns(b + 1, 0)
                if not first:
                    divide(b - 1, 1)
                sum_scores(b, 1, 0)
                if not last:
                    turns(b + 1, 1)
                sum_scores(b, 1, 1)
                less_maximum(b, 1)
                denominators(b, 0)
                if not first:
                    add_attention(b - 1, q)
                if not last:
                    statistics(b + 2, p)
                sum_values(b, 0)
                if not last:
                    scores(b + 1, q, 0)
                    hidden(b + 1, 0)
                    sum_scores(b + 1, 0, 0)
                divide(b, 0)
                if not last:
                    hidden(b + 1, 1)
                    sum_scores(b + 1, 0, 1)
                    hidden(b + 1, 2)
                    less_maximum(b + 1, 0)
                    normalize(b + 2, p)
                denominators(b, 1)
                sum_values(b, 1)
                if not last:
                    add_ffn(b + 1, q)

            schedule(batch, tail, prologue, dve)

        @block.tensor
        def _(pe):
            start(pe, [raw_full, xt_full, q_full, lat_full, gate_full, up_full, down_full, back_full])
            pe.wait_ge(loaded0, 16 * len(small_loads))
            pe.wait_ge(setup, 6)

            def by_tile(to, lhs, rhs, bias=None):
                for t in range(TT):
                    ins = nc.tensor.matmul(to[:, bass.ts(t, 128)], lhs[:, bass.ts(t, 128)], rhs, start=True, stop=bias is None)
                    if bias is not None:
                        ins = nc.tensor.matmul(to[:, bass.ts(t, 128)], one_row[:], bias, start=False, stop=True)
                return ins

            def turned_tiles(to, src):
                for t in range(TT):
                    ins = nc.tensor.transpose(to[:, bass.ts(t, 128)], src[:, t], ident[:])
                return ins

            def project_in(b):
                pe.wait_ge(ln_done.sem, ln_done.at(b))
                turned_tiles(p_xt, xn).then_inc(xt_full.sem, 1)
                pe.wait_ge(xt_copied.sem, xt_copied.at(b))
                pe.wait_ge(lat_copied.sem, lat_copied.at(b - 1))
                nc.tensor.matmul(p_lat[0:LAT], wdown[:], xt[:], start=True, stop=True).then_inc(lat_full.sem, 1)
                pe.wait_ge(turned.sem, turned.at(b - 1, 3))
                by_tile(p_q, xt, wq[:, 0], bq[:, 0]).then_inc(q_full.sem, 1)
                pe.wait_ge(turned.sem, turned.at(b - 1, 4))
                by_tile(p_qs, xt, wq[:, 1], bq[:, 1]).then_inc(q_full.sem, 1)

            def project_up(b):
                pe.wait_ge(lat_copied.sem, lat_copied.at(b, 1))
                by_tile(p_lat, lat, wup[:, 2]).then_inc(lat_full.sem, 1)
                for n, to in enumerate((p_q, p_qs)):
                    pe.wait_ge(turned.sem, turned.at(b, n + 1))
                    by_tile(to, lat, wup[:, n]).then_inc(q_full.sem, 1)

            def ffn_up(b, f):
                if f == 0:
                    pe.wait_ge(x1_done.sem, x1_done.at(b - 2))
                pe.wait_ge(gated.sem, gated.at(b, f) if f else gated.at(b - 1))
                nc.tensor.matmul(p_back[:], wg[:, bass.ts(f, 128)], xt[:], start=True, stop=True).then_inc(gate_full.sem, 1)
                pe.wait_ge(hidden_done.sem, hidden_done.at(b, f) if f else hidden_done.at(b - 1))
                nc.tensor.matmul(p_up[:], wu[:, bass.ts(f, 128)], xt[:], start=True, stop=True).then_inc(up_full.sem, 1)

            def ffn_down(b):
                pe.wait_ge(hidden_done.sem, hidden_done.at(b))
                pe.wait_ge(xf_done.sem, xf_done.at(b - 1))
                for t in range(TT):
                    for f in range(FT0):
                        ins = nc.tensor.matmul(p_down[:, bass.ts(t, 128)], hid[:, f, bass.ts(t, 128)], wd[:, f],
                                               start=(f == 0), stop=(f == FT0 - 1))
                ins.then_inc(down_full.sem, 1)

            def sum_values(b, j):
                pe.wait_ge(weighed.sem, weighed.at(b, HALF * (j + 1)))
                pe.wait_ge(attn_done.sem, attn_done.at(b, 1) if j else attn_done.at(b - 1))
                products_of = value_prod[:, 1].rearrange("p (hd g) -> p hd g", g=H)
                for g in range(H):
                    ins = nc.tensor.matmul(p_raw[:], ident[:], products_of[:, :, g], start=(g == 0), stop=(g == H - 1))
                ins.then_inc(raw_full.sem, 1)

            def turn_attention(b, newest):
                pe.wait_ge(gated.sem, gated.at(newest))
                pe.wait_ge(attn_done.sem, attn_done.at(b))
                pe.wait_ge(x1_done.sem, x1_done.at(b - 1))
                turned_tiles(p_back, attn).then_inc(back_full.sem, 1)

            def project_out(b):
                pe.wait_ge(attn_copied.sem, attn_copied.at(b))
                by_tile(p_back, attn_t, wout[:], bout[:]).then_inc(back_full.sem, 1)

            def prologue():
                project_in(1)
                project_up(1)
                for f in range(FT0):
                    ffn_up(1, f)
                ffn_down(1)

            def tail(b, p):
                sum_values(b, 1)
                turn_attention(b, b)
                project_out(b)

            def batch(b, p, first, last):
                if not last:
                    project_in(b + 1)
                if not first:
                    sum_values(b - 1, 1)
                if not last:
                    project_up(b + 1)
                if not first:
                    turn_attention(b - 1, b)
                    project_out(b - 1)
                if not last:
                    ffn_up(b + 1, 0)
                sum_values(b, 0)
                if not last:
                    for f in range(1, FT0):
                        ffn_up(b + 1, f)
                    ffn_down(b + 1)

            schedule(batch, tail, prologue, pe)


def layer1(nc, outer, io, dram, out, ident, minus_half, w_loaded, n_loads, stored0, hold, w):
    with ExitStack() as ctx:
        def sb(name, shape, dt=F32):
            return ctx.enter_context(nc.sbuf_tensor(name, shape, dt))

        def ps(name, shape, dt=F32):
            return ctx.enter_context(nc.psum_tensor(name, shape, dt))

        def count(name, per, by=1):
            return Count(outer.enter_context(nc.semaphore(name)), per, by)

        ND = 4
        NA = 8
        NG = 3
        SEG = GROUPS // ST
        UNIT_LAG = 4
        w1, w3, w2 = w["w1"], w["w3"], w["w2"]
        spread = sb("spread", [96, 4, 128], BF16)
        pick = sb("pick", [3 * E, E, 128], BF16)
        ident_b = sb("ident_b", [128, 128], BF16)
        a_neg = sb("a_neg", [128, GROUPS])
        x = sb("y_x", [128, 2, TT, D])
        stats = sb("y_stats", [128, TT, 6])
        mv = sb("y_mv", [128, TT, 2])
        ve = sb("y_ve", [128, 2, TT])
        rstd = sb("y_rstd", [128, 2, TT])
        xn = sb("y_xn", [128, 2, TT, D])
        xr = sb("y_xr", [128, 2, TT, D])
        xt = sb("y_xt", [128, 2, T])
        ht = sb("y_ht", [128, T])
        ur = sb("ur", [128, ST, CONV - 1 + T])
        conv = sb("conv", [128, 2, ST, T])
        u = sb("u", [128, 2, ST, T])
        sz = sb("sz", [128, 2, ST, T])
        xd = sb("xd", [RDT + 2 * N, T])
        b_rep = sb("b_rep", [128, 2, T])
        c_rep = sb("c_rep", [128, 2, T])
        dtu = sb("dtu", [128, 2, ST, T])
        ez, rz = dtu[:, 0], dtu[:, 1]
        az, wz = conv[:, 0], conv[:, 1]
        rest = conv
        part = sb("y_part", [128, 3, 2, T], BF16)
        block_in = sb("block_in", [96, 2, ST, 4, T], BF16)
        eg = sb("eg", [128, TT, E])
        gates = sb("gates", [128, 2, TT, E])
        rank2 = sb("rank2", [128, 2, TT, E, E])
        rank = sb("rank", [128, TT, E])
        wsum = sb("wsum", [128, 2, TT])
        ms = sb("ms", [128, 2, TT])
        wpart = sb("wpart", [128, TT, 3, E], BF16)
        wrest = sb("wrest", [128, TT, E])
        wt = sb("wt", [3 * E, T], BF16)
        xw = sb("xw", [128, 2, T])
        da = sb("da", [128, ND, T])
        dbu = sb("dbu", [128, 4, T])
        hs = sb("hs", [128, 4, T])
        hc = sb("hc", [128, NA, T])
        y1 = sb("y1", [128, T])
        yt = sb("yt", [128, ST, T])
        g_in = sb("g_in", [128, NG, T])
        sg = sb("sg", [128, NG, T])
        hid = sb("y_hid", [128, 2, T])
        ot = sb("ot", [128, T])

        p_misc = ps("y_misc", [128, T])
        p_dt = ps("p_dt", [128, T])
        p_w = ps("p_w", [128, T])
        p_du = ps("p_du", [128, T])
        p_y = ps("p_y", [128, T])
        p_g = ps("p_g", [128, T])
        p_u = ps("p_u", [128, T])
        p_acc = ps("p_acc", [128, T])

        begun = outer.enter_context(nc.semaphore("begun"))
        staged = outer.enter_context(nc.semaphore("staged"))
        x_in = count("y_in", 1, 16)
        bc_out = count("bc_out", 1, 16)
        bc_in = count("bc_in", 2, 16)
        ln_stats = count("y_ln_stats", 4)
        ln_var = count("y_ln_var", 2)
        ln_rstd = count("y_ln_rstd", 2)
        ln_done = count("y_ln_done", 2)
        xr_done = count("y_xr_done", 1)
        (XT, HT, U0, U1, GATE, Z0, Z1, XD, DT0, DT1, WT) = range(1, 12)
        prep_full = count("y_prep_full", WT)
        prep_free = count("y_prep_free", WT)
        z_done = count("z_done", 1)
        w_full = count("w_full", E)
        xw_done = count("xw_done", E + 1)
        conv_step = count("conv_step", 2 * CONV)
        u_done = count("u_done", 2)
        sp_exp = count("sp_exp", 1)
        sp_one = count("sp_one", 1)
        sp_ln = count("sp_ln", 1)
        sp_step = count("sp_step", 2)
        dt_step = count("dt_step", 4)
        part1 = count("y_part1", 2)
        rest1 = count("y_rest1", 2)
        part2 = count("y_part2", 2)
        part3 = count("y_part3", 2)
        stacked = [count(f"y_stacked{i}", 3 * 4, 16) for i in range(ST)]
        route = count("route", 15)
        dt_full = count("dt_full", GROUPS)
        du_full = count("du_full", GROUPS)
        da_done = count("da_done", GROUPS)
        dbu_done = count("dbu_done", GROUPS)
        scanned = count("scanned", GROUPS)
        hc_done = count("hc_done", GROUPS)
        gathered = count("gathered", GROUPS // 4)
        y1_done = count("y1_done", ST)
        y_done = count("y_done", ST)
        g_full = count("g_full", UNITS)
        g_read = count("g_read", UNITS)
        one_more = count("one_more", UNITS)
        silu_done = count("silu_done", UNITS)
        u_full = count("u_full", UNITS)
        hid_done = count("hid_done", UNITS)
        hid_used = count("hid_used", UNITS)
        acc_full = count("acc_full", ST)
        acc_read = count("acc_read", 1)
        back_full = count("back_full", 1)
        res_done = count("res_done", 1)
        stored = count("y_stored", 1, 16)

        x_d = dram.rearrange("b (t p) d -> b p t d", p=128)
        out_d = out.rearrange("b (t p) d -> b p t d", p=128)
        bc_d = nc.dram_tensor("bc", (2 * N, T), F32, kind="Internal").ap()

        order = [(s, j, i) for s in range(ST) for i in range(4) for j in range(4)]
        unit_slot = [UNIT_LAG + m * GROUPS // UNITS for m in range(UNITS)]

        block = ctx.enter_context(nc.Block())

        def start(eng, mine):
            for c in mine:
                eng.sem_inc(c.sem, c.start)

        def schedule(batch, prologue, eng):
            prologue()
            batch(1, 0, old=False, new=True, nxt=True)
            with eng.Fori(0, B // 2 - 1) as pair:
                for i in range(2):
                    batch(pair * 2 + (2 + i), (1 + i) % 2, old=True, new=True, nxt=True)
            batch(B, (B - 1) % 2, old=True, new=True, nxt=False)
            batch(B + 1, 0, old=True, new=False, nxt=False)

        def units(b, p, k, ahead, old, new):
            for m, at in enumerate(unit_slot):
                if new and at == k + ahead:
                    yield b, p, m
                if old and at == k + ahead + GROUPS:
                    yield b - 1, 1 - p, m

        def experts(k, ahead):
            return [e for e in range(E + 1) if unit_slot[FT1 * e] == k + ahead]

        @block.sync
        def _(sp):
            start(sp, [x_in, bc_out, bc_in, *stacked, stored])
            sp.dma_start(da[0:3 * E, 0:2], io["c_pick"].rearrange("r (a e) c -> r a (e c)", a=2)).then_inc(staged, 16)
            sp.dma_start(da[0:96, 2], io["c_spread"].rearrange("r i c -> r (i c)")).then_inc(staged, 16)
            sp.wait_ge(stored0, 1)

            def load(index, b, p):
                sp.wait_ge(xr_done.sem, xr_done.at(b - 2))
                hold(sp)
                sp.wait_ge(ln_done.sem, ln_done.at(b - 1))
                hold(sp)
                sp.dma_start(x[:, p], x_d[bass.ds(index, 1)].rearrange("o p t d -> p (o t) d")).then_inc(x_in.sem, 16)

            def stack(b, s):
                sp.wait_ge(du_full.sem, du_full.at(b - 1, SEG * (s + 1)))
                hold(sp)
                for i, made in enumerate((part1, part2, part3)):
                    sp.wait_ge(made.sem, made.at(b, s + 1))
                    hold(sp)
                    for c in range(4):
                        sp.dma_start(block_in[32 * i:32 * i + 32, :, s, c], part[32 * c:32 * c + 32, i]).then_inc(stacked[s].sem, 16)

            def repeat_bc(b, p):
                sp.wait_ge(prep_free.sem, prep_free.at(b, XD))
                hold(sp)
                sp.wait_ge(bc_in.sem, bc_in.at(b - 1))
                hold(sp)
                sp.dma_start(bc_d, xd[RDT:, :]).then_inc(bc_out.sem, 16)
                sp.wait_ge(dbu_done.sem, dbu_done.at(b - 2))
                hold(sp)
                sp.wait_ge(hc_done.sem, hc_done.at(b - 2))
                hold(sp)
                sp.wait_ge(bc_out.sem, bc_out.at(b))
                hold(sp)
                for i, tile in enumerate((b_rep, c_rep)):
                    rows = bc_d[N * i:N * i + N].unsqueeze(0).to_broadcast([128 // N, N, T])
                    sp.dma_start(tile[:, p], rows).then_inc(bc_in.sem, 16)

            def store(b, p):
                sp.wait_ge(res_done.sem, res_done.at(b))
                hold(sp)
                sp.dma_start(out_d[bass.ds(b - 1, 1)].rearrange("o p t d -> p (o t) d"), xr[:, p]).then_inc(stored.sem, 16)

            def prologue():
                load(0, 1, 0)
                load(1, 2, 1)
                repeat_bc(1, 0)
                stack(1, 0)

            def batch(b, p, old, new, nxt):
                if nxt:
                    load((b + 1) % B, b + 2, p)
                if new:
                    stack(b, 1)
                if old:
                    store(b - 1, 1 - p)
                if nxt:
                    repeat_bc(b + 1, 1 - p)
                    stack(b + 1, 0)

            schedule(batch, prologue, sp)
            sp.wait_ge(stored.sem, stored.at(B))
            sp.wait_ge(x_in.sem, x_in.at(B + 1))

        @block.gpsimd
        def _(pool):
            start(pool, [ln_rstd, xr_done, dt_step, hc_done, y_done, silu_done])
            nc.gpsimd.memset(ur[:, :, 0:CONV - 1], 0.0).then_inc(begun, 1)
            pool.wait_ge(begun, 5)

            def root(b, i):
                pool.wait_ge(ln_var.sem, ln_var.at(b, i + 1))
                nc.gpsimd.tensor_tensor(rstd[:, i], ve[:, i], minus_half[:], ALU.pow).then_inc(ln_rstd.sem, 1)

            def residual(b, p):
                pool.wait_ge(ln_done.sem, ln_done.at(b, 1))
                pool.wait_ge(stored.sem, stored.at(b - 2))
                nc.gpsimd.tensor_tensor(xr[:, p], x[:, p], xn[:, 0], ALU.add).then_inc(xr_done.sem, 1)

            def steps(b, p, s):
                if s == 0:
                    pool.wait_ge(sp_step.sem, sp_step.at(b))
                nc.gpsimd.tensor_tensor(dtu[:, 0, s], ez[:, s], rz[:, s], ALU.add).then_inc(dt_step.sem, 1)
                pool.wait_ge(dt_step.sem, dt_step.at(b, 2 * s + 1))
                if s == 0:
                    pool.wait_ge(u_done.sem, u_done.at(b))
                nc.gpsimd.tensor_tensor(dtu[:, 1, s], dtu[:, 0, s], u[:, p, s], ALU.mult).then_inc(dt_step.sem, 1)

            def times_c(b, p, k):
                pool.wait_ge(scanned.sem, scanned.at(b, k + 1))
                if k % 4 == 0:
                    pool.wait_ge(gathered.sem, gathered.at(b, k // 4 - 1) if k >= 8 else gathered.at(b - 1, 7 + k // 4))
                if k == 0:
                    pool.wait_ge(bc_in.sem, bc_in.at(b))
                nc.gpsimd.tensor_tensor(hc[:, k % NA], hs[:, k % 4], c_rep[:, p], ALU.mult).then_inc(hc_done.sem, 1)

            def gate_y(b, p, s):
                pool.wait_ge(y1_done.sem, y1_done.at(b, s + 1))
                if s == 0:
                    pool.wait_ge(acc_full.sem, acc_full.at(b - 1))
                    pool.wait_ge(z_done.sem, z_done.at(b))
                nc.gpsimd.tensor_tensor(yt[:, s], y1[:], sz[:, p, s], ALU.mult).then_inc(y_done.sem, 1)

            def silu(b, m):
                pool.wait_ge(one_more.sem, one_more.at(b, m + 1))
                nc.gpsimd.tensor_tensor(sg[:, m % NG], sg[:, m % NG], g_in[:, m % NG], ALU.mult).then_inc(silu_done.sem, 1)

            def prologue():
                root(1, 0)
                root(1, 1)
                residual(1, 0)
                for s in range(ST):
                    steps(1, 0, s)
                root(2, 0)
                root(2, 1)

            def batch(b, p, old, new, nxt):
                q = 1 - p
                for k in range(GROUPS):
                    if old and k == 0:
                        times_c(b - 1, q, GROUPS - 1)
                    if new and k:
                        times_c(b, p, k - 1)
                    for c, _, m in units(b, p, k, 2, old, new):
                        silu(c, m)
                    if old and k == 2:
                        gate_y(b - 1, q, 1)
                    if new and k == 20:
                        gate_y(b, p, 0)
                    if nxt:
                        if k == 9:
                            residual(b + 1, q)
                        if k in (22, 24):
                            steps(b + 1, q, (k - 22) // 2)
                        if k in (28, 30):
                            root(b + 2, (k - 28) // 2)

            schedule(batch, prologue, pool)

        @block.scalar
        def _(act):
            start(act, [prep_free, z_done, u_done, sp_exp, sp_ln, part1, part2, da_done, g_read, one_more, acc_read])
            act.wait_ge(w_loaded, 16 * n_loads)
            nc.scalar.activation(a_neg[:], w["a_log"][:], ACT.Exp).then_inc(begun, 1)
            act.wait_ge(begun, 6)

            def copy_out(b, n, to, rows=slice(0, 128), func=ACT.Copy, **how):
                act.wait_ge(prep_full.sem, prep_full.at(b, n))
                nc.scalar.activation(to, p_misc[rows, :], func, **how).then_inc(prep_free.sem, 1)

            def silu_u_z(b, p):
                for s in range(ST):
                    act.wait_ge(conv_step.sem, conv_step.at(b, 4 * s + 4))
                    nc.scalar.activation(u[:, p, s], conv[:, 1, s], ACT.Silu, bias=w["conv_b"][:, s:s + 1]).then_inc(u_done.sem, 1)
                act.wait_ge(prep_free.sem, prep_free.at(b, Z1))
                nc.scalar.activation(sz[:, p], sz[:, p], ACT.Silu).then_inc(z_done.sem, 1)

            def dt_in(b, s):
                act.wait_ge(prep_full.sem, prep_full.at(b, DT0 + s))
                if s == 0:
                    act.wait_ge(rest1.sem, rest1.at(b - 1))
                nc.scalar.activation(rz[:, s], p_misc[:], ACT.Relu, bias=w["dt_b"][:, s:s + 1])
                nc.scalar.activation(az[:, s], p_misc[:], ACT.Abs, bias=w["dt_b"][:, s:s + 1]).then_inc(prep_free.sem, 1)

            def exp_z(b):
                act.wait_ge(prep_free.sem, prep_free.at(b, DT1))
                nc.scalar.activation(ez, az, ACT.Exp, scale=-1.0).then_inc(sp_exp.sem, 1)

            def exp_gates(b):
                act.wait_ge(prep_full.sem, prep_full.at(b, GATE))
                nc.scalar.activation(eg[:], p_misc[:, 0:TT * E].rearrange("p (t e) -> p t e", e=E), ACT.Exp, scale=-1.0)\
                    .then_inc(prep_free.sem, 1)

            def log_in(b):
                act.wait_ge(sp_one.sem, sp_one.at(b))
                nc.scalar.activation(az, wz, ACT.Ln).then_inc(sp_ln.sem, 1)

            def first_part(b, s):
                act.wait_ge(dt_step.sem, dt_step.at(b, 2 * s + 2))
                before = stacked[0].at(b) if s else stacked[1].at(b - 1)
                act.wait_ge(stacked[1 - s].sem, before)
                nc.scalar.activation(part[:, 0], dtu[:, :, s], ACT.Copy).then_inc(part1.sem, 1)

            def second_part(b, s):
                act.wait_ge(rest1.sem, rest1.at(b, s + 1))
                nc.scalar.activation(part[:, 1], rest[:, :, s], ACT.Copy).then_inc(part2.sem, 1)

            def decay(b, k):
                s, j, i = order[k]
                g = 16 * s + 4 * j + i
                act.wait_ge(dt_full.sem, dt_full.at(b, k + 1))
                act.wait_ge(scanned.sem, scanned.at(b, k - ND + 1) if k >= ND else scanned.at(b - 1, GROUPS - ND + k + 1))
                nc.scalar.activation(da[:, k % ND], p_dt[:], ACT.Exp, scale=a_neg[:, g:g + 1]).then_inc(da_done.sem, 1)

            def gate(b, m):
                act.wait_ge(g_full.sem, g_full.at(b, m + 1))
                act.wait_ge(silu_done.sem, silu_done.at(b, m - NG + 1) if m >= NG else silu_done.at(b - 1, UNITS - NG + m + 1))
                act.wait_ge(hid_done.sem, hid_done.at(b, m - NG + 1) if m >= NG else hid_done.at(b - 1, UNITS - NG + m + 1))
                nc.scalar.activation(g_in[:, m % NG], p_g[:], ACT.Copy)
                nc.scalar.activation(sg[:, m % NG], p_g[:], ACT.Tanh, scale=0.5).then_inc(g_read.sem, 1)

            def add_one(b, m):
                act.wait_ge(g_read.sem, g_read.at(b, m + 1))
                nc.scalar.activation(sg[:, m % NG], sg[:, m % NG], ACT.Copy, bias=1.0).then_inc(one_more.sem, 1)

            def weights_out(b):
                act.wait_ge(prep_full.sem, prep_full.at(b, WT))
                act.wait_ge(w_full.sem, w_full.at(b - 1))
                nc.scalar.activation(wt[:], p_misc[:].bitcast(BF16)[0:3 * E, 0:T], ACT.Copy).then_inc(prep_free.sem, 1)

            def copy_sum(b):
                act.wait_ge(acc_full.sem, acc_full.at(b))
                act.wait_ge(back_full.sem, back_full.at(b - 1))
                nc.scalar.activation(ot[:], p_acc[:], ACT.Copy).then_inc(acc_read.sem, 1)

            def prologue():
                copy_out(1, XT, xt[:, 0])
                copy_out(1, HT, ht[:], scale=w["norm_w"])
                copy_out(1, U0, ur[:, 0, CONV - 1:])
                copy_out(1, U1, ur[:, 1, CONV - 1:])
                exp_gates(1)
                copy_out(1, Z0, sz[:, 0, 0])
                copy_out(1, Z1, sz[:, 0, 1])
                silu_u_z(1, 0)
                copy_out(1, XD, xd[:], slice(0, RDT + 2 * N))
                dt_in(1, 0)
                dt_in(1, 1)
                exp_z(1)
                log_in(1)
                first_part(1, 0)
                second_part(1, 0)
                weights_out(1)

            def batch(b, p, old, new, nxt):
                q = 1 - p
                for k in range(GROUPS):
                    if new:
                        decay(b, k)
                    for c, _, m in units(b, p, k, 3, old, new):
                        gate(c, m)
                    for c, _, m in units(b, p, k, 2, old, new):
                        add_one(c, m)
                    if old and k == 4:
                        copy_sum(b - 1)
                    if new and k == 5:
                        first_part(b, 1)
                    if new and k == 7:
                        second_part(b, 1)
                    if not nxt:
                        continue
                    if k == 0:
                        copy_out(b + 1, XT, xt[:, q])
                    if k == 1:
                        copy_out(b + 1, HT, ht[:], scale=w["norm_w"])
                    if k == 2:
                        copy_out(b + 1, U0, ur[:, 0, CONV - 1:])
                    if k == 3:
                        copy_out(b + 1, U1, ur[:, 1, CONV - 1:])
                    if k == 4:
                        exp_gates(b + 1)
                    if k == 8:
                        act.wait_ge(y_done.sem, y_done.at(b - 1))
                        copy_out(b + 1, Z0, sz[:, q, 0])
                    if k == 9:
                        copy_out(b + 1, Z1, sz[:, q, 1])
                    if k == 13:
                        silu_u_z(b + 1, q)
                    if k == 14:
                        act.wait_ge(bc_out.sem, bc_out.at(b))
                        copy_out(b + 1, XD, xd[:], slice(0, RDT + 2 * N))
                    if k in (15, 16):
                        dt_in(b + 1, k - 15)
                    if k == 17:
                        exp_z(b + 1)
                    if k == 19:
                        log_in(b + 1)
                    if k == 23:
                        first_part(b + 1, 0)
                    if k == 25:
                        second_part(b + 1, 0)
                    if k == 27:
                        weights_out(b + 1)

            schedule(batch, prologue, act)

        @block.vector
        def _(dve):
            start(dve, [ln_stats, ln_var, ln_done, conv_step, sp_one, sp_step, rest1, part3, route, xw_done, dbu_done, scanned,
                        y1_done, hid_done, res_done])
            dve.wait_ge(w_loaded, 16 * n_loads)
            dve.wait_ge(staged, 32)
            nc.vector.tensor_copy(spread[:].rearrange("r i c -> r (i c)"), da[0:96, 2]).then_inc(begun, 1)
            nc.vector.tensor_copy(pick[:].rearrange("r (a e) c -> r a (e c)", a=2), da[0:3 * E, 0:2]).then_inc(begun, 1)
            nc.vector.tensor_copy(ident_b[:], ident[:]).then_inc(begun, 1)
            dve.wait_ge(begun, 5)
            nc.vector.tensor_scalar(a_neg[:], a_neg[:], -1.0, None, ALU.mult).then_inc(begun, 1)

            def statistics(b, p):
                dve.wait_ge(x_in.sem, x_in.at(b))
                for t in range(TT):
                    ins = nc.vector.bn_stats(stats[:, t], x[:, p, t])
                ins.then_inc(ln_stats.sem, 1)
                dve.wait_ge(ln_stats.sem, ln_stats.at(b, 1))
                hold(dve)
                for t in range(TT):
                    ins = nc.vector.bn_aggr(mv[:, t], stats[:, t])
                ins.then_inc(ln_stats.sem, 1)
                dve.wait_ge(ln_stats.sem, ln_stats.at(b, 2))
                nc.vector.tensor_scalar(ve[:, 0], mv[:, :, 1], EPS, None, ALU.add).then_inc(ln_var.sem, 1)

            def normalize(b, p):
                dve.wait_ge(ln_rstd.sem, ln_rstd.at(b, 1))
                nc.vector.tensor_tensor(ms[:, 0], rstd[:, 0], rstd[:, 0], ALU.mult).then_inc(ln_stats.sem, 1)
                dve.wait_ge(ln_stats.sem, ln_stats.at(b, 3))
                nc.vector.tensor_tensor(ms[:, 1], ms[:, 0], mv[:, :, 1], ALU.mult).then_inc(ln_stats.sem, 1)
                dve.wait_ge(ln_stats.sem, ln_stats.at(b, 4))
                nc.vector.tensor_scalar(ve[:, 1], ms[:, 1], EPS, None, ALU.add).then_inc(ln_var.sem, 1)
                dve.wait_ge(prep_full.sem, prep_full.at(b - 1, HT))
                dve.wait_ge(xr_done.sem, xr_done.at(b - 1))
                for t in range(TT):
                    ins = nc.vector.tensor_scalar(xn[:, 0, t], x[:, p, t], mv[:, t, 0:1], rstd[:, 0, t:t + 1],
                                                  ALU.subtract, ALU.mult)
                ins.then_inc(ln_done.sem, 1)

            def normalize_rms(b):
                dve.wait_ge(ln_done.sem, ln_done.at(b, 1))
                dve.wait_ge(ln_rstd.sem, ln_rstd.at(b, 2))
                for t in range(TT):
                    ins = nc.vector.tensor_scalar(xn[:, 1, t], xn[:, 0, t], rstd[:, 1, t:t + 1], None, ALU.mult)
                ins.then_inc(ln_done.sem, 1)

            def convolve(b, n):
                s, k = divmod(n, CONV)
                if k == 0:
                    dve.wait_ge(prep_free.sem, prep_free.at(b, U0 + s))
                    dve.wait_ge(part3.sem, part3.at(b - 1, s + 1))
                taps = ur[:, s, k:k + T]
                wk = w["conv_w"][:, s, k:k + 1]
                if k == 0:
                    ins = nc.vector.tensor_scalar(conv[:, 0, s], taps, wk, None, ALU.mult)
                else:
                    dve.wait_ge(conv_step.sem, conv_step.at(b, n))
                    ins = nc.vector.scalar_tensor_tensor(conv[:, k % 2, s], taps, wk, conv[:, 1 - k % 2, s], ALU.mult, ALU.add)
                ins.then_inc(conv_step.sem, 1)

            def softplus_one(b):
                dve.wait_ge(sp_exp.sem, sp_exp.at(b))
                nc.vector.tensor_scalar(wz, ez, 1.0, None, ALU.add).then_inc(sp_one.sem, 1)

            def softplus_cut(b):
                dve.wait_ge(sp_one.sem, sp_one.at(b))
                nc.vector.scalar_tensor_tensor(ez, wz, -1.0, ez, ALU.add, ALU.subtract).then_inc(sp_step.sem, 1)

            def softplus_end(b):
                dve.wait_ge(sp_ln.sem, sp_ln.at(b))
                dve.wait_ge(sp_step.sem, sp_step.at(b, 1))
                nc.vector.tensor_tensor(ez, az, ez, ALU.subtract).then_inc(sp_step.sem, 1)

            def second_rest(b, s):
                dve.wait_ge(part1.sem, part1.at(b, s + 1))
                dve.wait_ge(dt_step.sem, dt_step.at(b, 2 * s + 2))
                nc.vector.tensor_tensor(rest[:, :, s], dtu[:, :, s], part[:, 0], ALU.subtract).then_inc(rest1.sem, 1)

            def third_part(b, s):
                dve.wait_ge(part2.sem, part2.at(b, s + 1))
                dve.wait_ge(rest1.sem, rest1.at(b, s + 1))
                nc.vector.tensor_tensor(part[:, 2], rest[:, :, s], part[:, 1], ALU.subtract).then_inc(part3.sem, 1)

            def routing(b, n):
                g = gates[:, 0]
                others = g.unsqueeze(2).to_broadcast([128, TT, E, E])
                mine = g.unsqueeze(3).to_broadcast([128, TT, E, E])
                first = w["before"][:].unsqueeze(1).to_broadcast([128, TT, E, E])
                if n == 0:
                    dve.wait_ge(prep_free.sem, prep_free.at(b, GATE))
                else:
                    dve.wait_ge(route.sem, route.at(b, n))
                if n == 0:
                    ins = nc.vector.tensor_scalar(gates[:, 1], eg[:], 1.0, None, ALU.add)
                elif n == 1:
                    hold(dve)
                    ins = nc.vector.reciprocal(gates[:, 0], gates[:, 1])
                elif n == 2:
                    nc.vector.tensor_tensor(rank2[:, 0], others, mine, ALU.is_gt)
                    ins = nc.vector.tensor_tensor(rank2[:, 1], others, mine, ALU.is_equal)
                elif n == 3:
                    ins = nc.vector.tensor_tensor(rank2[:, 1], rank2[:, 1], first, ALU.mult)
                elif n == 4:
                    ins = nc.vector.tensor_tensor(rank2[:, 0], rank2[:, 0], rank2[:, 1], ALU.add)
                elif n == 5:
                    ins = nc.vector.tensor_reduce(rank[:], rank2[:, 0], AX.X, ALU.add)
                elif n == 6:
                    ins = nc.vector.scalar_tensor_tensor(gates[:, 1], rank[:], 2.0, g, ALU.is_lt, ALU.mult)
                elif n == 7:
                    ins = nc.vector.tensor_reduce(wsum[:, 0], gates[:, 1], AX.X, ALU.add)
                elif n == 8:
                    ins = nc.vector.tensor_scalar(wsum[:, 1], wsum[:, 0], 6.0, None, ALU.mult)
                elif n == 9:
                    hold(dve)
                    ins = nc.vector.reciprocal(wsum[:, 0], wsum[:, 1])
                elif n == 10:
                    ins = nc.vector.tensor_tensor(gates[:, 0], gates[:, 1], wsum[:, 0].unsqueeze(2).to_broadcast([128, TT, E]),
                                                  ALU.mult)
                elif n == 11:
                    dve.wait_ge(prep_full.sem, prep_full.at(b - 1, WT))
                    ins = nc.vector.tensor_copy(wpart[:, :, 0], gates[:, 0])
                elif n == 12:
                    ins = nc.vector.tensor_tensor(wrest[:], gates[:, 0], wpart[:, :, 0], ALU.subtract)
                elif n == 13:
                    ins = nc.vector.tensor_copy(wpart[:, :, 1], wrest[:])
                else:
                    ins = nc.vector.tensor_tensor(wpart[:, :, 2], wrest[:], wpart[:, :, 1], ALU.subtract)
                ins.then_inc(route.sem, 1)

            def weigh_x(b, p, e):
                dve.wait_ge(u_full.sem, u_full.at(b, FT1 * (e - 1)) if e >= 2 else u_full.at(b - 1))
                if e < E:
                    dve.wait_ge(w_full.sem, w_full.at(b, e + 1))
                    ins = nc.vector.tensor_tensor(xw[:, e % 2], p_w[:], xt[:, p], ALU.mult)
                else:
                    ins = nc.vector.tensor_scalar(xw[:, e % 2], xt[:, p], 1.0 / 6.0, None, ALU.mult)
                ins.then_inc(xw_done.sem, 1)

            def inject(b, p, k):
                dve.wait_ge(scanned.sem, scanned.at(b, k - 3) if k >= 4 else scanned.at(b - 1, GROUPS - 3 + k))
                dve.wait_ge(du_full.sem, du_full.at(b, k + 1))
                if k == 0:
                    dve.wait_ge(bc_in.sem, bc_in.at(b))
                nc.vector.tensor_tensor(dbu[:, k % 4], p_du[:], b_rep[:, p], ALU.mult).then_inc(dbu_done.sem, 1)

            def scan(b, k):
                dve.wait_ge(da_done.sem, da_done.at(b, k + 1))
                dve.wait_ge(dbu_done.sem, dbu_done.at(b, k + 1))
                dve.wait_ge(hc_done.sem, hc_done.at(b, k - 3) if k >= 4 else hc_done.at(b - 1, GROUPS - 3 + k))
                nc.vector.tensor_tensor_scan(hs[:, k % 4], da[:, k % ND], dbu[:, k % 4], 0.0, ALU.mult, ALU.add)\
                    .then_inc(scanned.sem, 1)

            def skip(b, p, s):
                dve.wait_ge(gathered.sem, gathered.at(b, 4 * s + 4))
                dve.wait_ge(y_done.sem, y_done.at(b, s) if s else y_done.at(b - 1))
                nc.vector.scalar_tensor_tensor(y1[:], u[:, p, s], w["d_skip"][:, s:s + 1], p_y[:], ALU.mult, ALU.add)\
                    .then_inc(y1_done.sem, 1)

            def hidden(b, m):
                dve.wait_ge(silu_done.sem, silu_done.at(b, m + 1))
                dve.wait_ge(u_full.sem, u_full.at(b, m + 1))
                dve.wait_ge(hid_used.sem, hid_used.at(b, m - 1) if m >= 2 else hid_used.at(b - 1, UNITS - 1 + m))
                nc.vector.tensor_tensor(hid[:, m % 2], p_u[:], sg[:, m % NG], ALU.mult).then_inc(hid_done.sem, 1)

            def result(b, p):
                dve.wait_ge(back_full.sem, back_full.at(b))
                nc.vector.tensor_tensor(xr[:, p], p_misc[:].rearrange("p (t d) -> p t d", t=TT), xr[:, p], ALU.add)\
                    .then_inc(res_done.sem, 1)

            conv_slot = {7: (0,), 8: (1,), 9: (2,), 10: (3,), 11: (4, 5), 12: (6, 7)}

            def prologue():
                statistics(1, 0)
                normalize(1, 0)
                normalize_rms(1)
                for n in range(ST * CONV):
                    convolve(1, n)
                for n in range(15):
                    routing(1, n)
                softplus_one(1)
                softplus_cut(1)
                softplus_end(1)
                second_rest(1, 0)
                third_part(1, 0)
                statistics(2, 1)
                normalize(2, 1)
                normalize_rms(2)

            def batch(b, p, old, new, nxt):
                q = 1 - p
                for k in range(GROUPS):
                    if new:
                        inject(b, p, k)
                    if old and k == 0:
                        scan(b - 1, GROUPS - 1)
                    if new and k:
                        scan(b, k - 1)
                    for c, _, m in units(b, p, k, 0, old, new):
                        hidden(c, m)
                    if new:
                        for e in experts(k, 2):
                            weigh_x(b, p, e)
                    if old and k == 3:
                        skip(b - 1, q, 1)
                    if old and k == 7:
                        result(b - 1, q)
                    if new and k == 6:
                        second_rest(b, 1)
                    if new and k == 8:
                        third_part(b, 1)
                    if new and k == 19:
                        skip(b, p, 0)
                    if not nxt:
                        continue
                    if k in conv_slot:
                        for n in conv_slot[k]:
                            convolve(b + 1, n)
                    if 5 <= k < 20:
                        routing(b + 1, k - 5)
                    if k == 18:
                        softplus_one(b + 1)
                    if k == 19:
                        softplus_cut(b + 1)
                    if k == 21:
                        softplus_end(b + 1)
                    if k == 24:
                        second_rest(b + 1, 0)
                    if k == 26:
                        third_part(b + 1, 0)
                    if k == 28:
                        statistics(b + 2, p)
                    if k == 30:
                        normalize(b + 2, p)
                    if k == 31:
                        normalize_rms(b + 2)

            schedule(batch, prologue, dve)

        @block.tensor
        def _(pe):
            start(pe, [prep_full, w_full, dt_full, du_full, gathered, g_full, u_full, hid_used, acc_full, back_full])
            pe.wait_ge(w_loaded, 16 * n_loads)
            pe.wait_ge(begun, 6)

            def free(b, n):
                pe.wait_ge(prep_free.sem, prep_free.at(b, n))

            def turn_x(b, i):
                if i:
                    free(b, XT)
                else:
                    free(b - 1, WT)
                pe.wait_ge(ln_done.sem, ln_done.at(b, i + 1))
                for t in range(TT):
                    ins = nc.tensor.transpose(p_misc[:, bass.ts(t, 128)], xn[:, i, t], ident[:])
                ins.then_inc(prep_full.sem, 1)

            def in_proj(b, n):
                free(b, (HT, U0, GATE, Z0)[n])
                if n == 2:
                    pe.wait_ge(res_done.sem, res_done.at(b - 2))
                nc.tensor.matmul(p_misc[:], w["win"][:, bass.ts(n, 128)], ht[:], start=True, stop=True).then_inc(prep_full.sem, 1)

            def gate_logits(b, p):
                free(b, U1)
                for t in range(TT):
                    ins = nc.tensor.matmul(p_misc[:, bass.ts(t, E)], xt[:, p, bass.ts(t, 128)], w["wgate"][:], start=True, stop=True)
                ins.then_inc(prep_full.sem, 1)

            def x_proj(b, p):
                pe.wait_ge(u_done.sem, u_done.at(b))
                free(b, Z1)
                for s in range(ST):
                    ins = nc.tensor.matmul(p_misc[0:RDT + 2 * N], w["wx"][:, s], u[:, p, s], start=(s == 0), stop=(s == ST - 1))
                ins.then_inc(prep_full.sem, 1)

            def dt_proj(b, s):
                free(b, XD + s)
                nc.tensor.matmul(p_misc[:], w["wdt"][:, bass.ts(s, 128)], xd[0:RDT], start=True, stop=True).then_inc(prep_full.sem, 1)

            def turn_weights(b):
                free(b, DT1)
                pe.wait_ge(route.sem, route.at(b))
                turned = p_misc[:].bitcast(BF16)
                for t in range(TT):
                    ins = nc.tensor.transpose(turned[0:3 * E, bass.ts(t, 128)], wpart[:, t].rearrange("p i e -> p (i e)"), ident_b[:])
                ins.then_inc(prep_full.sem, 1)

            def spread_weight(b, e):
                if e == 0:
                    free(b, WT)
                pe.wait_ge(xw_done.sem, xw_done.at(b, e) if e else xw_done.at(b - 1))
                nc.tensor.matmul(p_w[:], pick[:, e], wt[:], start=True, stop=True).then_inc(w_full.sem, 1)

            def spread_dt(b, k):
                s, j, i = order[k]
                if k % SEG == 0:
                    pe.wait_ge(stacked[s].sem, stacked[s].at(b))
                pe.wait_ge(da_done.sem, da_done.at(b, k) if k else da_done.at(b - 1))
                nc.tensor.matmul(p_dt[:], spread[:, i], block_in[:, 0, s, j], start=True, stop=True).then_inc(dt_full.sem, 1)

            def spread_du(b, k):
                s, j, i = order[k]
                pe.wait_ge(dbu_done.sem, dbu_done.at(b, k) if k else dbu_done.at(b - 1))
                nc.tensor.matmul(p_du[:], spread[:, i], block_in[:, 1, s, j], start=True, stop=True).then_inc(du_full.sem, 1)

            def gather_y(b, q):
                pe.wait_ge(hc_done.sem, hc_done.at(b, 4 * q + 4))
                if q % 4 == 0:
                    pe.wait_ge(y1_done.sem, y1_done.at(b, q // 4) if q else y1_done.at(b - 1))
                for k in range(4 * q, 4 * q + 4):
                    s, j, i = order[k]
                    ins = nc.tensor.matmul(p_y[32 * j:32 * j + 32], w["gather"][:, i], hc[:, k % NA], start=(i == 0), stop=(i == 3))
                ins.then_inc(gathered.sem, 1)

            def gate(b, p, m):
                e, f = divmod(m, FT1)
                pe.wait_ge(g_read.sem, g_read.at(b, m) if m else g_read.at(b - 1))
                nc.tensor.matmul(p_g[:], w1[:, e, bass.ts(f, 128)], xt[:, p], start=True, stop=True).then_inc(g_full.sem, 1)

            def up(b, m):
                e, f = divmod(m, FT1)
                pe.wait_ge(hid_done.sem, hid_done.at(b, m) if m else hid_done.at(b - 1))
                pe.wait_ge(xw_done.sem, xw_done.at(b, e + 1))
                nc.tensor.matmul(p_u[:], w3[:, e, bass.ts(f, 128)], xw[:, e % 2], start=True, stop=True).then_inc(u_full.sem, 1)

            def down(b, m):
                e, f = divmod(m, FT1)
                if m == 0:
                    pe.wait_ge(acc_read.sem, acc_read.at(b - 1))
                pe.wait_ge(hid_done.sem, hid_done.at(b, m + 1))
                nc.tensor.matmul(p_acc[:], w2[:, e, f], hid[:, m % 2], start=(m == 0), stop=False).then_inc(hid_used.sem, 1)

            def out_proj(b, s):
                pe.wait_ge(y_done.sem, y_done.at(b, s + 1))
                nc.tensor.matmul(p_acc[:], w["wo1"][:, s], yt[:, s], start=False, stop=(s == ST - 1)).then_inc(acc_full.sem, 1)

            def turn_back(b, nxt):
                if nxt:
                    free(b + 2, GATE)
                else:
                    pe.wait_ge(res_done.sem, res_done.at(b - 1))
                pe.wait_ge(acc_read.sem, acc_read.at(b))
                for t in range(TT):
                    ins = nc.tensor.transpose(p_misc[:, bass.ts(t, 128)], ot[:, bass.ts(t, 128)], ident[:])
                ins.then_inc(back_full.sem, 1)

            def prologue():
                turn_x(1, 0)
                turn_x(1, 1)
                for n in range(2):
                    in_proj(1, n)
                gate_logits(1, 0)
                for n in range(2, 4):
                    in_proj(1, n)
                x_proj(1, 0)
                for s in range(ST):
                    dt_proj(1, s)
                turn_weights(1)

            def batch(b, p, old, new, nxt):
                q = 1 - p
                for k in range(GROUPS):
                    if new:
                        spread_dt(b, k)
                        spread_du(b, k)
                    for c, r, m in units(b, p, k, 3, old, new):
                        gate(c, r, m)
                    if nxt:
                        if k in (0, 1):
                            turn_x(b + 1, k)
                        if k in (2, 3):
                            in_proj(b + 1, k - 2)
                        if k == 4:
                            gate_logits(b + 1, q)
                        if k in (8, 9):
                            in_proj(b + 1, k - 6)
                        if k == 14:
                            x_proj(b + 1, q)
                        if k in (15, 16):
                            dt_proj(b + 1, k - 15)
                        if k == 27:
                            turn_weights(b + 1)
                    for c, _, m in units(b, p, k, 0, old, new):
                        up(c, m)
                    for c, _, m in units(b, p, k, -1, old, new):
                        down(c, m)
                    if new:
                        for e in experts(k, 3):
                            if e < E:
                                spread_weight(b, e)
                        if k >= 6 and k % 4 == 2:
                            gather_y(b, (k - 6) // 4)
                    if old and k == 1:
                        gather_y(b - 1, GROUPS // 4 - 1)
                    if old and k == 4:
                        out_proj(b - 1, 1)
                    if new and k == 22:
                        out_proj(b, 0)
                    if old and k == 6:
                        turn_back(b - 1, nxt)

            schedule(batch, prologue, pe)


def laid_out(i):
    a = {k: np.asarray(v) for k, v in i.items()}
    c = np.ascontiguousarray
    column = np.arange(H * DH)
    head, dim = column // DH, column % DH
    swapped = (dim + DH // 2) % DH
    q_cols = [column, head * DH + swapped]
    up_cols = [head * 2 * DH + dim, head * 2 * DH + swapped, (column % H) * 2 * DH + DH + column // H]
    wup = np.concatenate([a["L0_attn_Wup"], a["L0_attn_bup"][None]], 0)
    per_tile = lambda v: v.reshape(ST, 128, -1).transpose(1, 0, 2).reshape(128, -1)
    xp = a["L1_attn_x_proj_w"].reshape(ST, 128, RDT + 2 * N).transpose(1, 0, 2)
    stacked = lambda routed, shared: np.concatenate([routed, shared[None]], 0)
    return {
        "x": c(a["L0_attn_x"]),
        "wq": c(np.stack([a["L0_attn_Wq"][:, q] for q in q_cols], 1)),
        "wdown": c(a["L0_attn_Wdown"]),
        "wup": c(np.stack([wup[:, k] for k in up_cols], 1)),
        "wout": c(a["L0_attn_Wout"]),
        "bq": c(np.stack([a["L0_attn_bq"][q] for q in q_cols])[None]),
        "bdown": c(a["L0_attn_bdown"][:, None]),
        "bout": c(a["L0_attn_bout"][None]),
        "wg": c(a["L0_ffn_w_gate"].T),
        "wu": c(a["L0_ffn_w_up"].T),
        "wd": c(a["L0_ffn_w_down"].T.reshape(FT0, 128, D).transpose(1, 0, 2)),
        "w1": c(stacked(a["L1_ffn_We1"], a["L1_ffn_Ws1"]).transpose(1, 0, 2)),
        "w3": c(stacked(a["L1_ffn_We3"], a["L1_ffn_Ws3"]).transpose(1, 0, 2)),
        "w2": c(stacked(a["L1_ffn_We2"], a["L1_ffn_Ws2"]).reshape(E + 1, FT1, 128, D).transpose(2, 0, 1, 3)),
        "win": c(a["L1_attn_in_proj_w"]),
        "wx": c(xp),
        "wdt": c(a["L1_attn_dt_proj_w"]),
        "wo1": c(a["L1_attn_out_proj_w"].reshape(ST, 128, D).transpose(1, 0, 2)),
        "wgate": c(a["L1_ffn_Wg"]),
        "vecs": c(np.concatenate([a["L1_attn_norm_w"][:, None], per_tile(a["L1_attn_conv_w"]), per_tile(a["L1_attn_conv_b"]),
                                  per_tile(a["L1_attn_dt_proj_b"]), per_tile(a["L1_attn_D"])], 1)),
        "a_log": c(a["L1_attn_A_log"].reshape(GROUPS, 128 // N, N).transpose(1, 2, 0).reshape(128, GROUPS)),
    }


def kernel(**inputs):
    import concourse.bacc as bacc
    from concourse.bass_utils import run_bass_kernel_spmd

    arrays = {**laid_out(inputs), **constants()}
    nc = bacc.Bacc("TRN2", target_bir_lowering=False, num_devices=1)
    io = {n: nc.dram_tensor("in_" + n, v.shape, mybir.dt.from_np(v.dtype), kind="ExternalInput").ap() for n, v in arrays.items()}
    out = nc.dram_tensor("out", (B, T, D), F32, kind="ExternalOutput").ap()
    program(nc, io, out)
    return run_bass_kernel_spmd(nc, [{"in_" + n: v for n, v in arrays.items()}], core_ids=[0]).results[0]["out"]
```
